# Optimizing a Trainium2 kernel written in Bass

```python
import numpy as np
import jax
import jax.numpy as jnp

def _softmax(x, axis=-1):
    return jax.nn.softmax(x, axis=axis)

def _gelu(x):
    return jax.nn.gelu(x, approximate=True)

def _silu(x):
    return jax.nn.silu(x)

def _sigmoid(x):
    return jax.nn.sigmoid(x)

def _layernorm(x, axis=-1, eps=1e-05):
    m = jnp.mean(x, axis=axis, keepdims=True)
    v = jnp.var(x, axis=axis, keepdims=True)
    return (x - m) / jnp.sqrt(v + eps)

def _scatter_add(tgt, idx, src, axis=0):
    return tgt.at[idx].add(src)

def _segment_sum(src, seg, n):
    return jax.ops.segment_sum(src, seg, n)
kernel_name = 'mk_lm_tower_d2_tok_ids1024_r4_aa7728'

def setup_inputs(seed: int=0):
    np.random.seed(seed)
    _w = jnp.asarray

    def _rec_inputs():
        import jax
        import jax.numpy as jnp
        _rk = jax.random.key(seed)
        x = jax.random.randint(jax.random.fold_in(_rk, 1), (16, 256), 0, 12564, jnp.int32)
        return x
    x = _rec_inputs()

    def _L0_tok_setup():
        import jax, jax.numpy as jnp
        import numpy as np
        BITW = 1
        N_LEVELS = float(2 ** BITW - 1)
        key = jax.random.key(seed)
        k1, k2 = jax.random.split(key)
        input = jax.random.randint(k1, (8, 512), 0, 50257, dtype=jnp.int64)
        weight = jax.random.normal(k2, (50257, 256), dtype=jnp.float32)
        return {'input': input, 'weight': weight}
    _L0_tok_all = _L0_tok_setup()
    _L0_tok_in = {k: v for k, v in _L0_tok_all.items() if k in ('weight',)}
    del _L0_tok_all

    def _L0_attn_setup():
        import jax, jax.numpy as jnp
        import numpy as np
        NUM_HEADS = 16
        QMAX = 127.0

        def fake_quant(x):
            scale = jnp.maximum(jnp.max(jnp.abs(x)) / QMAX, 1e-08)
            q = jnp.clip(jnp.round(x / scale), -QMAX, QMAX) * scale
            return x + jax.lax.stop_gradient(q - x)
        key = jax.random.key(seed)
        ks = jax.random.split(key, 5)
        B, T, C = (2, 512, 256)
        return {'x': jax.random.normal(ks[0], (B, T, C), jnp.float32), 'Wqkv': jax.random.normal(ks[1], (3 * C, C), jnp.float32) * C ** (-0.5), 'bqkv': jax.random.normal(ks[2], (3 * C,), jnp.float32) * 0.01, 'Wproj': jax.random.normal(ks[3], (C, C), jnp.float32) * C ** (-0.5), 'bproj': jax.random.normal(ks[4], (C,), jnp.float32) * 0.01}
    _L0_attn_all = _L0_attn_setup()
    _L0_attn_in = {k: v for k, v in _L0_attn_all.items() if k in ('Wqkv', 'bqkv', 'Wproj', 'bproj')}
    del _L0_attn_all

    def _L0_ffn_setup():
        import jax, jax.numpy as jnp
        import numpy as np
        H = 8
        QD = 64
        HALF = QD // 2
        DIMS = (32, 32)
        TOPK = 16
        DTK = 4
        EPS_BN = 1e-05
        EPS_NORM = 1e-12

        def _l2norm(x):
            n = jnp.linalg.norm(x, axis=-1, keepdims=True)
            return x / jnp.maximum(n, EPS_NORM)
        key = jax.random.key(seed)
        ks = jax.random.split(key, 6)
        B, S, D, O, E = (2, 128, 256, 256, 256)
        hidden_states = jax.random.normal(ks[0], (B, S, D), jnp.float32)
        Wq = jax.random.normal(ks[1], (D, H * QD), jnp.float32) * 0.02
        bq = jnp.zeros((H * QD,), jnp.float32)
        bn_gamma = jnp.ones((QD,), jnp.float32)
        bn_beta = jnp.zeros((QD,), jnp.float32)
        sub_key0 = jax.random.normal(ks[2], (DIMS[0], HALF), jnp.float32) * 0.02
        sub_key1 = jax.random.normal(ks[3], (DIMS[1], HALF), jnp.float32) * 0.02
        expert_down = jax.random.normal(ks[4], (E, D), jnp.float32) * 0.02
        expert_up = jax.random.normal(ks[5], (E, O), jnp.float32) * 0.02
        return {'hidden_states': hidden_states, 'Wq': Wq, 'bq': bq, 'bn_gamma': bn_gamma, 'bn_beta': bn_beta, 'sub_key0': sub_key0, 'sub_key1': sub_key1, 'expert_down': expert_down, 'expert_up': expert_up}
    _L0_ffn_all = _L0_ffn_setup()
    _L0_ffn_in = {k: v for k, v in _L0_ffn_all.items() if k in ('Wq', 'bq', 'bn_gamma', 'bn_beta', 'sub_key0', 'sub_key1', 'expert_down', 'expert_up')}
    del _L0_ffn_all

    def _L1_attn_setup():
        import jax, jax.numpy as jnp
        import numpy as np
        import math
        D = 256
        H = 16
        DH = D // H

        def sinusoidal_pe(length, d):
            pos = jnp.arange(length, dtype=jnp.float32)[:, None]
            div = jnp.exp(jnp.arange(0, d, 2, dtype=jnp.float32) * (-math.log(10000.0) / d))
            ang = pos * div
            return jnp.stack([jnp.sin(ang), jnp.cos(ang)], axis=-1).reshape(length, d)

        def _relative_shift(pos_score):
            B, Hh, S1, S2 = pos_score.shape
            padded = jnp.concatenate([jnp.zeros((B, Hh, S1, 1), pos_score.dtype), pos_score], axis=-1)
            padded = padded.reshape(B, Hh, S2 + 1, S1)
            return padded[:, :, 1:].reshape(B, Hh, S1, S2)
        key = jax.random.key(seed)
        ks = jax.random.split(key, 12)
        s = 0.02
        x = jax.random.normal(ks[0], (2, 512, D), dtype=jnp.float32)
        return {'x': x, 'ln_g': jnp.ones((D,), jnp.float32), 'ln_b': jnp.zeros((D,), jnp.float32), 'Wq': jax.random.normal(ks[1], (D, D), jnp.float32) * s, 'bq': jnp.zeros((D,), jnp.float32), 'Wk': jax.random.normal(ks[2], (D, D), jnp.float32) * s, 'bk': jnp.zeros((D,), jnp.float32), 'Wv': jax.random.normal(ks[3], (D, D), jnp.float32) * s, 'bv': jnp.zeros((D,), jnp.float32), 'Wp': jax.random.normal(ks[4], (D, D), jnp.float32) * s, 'Wo': jax.random.normal(ks[5], (D, D), jnp.float32) * s, 'bo': jnp.zeros((D,), jnp.float32), 'u_bias': jax.random.normal(ks[6], (H, DH), jnp.float32) * 0.05, 'v_bias': jax.random.normal(ks[7], (H, DH), jnp.float32) * 0.05}
    _L1_attn_all = _L1_attn_setup()
    _L1_attn_in = {k: v for k, v in _L1_attn_all.items() if k in ('ln_g', 'ln_b', 'Wq', 'bq', 'Wk', 'bk', 'Wv', 'bv', 'Wp', 'Wo', 'bo', 'u_bias', 'v_bias')}
    del _L1_attn_all

    def _L1_ffn_setup():
        import jax, jax.numpy as jnp
        import numpy as np
        H = 256
        DFF = 1024
        E_ROUTED = 7
        TOP_K = 2

        def _swiglu(flat, gate_w, up_w, down_w):
            g = flat @ gate_w.T
            up = flat @ up_w.T
            return jax.nn.silu(g) * up @ down_w.T
        key = jax.random.key(seed)
        ks = jax.random.split(key, 8)
        s = 0.02
        return {'x': jax.random.normal(ks[0], (4, 512, H), jnp.float32), 'shared_up': jax.random.normal(ks[1], (DFF, H), jnp.float32) * s, 'shared_gate': jax.random.normal(ks[2], (DFF, H), jnp.float32) * s, 'shared_down': jax.random.normal(ks[3], (H, DFF), jnp.float32) * s, 'routed_up': jax.random.normal(ks[4], (E_ROUTED, DFF, H), jnp.float32) * s, 'routed_gate': jax.random.normal(ks[5], (E_ROUTED, DFF, H), jnp.float32) * s, 'routed_down': jax.random.normal(ks[6], (E_ROUTED, H, DFF), jnp.float32) * s, 'router_w': jax.random.normal(ks[7], (E_ROUTED, H), jnp.float32) * 0.02}
    _L1_ffn_all = _L1_ffn_setup()
    _L1_ffn_in = {k: v for k, v in _L1_ffn_all.items() if k in ('shared_up', 'shared_gate', 'shared_down', 'routed_up', 'routed_gate', 'routed_down', 'router_w')}
    del _L1_ffn_all
    return {'x': x, 'L0_tok_weight': _L0_tok_in['weight'], 'L0_attn_Wqkv': _L0_attn_in['Wqkv'], 'L0_attn_bqkv': _L0_attn_in['bqkv'], 'L0_attn_Wproj': _L0_attn_in['Wproj'], 'L0_attn_bproj': _L0_attn_in['bproj'], 'L0_ffn_Wq': _L0_ffn_in['Wq'], 'L0_ffn_bq': _L0_ffn_in['bq'], 'L0_ffn_bn_gamma': _L0_ffn_in['bn_gamma'], 'L0_ffn_bn_beta': _L0_ffn_in['bn_beta'], 'L0_ffn_sub_key0': _L0_ffn_in['sub_key0'], 'L0_ffn_sub_key1': _L0_ffn_in['sub_key1'], 'L0_ffn_expert_down': _L0_ffn_in['expert_down'], 'L0_ffn_expert_up': _L0_ffn_in['expert_up'], 'L1_attn_ln_g': _L1_attn_in['ln_g'], 'L1_attn_ln_b': _L1_attn_in['ln_b'], 'L1_attn_Wq': _L1_attn_in['Wq'], 'L1_attn_bq': _L1_attn_in['bq'], 'L1_attn_Wk': _L1_attn_in['Wk'], 'L1_attn_bk': _L1_attn_in['bk'], 'L1_attn_Wv': _L1_attn_in['Wv'], 'L1_attn_bv': _L1_attn_in['bv'], 'L1_attn_Wp': _L1_attn_in['Wp'], 'L1_attn_Wo': _L1_attn_in['Wo'], 'L1_attn_bo': _L1_attn_in['bo'], 'L1_attn_u_bias': _L1_attn_in['u_bias'], 'L1_attn_v_bias': _L1_attn_in['v_bias'], 'L1_ffn_shared_up': _L1_ffn_in['shared_up'], 'L1_ffn_shared_gate': _L1_ffn_in['shared_gate'], 'L1_ffn_shared_down': _L1_ffn_in['shared_down'], 'L1_ffn_routed_up': _L1_ffn_in['routed_up'], 'L1_ffn_routed_gate': _L1_ffn_in['routed_gate'], 'L1_ffn_routed_down': _L1_ffn_in['routed_down'], 'L1_ffn_router_w': _L1_ffn_in['router_w']}

def reference(x, L0_tok_weight, L0_attn_Wqkv, L0_attn_bqkv, L0_attn_Wproj, L0_attn_bproj, L0_ffn_Wq, L0_ffn_bq, L0_ffn_bn_gamma, L0_ffn_bn_beta, L0_ffn_sub_key0, L0_ffn_sub_key1, L0_ffn_expert_down, L0_ffn_expert_up, L1_attn_ln_g, L1_attn_ln_b, L1_attn_Wq, L1_attn_bq, L1_attn_Wk, L1_attn_bk, L1_attn_Wv, L1_attn_bv, L1_attn_Wp, L1_attn_Wo, L1_attn_bo, L1_attn_u_bias, L1_attn_v_bias, L1_ffn_shared_up, L1_ffn_shared_gate, L1_ffn_shared_down, L1_ffn_routed_up, L1_ffn_routed_gate, L1_ffn_routed_down, L1_ffn_router_w):
    import jax
    import jax.numpy as jnp

    def _L0_tok_ref(input, weight):
        import jax, jax.numpy as jnp
        import numpy as np
        BITW = 1
        N_LEVELS = float(2 ** BITW - 1)
        max_value = jax.lax.stop_gradient(jnp.max(jnp.abs(weight)))
        pre = weight / max_value * 0.5 + 0.5
        q = jnp.round(pre * N_LEVELS) / N_LEVELS
        quantized_weight = max_value * (2.0 * q - 1.0)
        return quantized_weight[input]

    def _L0_attn_ref(x, Wqkv, bqkv, Wproj, bproj):
        import jax, jax.numpy as jnp
        import numpy as np
        NUM_HEADS = 16
        QMAX = 127.0

        def fake_quant(x):
            scale = jnp.maximum(jnp.max(jnp.abs(x)) / QMAX, 1e-08)
            q = jnp.clip(jnp.round(x / scale), -QMAX, QMAX) * scale
            return x + jax.lax.stop_gradient(q - x)
        B, T, C = x.shape
        H = NUM_HEADS
        D = C // H
        scale = D ** (-0.5)
        xq = fake_quant(x)
        qkv = xq @ fake_quant(Wqkv).T + bqkv
        qkv = qkv.reshape(B, T, 3, H, D).transpose(2, 0, 3, 1, 4)
        q, k, v = (qkv[0], qkv[1], qkv[2])
        scores = jnp.einsum('bhqd,bhkd->bhqk', q, k) * scale
        causal = jnp.triu(jnp.full((T, T), -jnp.inf, jnp.float32), k=1)
        attn = jax.nn.softmax(scores + causal, axis=-1)
        out = jnp.einsum('bhqk,bhkd->bhqd', attn, v)
        out = out.transpose(0, 2, 1, 3).reshape(B, T, C)
        outq = fake_quant(out)
        return outq @ fake_quant(Wproj).T + bproj

    def _L0_ffn_ref(hidden_states, Wq, bq, bn_gamma, bn_beta, sub_key0, sub_key1, expert_down, expert_up):
        import jax, jax.numpy as jnp
        import numpy as np
        H = 8
        QD = 64
        HALF = QD // 2
        DIMS = (32, 32)
        TOPK = 16
        DTK = 4
        EPS_BN = 1e-05
        EPS_NORM = 1e-12

        def _l2norm(x):
            n = jnp.linalg.norm(x, axis=-1, keepdims=True)
            return x / jnp.maximum(n, EPS_NORM)
        B, S, D = hidden_states.shape
        q = (hidden_states @ Wq + bq).reshape(B, S, H, QD)
        mean = q.mean(axis=(0, 1, 2))
        var = q.var(axis=(0, 1, 2))
        q = (q - mean) / jnp.sqrt(var + EPS_BN) * bn_gamma + bn_beta
        q0 = _l2norm(q[..., :HALF])
        q1 = _l2norm(q[..., HALF:])
        k0 = _l2norm(sub_key0)
        k1 = _l2norm(sub_key1)
        s0 = jnp.einsum('bshq,kq->bshk', q0, k0)
        s1 = jnp.einsum('bshq,kq->bshk', q1, k1)
        ts0, ti0 = jax.lax.top_k(s0, DTK)
        ts1, ti1 = jax.lax.top_k(s1, DTK)
        comb_s = (ts0[..., :, None] + ts1[..., None, :]).reshape(B, S, H, DTK * DTK)
        comb_i = (ti0[..., :, None] * DIMS[1] + ti1[..., None, :]).reshape(B, S, H, DTK * DTK)
        top_s, pos = jax.lax.top_k(comb_s, TOPK)
        idx = jnp.take_along_axis(comb_i, pos, axis=-1)
        w = jax.nn.softmax(top_s, axis=-1)
        down = expert_down[idx]
        up = expert_up[idx]
        eh = jnp.einsum('bshkd,bsd->bshk', down, hidden_states)
        eh = jax.nn.gelu(eh, approximate=False)
        out = jnp.einsum('bshko,bshk->bso', up, eh * w)
        return out

    def _L1_attn_ref(x, ln_g, ln_b, Wq, bq, Wk, bk, Wv, bv, Wp, Wo, bo, u_bias, v_bias):
        import jax, jax.numpy as jnp
        import numpy as np
        import math
        D = 256
        H = 16
        DH = D // H

        def sinusoidal_pe(length, d):
            pos = jnp.arange(length, dtype=jnp.float32)[:, None]
            div = jnp.exp(jnp.arange(0, d, 2, dtype=jnp.float32) * (-math.log(10000.0) / d))
            ang = pos * div
            return jnp.stack([jnp.sin(ang), jnp.cos(ang)], axis=-1).reshape(length, d)

        def _relative_shift(pos_score):
            B, Hh, S1, S2 = pos_score.shape
            padded = jnp.concatenate([jnp.zeros((B, Hh, S1, 1), pos_score.dtype), pos_score], axis=-1)
            padded = padded.reshape(B, Hh, S2 + 1, S1)
            return padded[:, :, 1:].reshape(B, Hh, S1, S2)
        B, S, Dm = x.shape
        dh = Dm // H
        scale = dh ** (-0.5)
        pe = sinusoidal_pe(S, Dm)
        mu = jnp.mean(x, axis=-1, keepdims=True)
        var = jnp.var(x, axis=-1, keepdims=True)
        xn = (x - mu) / jnp.sqrt(var + 1e-05) * ln_g + ln_b
        q = (xn @ Wq + bq).reshape(B, S, H, dh)
        k = (xn @ Wk + bk).reshape(B, S, H, dh)
        v = (xn @ Wv + bv).reshape(B, S, H, dh)
        p = (pe @ Wp).reshape(S, H, dh)
        content = jnp.einsum('bihd,bjhd->bhij', q + u_bias, k)
        pos = jnp.einsum('bihd,jhd->bhij', q + v_bias, p)
        pos = _relative_shift(pos)
        attn = jax.nn.softmax((content + pos) * scale, axis=-1)
        head = jnp.einsum('bhij,bjhd->bihd', attn, v).reshape(B, S, Dm)
        return head @ Wo + bo

    def _L1_ffn_ref(x, shared_up, shared_gate, shared_down, routed_up, routed_gate, routed_down, router_w):
        import jax, jax.numpy as jnp
        import numpy as np
        H = 256
        DFF = 1024
        E_ROUTED = 7
        TOP_K = 2

        def _swiglu(flat, gate_w, up_w, down_w):
            g = flat @ gate_w.T
            up = flat @ up_w.T
            return jax.nn.silu(g) * up @ down_w.T
        orig_shape = x.shape
        flat = x.reshape(-1, H)
        out = _swiglu(flat, shared_gate, shared_up, shared_down)
        logits = flat @ router_w.T
        probs = jax.nn.softmax(logits, axis=-1)
        top_vals, top_idx = jax.lax.top_k(probs, TOP_K)
        top_vals = top_vals / (top_vals.sum(-1, keepdims=True) + 1e-09)
        combine = jnp.sum(jax.nn.one_hot(top_idx, E_ROUTED, dtype=flat.dtype) * top_vals[..., None], axis=1)
        routed = jnp.zeros_like(flat)
        for e in range(E_ROUTED):
            eo = _swiglu(flat, routed_gate[e], routed_up[e], routed_down[e])
            routed = routed + combine[:, e:e + 1] * eo
        return (out + routed).reshape(orig_shape)
    h = _L0_tok_ref(x, L0_tok_weight)
    h = h + _L0_attn_ref(_layernorm(h, axis=-1), L0_attn_Wqkv, L0_attn_bqkv, L0_attn_Wproj, L0_attn_bproj)
    h = h + _L0_ffn_ref(_layernorm(h, axis=-1), L0_ffn_Wq, L0_ffn_bq, L0_ffn_bn_gamma, L0_ffn_bn_beta, L0_ffn_sub_key0, L0_ffn_sub_key1, L0_ffn_expert_down, L0_ffn_expert_up)
    h = h + _L1_attn_ref(_layernorm(h, axis=-1), L1_attn_ln_g, L1_attn_ln_b, L1_attn_Wq, L1_attn_bq, L1_attn_Wk, L1_attn_bk, L1_attn_Wv, L1_attn_bv, L1_attn_Wp, L1_attn_Wo, L1_attn_bo, L1_attn_u_bias, L1_attn_v_bias)
    h = h + _L1_ffn_ref(_layernorm(h, axis=-1), L1_ffn_shared_up, L1_ffn_shared_gate, L1_ffn_shared_down, L1_ffn_routed_up, L1_ffn_routed_gate, L1_ffn_routed_down, L1_ffn_router_w)
    return h

_drawn_inputs = setup_inputs


def setup_inputs(seed=0):
    import zlib

    import numpy as np

    out = dict(_drawn_inputs(seed))
    spreads = {'L0_ffn_bq': (0.0, 0.8),
     'L0_ffn_bn_gamma': (1.0, 0.6),
     'L0_ffn_bn_beta': (0.0, 0.8),
     'L1_attn_ln_g': (1.0, 0.6),
     'L1_attn_ln_b': (0.0, 0.8),
     'L1_attn_bq': (0.0, 0.8),
     'L1_attn_bk': (0.0, 0.8),
     'L1_attn_bv': (0.0, 0.8),
     'L1_attn_bo': (0.0, 0.449)}
    factors = {'L0_attn_bqkv': 8.0,
     'L0_attn_bproj': 8.0,
     'L0_ffn_Wq': 8.0,
     'L0_ffn_sub_key0': 8.0,
     'L0_ffn_sub_key1': 8.0,
     'L0_ffn_expert_down': 8.0,
     'L0_ffn_expert_up': 8.0,
     'L1_attn_Wq': 8.0,
     'L1_attn_Wk': 8.0,
     'L1_attn_Wv': 8.0,
     'L1_attn_Wp': 8.0,
     'L1_attn_Wo': 8.0,
     'L1_attn_u_bias': 8.0,
     'L1_attn_v_bias': 8.0,
     'L1_ffn_shared_up': 8.0,
     'L1_ffn_shared_gate': 8.0,
     'L1_ffn_shared_down': 8.0,
     'L1_ffn_routed_up': 8.0,
     'L1_ffn_routed_gate': 8.0,
     'L1_ffn_routed_down': 8.0,
     'L1_ffn_router_w': 8.0}
    for name, (base, spread) in spreads.items():
        noise = np.random.default_rng([zlib.crc32(name.encode()), seed]).standard_normal(out[name].shape)
        drawn = base * np.exp(spread * noise) if base else spread * noise
        out[name] = jnp.asarray(drawn.astype(out[name].dtype))
    for name, factor in factors.items():
        out[name] = (out[name] * factor).astype(out[name].dtype)
    return out
```

```python
import numpy as np
import concourse.bass as bass
from concourse import mybir
from contextlib import ExitStack

FP32 = mybir.dt.float32
BF16 = mybir.dt.bfloat16
FP16 = mybir.dt.float16
I32 = mybir.dt.int32
ALU = mybir.AluOpType
ACT = mybir.ActivationFunctionType
AX = mybir.AxisListType

P = 128
B, T, C = 16, 256, 256
NT = B * T // P
CK = C // P
V = 50257


class Count:

    def __init__(self, sem, base=0):
        self.sem, self.base, self.n = sem, base, 0

    def then(self, instruction, by=1):
        instruction.then_inc(self.sem, by)
        self.n += by
        return instruction

    def wait(self, engine):
        engine.wait_ge(self.sem, self.base + self.n)


def link(engine, count, instruction):
    count.then(instruction)
    count.wait(engine)


class Room:

    def __init__(self, nc, ctx, stage):
        self.nc, self.ctx, self.stage, self.sems = nc, ctx, stage, []
        ctx.callback(self.close)

    def close(self):
        for sem in self.sems:
            self.nc.gpsimd.sem_clear(sem)
            self.nc.release_semaphore(sem)

    def sb(self, name, shape, dt=FP32):
        return self.ctx.enter_context(self.nc.sbuf_tensor(f"{self.stage}_{name}", shape, dt))

    def ps(self, name, shape, dt=FP32):
        return self.ctx.enter_context(self.nc.psum_tensor(f"{self.stage}_{name}", shape, dt))

    def dma_sem(self, name):
        return self.nc.alloc_semaphore(f"{self.stage}_{name}")

    def sem(self, name):
        self.sems.append(self.nc.alloc_semaphore(f"{self.stage}_{name}"))
        return self.sems[-1]


def embed_stage(nc, ids, table, h):
    WHOLE = V * C // P
    CH = WHOLE // 58
    LOADS = WHOLE // CH
    RING = 6
    with ExitStack() as ctx:
        room = Room(nc, ctx, "emb")
        ring = room.sb("ring", [P, RING, CH])
        idsb = room.sb("ids", [P, NT], I32)
        part = room.sb("part", [P, LOADS])
        top = room.sb("top", [P, 1])
        maxw = room.sb("maxw", [P, 1])
        max2 = room.sb("max2", [P, 1])
        inv = room.sb("inv", [P, 1])
        ids_in = room.sem("ids_in")
        rows_in = room.dma_sem("rows_in")
        slot_in = [room.sem(f"slot_in{r}") for r in range(RING)]
        reduced = room.sem("reduced")
        top_ready = room.sem("top_ready")
        max_ready = room.sem("max_ready")
        dve_done = room.sem("dve_done")
        block = ctx.enter_context(nc.Block())
        flat = table.rearrange("v c -> (v c)").rearrange("(p n) -> p n", p=P)

        @block.sync
        def _(sp):
            sp.dma_start(idsb[:, :], ids).then_inc(ids_in, 16)
            for n in range(LOADS):
                if n >= RING:
                    sp.wait_ge(reduced, n - RING + 1)
                sp.dma_start(ring[:, n % RING, :], flat[:, n * CH:(n + 1) * CH]).then_inc(slot_in[n % RING], 16)

        @block.gpsimd
        def _(pool):
            pool.wait_ge(ids_in, 16)
            for n in range(NT):
                pool.indirect_dma_start(h[:, n, :], None, table[:, :],
                                        bass.IndirectOffsetOnAxis(ap=idsb[:, n:n + 1], axis=0)).then_inc(rows_in, 16)
            pool.wait_ge(top_ready, 1)
            pool.partition_all_reduce(maxw[:, :], top[:, :], P, bass.bass_isa.ReduceOp.max).then_inc(max_ready, 1)

        @block.vector
        def _(dve):
            done = Count(dve_done)
            for n in range(LOADS):
                dve.wait_ge(slot_in[n % RING], 16 * (n // RING + 1))
                dve.tensor_reduce(part[:, n:n + 1], ring[:, n % RING, :], AX.X, ALU.max,
                                  apply_absolute_value=True).then_inc(reduced, 1)
            dve.wait_ge(reduced, LOADS)
            dve.tensor_reduce(top[:, :], part[:, :], AX.X, ALU.max).then_inc(top_ready, 1)
            dve.wait_ge(max_ready, 1)
            dve.wait_ge(rows_in, 16 * NT)
            link(dve, done, dve.tensor_scalar(max2[:, :], maxw[:, :], 2.0, None, ALU.mult))
            link(dve, done, dve.reciprocal(inv[:, :], maxw[:, :]))
            QT = NT // 4
            for q in range(4):
                hq = h[:, q * QT:(q + 1) * QT, :]
                link(dve, done, dve.tensor_scalar(hq, hq, inv[:, 0:1], 0.5, ALU.mult, ALU.mult))
                link(dve, done, dve.tensor_scalar(hq, hq, 0.5, 0.5, ALU.add, ALU.is_gt))
                link(dve, done, dve.tensor_scalar(hq, hq, max2[:, 0:1], maxw[:, 0:1], ALU.mult, ALU.subtract))


def write_stage(nc, h, y, out):
    with ExitStack() as ctx:
        room = Room(nc, ctx, "wr")
        added = room.sem("added")
        out_done = room.sem("out_done")
        block = ctx.enter_context(nc.Block())
        quarter = [slice(q * NT // 4, (q + 1) * NT // 4) for q in range(4)]

        @block.vector
        def _(dve):
            for r in quarter:
                dve.tensor_tensor(h[:, r, :], h[:, r, :], y[:, r, :], ALU.add).then_inc(added, 1)

        @block.sync
        def _(sp):
            tiles = out.rearrange("b (t p) c -> p (b t) c", p=P)
            for q, r in enumerate(quarter):
                sp.wait_ge(added, q + 1)
                sp.dma_start(tiles[:, r, :], h[:, r, :]).then_inc(out_done, 16)
            sp.wait_ge(out_done, 64)


MAGIC = 1.5 * 2.0 ** 23
QMAX = 127.0
EPS = 1e-5
H, DH = 16, 16


def layernorm_stats(dve, count, h, room, sqrt_in, sqrt_out):
    st = room.sb("ln_st", [P, NT, 6])
    mean = room.sb("ln_mean", [P, NT])
    gap = room.sb("ln_gap", [P, NT])
    gap2 = room.sb("ln_gap2", [P, NT])
    var = room.sb("ln_var", [P, NT])
    root = room.sb("ln_root", [P, NT])
    rstd = room.sb("ln_rstd", [P, NT])
    mean_e, mean_o, m2_e, m2_o = st[:, :, 1], st[:, :, 4], st[:, :, 2], st[:, :, 5]

    def on_vector():
        with dve.Fori(0, NT) as n:
            dve.bn_stats(st[:, n, :], h[:, n, :]).then_inc(count.sem, 1)
        count.n += NT
        count.wait(dve)
        link(dve, count, dve.tensor_tensor(gap[:, :], mean_e, mean_o, ALU.subtract))
        link(dve, count, dve.tensor_tensor(mean[:, :], mean_e, mean_o, ALU.add))
        link(dve, count, dve.tensor_tensor(var[:, :], m2_e, m2_o, ALU.add))
        link(dve, count, dve.tensor_tensor(gap2[:, :], gap[:, :], gap[:, :], ALU.mult))
        link(dve, count, dve.tensor_scalar(mean[:, :], mean[:, :], 0.5, None, ALU.mult))
        link(dve, count, dve.tensor_scalar(gap2[:, :], gap2[:, :], 0.25, EPS, ALU.mult, ALU.add))
        dve.scalar_tensor_tensor(var[:, :], var[:, :], 1.0 / C, gap2[:, :], ALU.mult, ALU.add).then_inc(sqrt_in, 1)
        dve.wait_ge(sqrt_out, 1)
        link(dve, count, dve.reciprocal(rstd[:, :], root[:, :]))

    def on_scalar(act):
        act.wait_ge(sqrt_in, 1)
        act.activation(root[:, :], var[:, :], ACT.Sqrt).then_inc(sqrt_out, 1)

    return mean, rstd, on_vector, on_scalar


def split_tokens_T(nc, name, parts, ident):
    GRP = 4
    with ExitStack() as ctx:
        room = Room(nc, ctx, name)
        bank = [room.ps(f"bank{i}", [P, GRP * P]) for i in range(4)]
        turned = room.sem("turned")
        copied_a = room.sem("copied_a")
        copied_d = room.sem("copied_d")
        block = ctx.enter_context(nc.Block())
        jobs = [(s, d, ck) for s, d in parts for ck in range(CK)]
        J = len(jobs)
        assert J in (2, 4)

        @block.tensor
        def _(pe):
            with pe.Fori(0, NT // GRP) as g:
                for j, (src, dst, ck) in enumerate(jobs):
                    pe.wait_ge(copied_a if j % 2 else copied_d, (g * J + j) // 2 + 1 if isinstance(g, int) else g * (J // 2) + j // 2 + 1)
                    for k in range(GRP):
                        last = pe.matmul(bank[j][:, k * P:(k + 1) * P], src[:, g * GRP + k, ck * P:(ck + 1) * P],
                                         ident, start=True, stop=True)
                    last.then_inc(turned, 1)

        def copies(eng, odd, sem, copy):
            eng.sem_inc(sem, J // 2)
            with eng.Fori(0, NT // GRP) as g:
                for j, (src, dst, ck) in enumerate(jobs):
                    if j % 2 == odd:
                        eng.wait_ge(turned, g * J + j + 1)
                        copy(dst[:, ck, bass.ds(g * GRP * P, GRP * P)], bank[j][:, :]).then_inc(sem, 1)

        @block.scalar
        def _(act):
            copies(act, 1, copied_a, act.copy)

        @block.vector
        def _(dve):
            copies(dve, 0, copied_d, dve.tensor_copy)


def quantise(dve, count, out, x, inv):
    link(dve, count, dve.tensor_scalar(x, x, inv, MAGIC, ALU.mult, ALU.add))
    link(dve, count, dve.tensor_scalar(x, x, MAGIC, QMAX, ALU.subtract, ALU.min))
    link(dve, count, dve.tensor_scalar(out, x, -QMAX, None, ALU.max))


def attention0_stage(nc, a, h, ident, side):
    with ExitStack() as outer:
        oroom = Room(nc, outer, "a0")
        xn = oroom.sb("xn", [P, NT, C])
        xT = oroom.sb("xT", [P, CK, NT * P], BF16)
        qk_w = oroom.sb("qk_w", [P, CK, 2 * C], BF16)
        v_w = oroom.sb("v_w", [P, CK, C], BF16)
        o_w = oroom.sb("o_w", [P, CK, C], BF16)
        qk_bias = oroom.sb("qk_bias", [P, 2 * CK])
        v_bias = oroom.sb("v_bias", [P, C])
        o_bias = oroom.sb("o_bias", [P, C])
        scale = oroom.sb("scale", [P, 8])
        S_X, S_QKV, S_O, S_K, S_AO, S_OUT = range(6)

        def col(i):
            return scale[:, i:i + 1]

        with ExitStack() as ctx:
            room = Room(nc, ctx, "a0q")
            xi = room.sb("xi", [P, NT, C], BF16)
            raw = room.sb("raw", [P, CK, 3 * C])
            raw_o = room.sb("raw_o", [P, CK, C])
            top = room.sb("top", [P, 3])
            maxs = room.sb("maxs", [P, 3])
            inv = room.sb("inv", [P, 3])
            loaded = room.sem("loaded")
            tops = room.sem("tops")
            maxed = room.sem("maxed")
            var_ready = room.sem("var_ready")
            root_ready = room.sem("root_ready")
            dve_done = room.sem("dve_done")
            count = Count(dve_done)
            mean, rstd, ln_vector, ln_scalar = layernorm_stats(nc.vector, count, h, room, var_ready, root_ready)
            with nc.Block() as block:

                @block.sync
                def _(sp):
                    sp.dma_start(raw[:, :, :], a["a0_wqkv"].rearrange("(k p) n -> p k n", p=P)).then_inc(loaded, 16)
                    sp.dma_start(raw_o[:, :, :], a["a0_wo"].rearrange("(k p) n -> p k n", p=P)).then_inc(loaded, 16)
                    sp.dma_start(qk_bias[:, :], a["a0_qkb"]).then_inc(loaded, 16)
                    sp.dma_start(v_bias[:, :], a["a0_vb"]).then_inc(loaded, 16)
                    sp.dma_start(o_bias[:, :], a["a0_ob"]).then_inc(loaded, 16)

                @block.scalar
                def _(act):
                    ln_scalar(act)

                @block.gpsimd
                def _(pool):
                    pool.wait_ge(tops, 1)
                    pool.partition_all_reduce(maxs[:, :], top[:, :], P, bass.bass_isa.ReduceOp.max).then_inc(maxed, 1)

                @block.vector
                def _(dve):
                    ln_vector()
                    with dve.Fori(0, NT) as n:
                        dve.tensor_scalar(xn[:, n, :], h[:, n, :], mean[:, bass.ds(n, 1)], rstd[:, bass.ds(n, 1)],
                                          ALU.subtract, ALU.mult).then_inc(dve_done, 1)
                    count.n += NT
                    count.wait(dve)
                    dve.wait_ge(loaded, 80)
                    for i, x in enumerate((xn, raw, raw_o)):
                        link(dve, count, dve.tensor_reduce(top[:, i:i + 1], x[:, :, :], AX.XY, ALU.max,
                                                           apply_absolute_value=True))
                    dve.sem_inc(tops, 1)
                    dve.wait_ge(maxed, 1)
                    link(dve, count, dve.tensor_scalar(scale[:, 0:3], maxs[:, :], 1.0 / QMAX, 1e-8, ALU.mult, ALU.max))
                    link(dve, count, dve.reciprocal(inv[:, :], scale[:, 0:3]))
                    link(dve, count, dve.tensor_tensor(col(S_K), col(S_X), col(S_QKV), ALU.mult))
                    quantise(dve, count, xi[:, :, :], xn[:, :, :], inv[:, 0:1])
                    link(dve, count, dve.tensor_scalar(raw[:, :, :], raw[:, :, :], inv[:, 1:2], MAGIC, ALU.mult, ALU.add))
                    link(dve, count, dve.tensor_scalar(raw[:, :, :], raw[:, :, :], MAGIC, QMAX, ALU.subtract, ALU.min))
                    link(dve, count, dve.tensor_scalar(qk_w[:, :, :], raw[:, :, 0:2 * C], -QMAX, None, ALU.max))
                    link(dve, count, dve.tensor_scalar(v_w[:, :, :], raw[:, :, 2 * C:], -QMAX, None, ALU.max))
                    quantise(dve, count, o_w[:, :, :], raw_o[:, :, :], inv[:, 2:3])

            split_tokens_T(nc, "a0t", [(xi, xT)], ident)

        q_dram = nc.dram_tensor("a0_q", [2, C, NT * P], FP16, kind="Internal").ap()
        k_dram = nc.dram_tensor("a0_k", [2, C, NT * P], FP16, kind="Internal").ap()
        with ExitStack() as ctx:
            vs = Room(nc, ctx, "a0m").sb("vs", [P, NT, H, 2, DH], FP16)
            project_stage(nc, "a0j", (xT,), [((qk_w,), 0, col(S_K), qk_bias[:, 0:CK], q_dram),
                                             ((qk_w,), C, col(S_K), qk_bias[:, CK:], k_dram)],
                          ((v_w,), 0), v_bias, col(S_K), vs, matmul1)
            attend_stage(nc, "a0a", q_dram, k_dram, vs, xn, causal=True, side=side)

        with ExitStack() as ctx:
            room = Room(nc, ctx, "a0p")
            oi = room.sb("oi", [P, NT, C], BF16)
            top = room.sb("top", [P, 1])
            maxs = room.sb("maxs", [P, 1])
            inv = room.sb("inv", [P, 1])
            tops = room.sem("tops")
            maxed = room.sem("maxed")
            dve_done = room.sem("dve_done")
            with nc.Block() as block:

                @block.gpsimd
                def _(pool):
                    pool.wait_ge(tops, 1)
                    pool.partition_all_reduce(maxs[:, :], top[:, :], P, bass.bass_isa.ReduceOp.max).then_inc(maxed, 1)

                @block.vector
                def _(dve):
                    count = Count(dve_done)
                    dve.tensor_reduce(top[:, :], xn[:, :, :], AX.XY, ALU.max, apply_absolute_value=True).then_inc(tops, 1)
                    dve.wait_ge(maxed, 1)
                    link(dve, count, dve.tensor_scalar(col(S_AO), maxs[:, :], 1.0 / QMAX, 1e-8, ALU.mult, ALU.max))
                    link(dve, count, dve.reciprocal(inv[:, :], col(S_AO)))
                    link(dve, count, dve.tensor_tensor(col(S_OUT), col(S_AO), col(S_O), ALU.mult))
                    quantise(dve, count, oi[:, :, :], xn[:, :, :], inv[:, 0:1])

            split_tokens_T(nc, "a0pt", [(oi, xT)], ident)
            pr = [room.ps(f"pr{i}", [P, 2, C]) for i in range(2)]
            pr_ready = room.sem("pr_ready")
            added = room.sem("added")
            with nc.Block() as block:

                @block.tensor
                def _(pe):
                    with pe.Fori(0, NT // 4) as i:
                        for u in range(2):
                            pe.wait_ge(added, i * 2 + u + 1)
                            for t in range(2):
                                for ck in range(CK):
                                    last = pe.matmul(pr[u][:, t, :], xT[:, ck, bass.ds((i * 4 + u * 2 + t) * P, P)], o_w[:, ck, :],
                                                     start=ck == 0, stop=ck == CK - 1)
                            last.then_inc(pr_ready, 1)

                @block.vector
                def _(dve):
                    dve.sem_inc(added, 2)
                    with dve.Fori(0, NT // 4) as i:
                        for u in range(2):
                            rows = h[:, bass.ds(i * 4 + u * 2, 2), :]
                            dve.wait_ge(pr_ready, i * 2 + u + 1)
                            dve.scalar_tensor_tensor(rows, pr[u][:, :, :], col(S_OUT), rows, ALU.mult, ALU.add).then_inc(added, 1)
                    dve.wait_ge(added, 2 + NT // 2)
                    dve.tensor_tensor(h[:, :, :], h[:, :, :], o_bias[:, :].unsqueeze(1).to_broadcast([P, NT, C]), ALU.add)


def constants_stage(nc, ident16b, ident16f):
    with ExitStack() as ctx:
        room = Room(nc, ctx, "cst")
        zeroed = room.sem("zeroed")
        block = ctx.enter_context(nc.Block())

        @block.gpsimd
        def _(pool):
            for n, m in enumerate((ident16b, ident16f)):
                pool.memset(m[:, :], 0.0).then_inc(zeroed, 1)
                pool.wait_ge(zeroed, n + 1)
                pool.affine_select(out=m[:, :], in_=m[:, :], compare_op=ALU.not_equal, fill=1.0, base=0,
                                   pattern=[[-1, P]], channel_multiplier=1)


class Steps:

    def __init__(self, total, c, i=None, unroll=1):
        self.total, self.c, self.i, self.unroll = total, c, i, unroll

    def __call__(self, k):
        return self.i is not None or 0 <= self.c - k < self.total

    def per(self, k, m):
        if self.i is None:
            return (self.c - k) // m
        assert self.unroll % m == 0
        return self.i * (self.unroll // m) + (self.c - k) // m


def steps(engine, total, lag, step, unroll=2):
    head = -(-lag // unroll) * unroll
    assert total % unroll == 0 and total > head
    for s in range(head):
        step(s, s % unroll, Steps(total, s))
    with engine.Fori(0, (total - head) // unroll) as i:
        for u in range(unroll):
            step(i * unroll + head + u, u, Steps(total, head + u, i, unroll))
    for s in range(total, total + lag):
        step(s, s % unroll, Steps(total, s))


def wait(engine, sem, value):
    if not isinstance(value, int) or value > 0:
        engine.wait_ge(sem, value)


def held(engine, value):
    return value if isinstance(value, int) else engine.snap(value)


def matmul3(pe, out, stationary, moving, chunks=CK):
    pairs = [(k, s, m) for k in range(chunks) for s, m in ((0, 0), (0, 1), (1, 0))]
    for j, (k, s, m) in enumerate(pairs):
        last = pe.matmul(out, stationary(s, k), moving(m, k), start=j == 0, stop=j == len(pairs) - 1)
    return last


def matmul1(pe, out, stationary, moving, chunks=CK):
    for k in range(chunks):
        last = pe.matmul(out, stationary(0, k), moving(0, k), start=k == 0, stop=k == chunks - 1)
    return last


def project_stage(nc, stage, xT, dims, v_w, v_bias, v_scale, vs, mm):
    TB = 512
    NB = NT * P // TB
    D = len(dims)
    with ExitStack() as ctx:
        room = Room(nc, ctx, stage)
        ps = [room.ps(f"d{i}", [P, TB]) for i in range(4)]
        pv = [room.ps(f"v{i}", [P, 2, C]) for i in range(4)]
        full = [room.sb(f"full{i}", [P, TB]) for i in range(4)]
        part = [room.sb(f"part{i}", [P, 2, TB], FP16) for i in range(4)]
        vfull = [room.sb(f"vfull{i}", [P, 2, C]) for i in range(2)]
        summed = room.sem("summed")
        taken = room.sem("taken")
        split = room.sem("split")
        hi_done = room.sem("hi_done")
        stored = [room.sem(f"stored{i}") for i in range(4)]
        v_summed = room.sem("v_summed")
        v_taken = room.sem("v_taken")
        v_hi = room.sem("v_hi")
        v_split = room.sem("v_split")
        block = ctx.enter_context(nc.Block())
        jobs = [(d, ck) for d in range(D) for ck in range(CK)]
        J = len(jobs)
        NI = J * NB
        U = J * 2 if J % 4 else J

        def place(u, has):
            d, ck = jobs[u % J]
            return d, ck, has.per(0, J)

        @block.tensor
        def _(pe):
            def step(s, u, has):
                if has(0):
                    d, ck, b = place(u, has)
                    w, col = dims[d][0], dims[d][1]
                    wait(pe, taken, s - 3)
                    mm(pe, ps[u % 4][:, :], lambda q, k: w[q][:, k, col + ck * P:col + (ck + 1) * P],
                       lambda m, k: xT[m][:, k, bass.ds(b * TB, TB)]).then_inc(summed, 1)
            steps(pe, NI, 4, step, U)

            def vstep(s, u, has):
                if has(0):
                    wait(pe, v_taken, s - 3)
                    for t in range(2):
                        last = mm(pe, pv[u][:, t, :], lambda q, k: xT[q][:, k, bass.ds((s * 2 + t) * P, P)],
                                  lambda m, k: v_w[0][m][:, k, v_w[1]:v_w[1] + C])
                    last.then_inc(v_summed, 1)
            steps(pe, NT // 2, 4, vstep, 4)

        @block.scalar
        def _(act):
            def step(s, u, has):
                if has(0):
                    d, ck, b = place(u, has)
                    wait(act, split, s - 3)
                    wait(act, summed, s + 1)
                    act.activation(full[u % 4][:, :], ps[u % 4][:, :], ACT.Identity, bias=dims[d][3][:, ck:ck + 1],
                                   scale=dims[d][2]).then_inc(taken, 1)
            steps(act, NI, 4, step, U)

            def vstep(s, u, has):
                if has(0):
                    wait(act, v_taken, s + 1)
                    act.copy(vs[:, bass.ds(s * 2, 2), :, 0, :], vfull[u % 2][:, :, :].rearrange("p t (h d) -> p t h d", h=H)).then_inc(v_hi, 1)
            steps(act, NT // 2, 4, vstep, 4)

        @block.vector
        def _(dve):
            def step(s, u, has):
                if has(0):
                    wait(dve, taken, s + 1)
                    if not isinstance(s, int) or s >= 4:
                        dve.wait_ge(stored[u % 4], has.per(0, 4) * 16)
                    dve.tensor_copy(part[u % 4][:, 0, :], full[u % 4][:, :]).then_inc(hi_done, 1)
                    dve.wait_ge(hi_done, s + 1)
                    dve.tensor_tensor(part[u % 4][:, 1, :], full[u % 4][:, :], part[u % 4][:, 0, :], ALU.subtract).then_inc(split, 1)
            steps(dve, NI, 4, step, U)

            def vstep(s, u, has):
                if has(0):
                    wait(dve, v_summed, s + 1)
                    wait(dve, v_split, s - 1)
                    dve.scalar_tensor_tensor(vfull[u % 2][:, :, :], pv[u][:, :, :], v_scale,
                                             v_bias[:, :].unsqueeze(1).to_broadcast([P, 2, C]), ALU.mult, ALU.add).then_inc(v_taken, 1)
                if has(1):
                    v = (u - 1) % 4
                    wait(dve, v_hi, s)
                    rows4 = vs[:, bass.ds((s - 1) * 2, 2), :, :, :]
                    dve.tensor_tensor(rows4[:, :, :, 1, :], vfull[v % 2][:, :, :].rearrange("p t (h d) -> p t h d", h=H),
                                      rows4[:, :, :, 0, :], ALU.subtract).then_inc(v_split, 1)
            steps(dve, NT // 2, 4, vstep, 4)

        @block.sync
        def _(sp):
            def step(s, u, has):
                if has(0):
                    d, ck, b = place(u, has)
                    wait(sp, split, s + 1)
                    sp.dma_start(dims[d][4][:, ck * P:(ck + 1) * P, bass.ds(b * TB, TB)].rearrange("q p n -> p q n"),
                                 part[u % 4][:, :, :]).then_inc(stored[u % 4], 16)
            steps(sp, NI, 4, step, U)
            for i in range(4):
                sp.wait_ge(stored[i], NI // 4 * 16)


def attend_stage(nc, stage, qd, kd, vs, ao, causal, pd=None, qvd=None, posd=None, side=None):
    NH = B * H
    PRE = 6
    LEAD = PRE + (8 if pd is not None else 0)
    U = 2 * H
    tiles = [(0, 0), (1, 0), (1, 1)] if causal else [(0, 0), (0, 1), (1, 0), (1, 1)]
    W = len(tiles) * P
    rows_of = [slice(0, P), slice(P, W)] if causal else [slice(0, T), slice(T, W)]
    R = 4 * DH
    with ExitStack() as ctx:
        room = Room(nc, ctx, stage)
        n_st = 3 if pd is not None else 2
        stacks = [[room.sb(f"stack{i}_{b}", [P, H // 2, T], FP16) for b in range(2)] for i in range(n_st)]
        mask = room.sb("mask", [P, W]) if causal else None
        neg = [room.sb(f"neg{i}", [P, W]) for i in range(2)]
        nmax = [room.sb(f"nmax{i}", [P, 2]) for i in range(2)]
        prob = [room.sb(f"prob{i}", [P, W]) for i in range(2)]
        pT = [room.sb(f"pT{i}", [P, 2, W], FP16) for i in range(4)]
        rsum = [room.sb(f"rsum{i}", [P, 2, H]) for i in range(2)]
        rinv = room.sb("rinv", [P, 2, H])
        lows = room.sb("lows", [P, 2, H, DH])
        identf = room.sb("identf", [P, P])
        sc = [room.ps(f"sc{i}", [P, 512]) for i in range(2)]
        tp = [room.ps(f"tp{i}", [P, 512]) for i in range(2)]
        ob = room.ps("ob", [P, 2, H, 2, DH])
        setup, setup2 = room.sem("setup"), room.sem("setup2")
        loaded = [room.sem(f"loaded{b}") for b in range(2)]
        if side:
            side_work = side(room)
        s_ready = room.sem("s_ready")
        masked = room.sem("masked")
        exped = room.sem("exped")
        turned = room.sem("turned")
        hi_done = room.sem("hi_done")
        lo_done = room.sem("lo_done")
        pv_done = room.sem("pv_done")
        o_read = room.sem("o_read")
        norm_done = room.sem("norm_done")
        if pd is not None:
            RING = 32
            pos_dram = posd
            pstack = room.sb("pstack", [P, H // 2, T], FP16)
            pps = [room.ps(f"pps{i}", [P, 512]) for i in range(2)]
            raw = [room.sb(f"raw{i}", [P, 2, T + 1]) for i in range(2)]
            pos = [room.sb(f"pos{i}", [P, W]) for i in range(4)]
            p_loaded = room.sem("p_loaded")
            g_loaded = [room.dma_sem(f"g_loaded{b}") for b in range(2)]
            zeroed = room.sem("zeroed")
            p_ready = room.sem("p_ready")
            p_taken = [room.sem(f"p_taken{i}") for i in range(2)]
            p_out = [room.sem(f"p_out{i}") for i in range(2)]
            p_in = [room.sem(f"p_in{i}") for i in range(4)]
        block = ctx.enter_context(nc.Block())
        LAG = LEAD + 5

        def stack_loads(sp, operand, dst, tok, n):
            for par in range(2):
                for slot in range(4):
                    q = slot // 2 if operand == 1 else slot % 2
                    src = (kd if operand == 1 else qvd if operand == 2 else qd) if operand != 3 else pd
                    if operand == 3:
                        q = slot // 2
                    v = src[q, :, tok].rearrange("(j two d) n -> two d j n", two=2, d=DH)[par]
                    sp.dma_start(dst[par * R + slot * DH:par * R + (slot + 1) * DH, :, :], v).then_inc(n, 16)

        def batch_loads(eng, s, u, has, operands, sems):
            if has(0) and u % H == 0:
                at = held(eng, has.per(0, H) * T)
                if not isinstance(s, int) or s >= 2 * H:
                    eng.wait_ge(s_ready, s - H)
                for o in operands:
                    stack_loads(eng, o, stacks[o][u // H % 2], bass.ds(at, T), sems[u // H % 2])

        @block.sync
        def _(sp):
            if pd is not None:
                stack_loads(sp, 3, pstack, slice(0, T), p_loaded)

            def step(s, u, has):
                batch_loads(sp, s, u, has, [1] if pd is not None else [0, 1], loaded)
                if pd is not None:
                    if has(PRE + 1):
                        v = (u - PRE - 1) % U
                        wait(sp, p_taken[v % 2], has.per(PRE + 1, 2) + 1)
                        sp.dma_start(pos_dram[v, 0:T * (T + 1)].rearrange("(t p c) -> p t c", p=P, t=2),
                                     raw[v % 2][:, :, :]).then_inc(p_out[v % 2], 16)
                    if has(PRE + 4):
                        v = (u - PRE - 4) % U
                        n = s - PRE - 4
                        landed = held(sp, has.per(PRE + 4, 2) * 16 + 16)
                        wait(sp, masked, n - 3)
                        sp.wait_ge(p_out[v % 2], landed)
                        sp.dma_start(pos[v % 4][:, :].rearrange("p (t c) -> p t c", t=2),
                                     pos_dram[v, T:T * (T + 1)].rearrange("(t p c) -> p t c", p=P, t=2)).then_inc(p_in[v % 4], 16)
            steps(sp, NH, LAG, step, U)

        @block.gpsimd
        def _(pool):
            pool.memset(identf[:, :], 0.0).then_inc(setup, 1)
            if causal:
                pool.memset(mask[:, :], 0.0).then_inc(setup, 1)
            pool.wait_ge(setup, 1 + causal)
            pool.affine_select(out=identf[:, :], in_=identf[:, :], compare_op=ALU.not_equal, fill=1.0, base=0,
                               pattern=[[-1, P]], channel_multiplier=1).then_inc(setup2, 1)
            if causal:
                for k0 in (0, 2 * P):
                    pool.affine_select(out=mask[:, k0:k0 + P], in_=mask[:, k0:k0 + P], compare_op=ALU.is_ge,
                                       fill=-1e30, base=0, pattern=[[-1, P]], channel_multiplier=1).then_inc(setup2, 1)
            else:
                for r in raw:
                    pool.memset(r[:, :, 0:1], 0.0).then_inc(zeroed, 1)
                steps(pool, NH, LAG, lambda s, u, has: batch_loads(pool, s, u, has, [2, 0], g_loaded), U)
            if side:
                side_work(pool)

        def item(u, k):
            v = (u - k) % U
            hd = v % H
            return v, hd // 2, slice(hd % 2 * R, hd % 2 * R + R)

        @block.tensor
        def _(pe):
            def arrived(pairs, slot):
                if pd is not None:
                    pe.wait_ge(loaded[slot], (pairs + 1) * 128)
                    pe.wait_ge(g_loaded[slot], (pairs + 1) * 256)
                else:
                    pe.wait_ge(loaded[slot], (pairs + 1) * 256)

            pe.wait_ge(setup2, 3 if causal else 1)
            if pd is not None:
                pe.wait_ge(p_loaded, 128)

            def step(s, u, has):
                if pd is not None and has(PRE):
                    v, j, rr = item(u, PRE)
                    if v % H == 0:
                        b2 = has.per(PRE, U)
                        arrived(b2, v // H)
                    wait(pe, p_taken[v % 2], has.per(PRE, 2))
                    for t in range(2):
                        last = pe.matmul(pps[v % 2][:, t * T:(t + 1) * T], stacks[2][v // H][rr, j, t * P:(t + 1) * P],
                                         pstack[rr, j, :], start=True, stop=True)
                    last.then_inc(p_ready, 1)
                if has(LEAD):
                    v, j, rr = item(u, LEAD)
                    n = s - LEAD
                    if v % H == 0:
                        b2 = has.per(LEAD, U)
                        arrived(b2, v // H)
                    wait(pe, masked, n - 1)
                    for t in range(2):
                        keys_ = slice(0, (t + 1) * P) if causal else slice(0, T)
                        last = pe.matmul(sc[v % 2][:, rows_of[t]], stacks[0][v // H][rr, j, t * P:(t + 1) * P],
                                         stacks[1][v // H][rr, j, keys_], start=True, stop=True)
                    last.then_inc(s_ready, 1)
                if has(LEAD + 2):
                    v, _, _ = item(u, LEAD + 2)
                    n = s - LEAD - 2
                    wait(pe, exped, n + 1)
                    wait(pe, lo_done, n - 1)
                    for k in range(len(tiles)):
                        last = pe.transpose(tp[v % 2][:, k * P:(k + 1) * P], prob[v % 2][:, k * P:(k + 1) * P], identf[:, :])
                    last.then_inc(turned, 1)
                if has(LEAD + 4):
                    v, _, _ = item(u, LEAD + 4)
                    n = s - LEAD - 4
                    if v % H == 0:
                        wait(pe, norm_done, has.per(LEAD + 4, H) * 2)
                    wait(pe, lo_done, n + 1)
                    b2 = has.per(LEAD + 4, H)
                    for t in range(2):
                        mine = [(x, kt) for x, (qt, kt) in enumerate(tiles) if qt == t]
                        for x, kt in mine:
                            for part in range(2):
                                last = pe.matmul(ob[:, t, v % H, :, :], pT[v % 4][:, part, x * P:(x + 1) * P],
                                                 vs[:, bass.ds(b2 * 2 + kt, 1), v % H, :, :].rearrange("p o q d -> p (o q d)"),
                                                 start=(x, kt) == mine[0] and part == 0, stop=(x, kt) == mine[-1] and part == 1)
                    last.then_inc(pv_done, 1)
            steps(pe, NH, LAG, step, U)

        def take_pos(eng, copy, s, v, has):
            n = s - PRE
            wait(eng, p_ready, n + 1)
            if not isinstance(n, int) or n >= 2:
                eng.wait_ge(p_out[v % 2], has.per(PRE, 2) * 16)
            if isinstance(n, int) and n < 2:
                eng.wait_ge(zeroed, 2)
            copy(raw[v % 2][:, :, 1:], pps[v % 2][:, :].rearrange("p (t c) -> p t c", t=2)).then_inc(p_taken[v % 2], 1)

        @block.scalar
        def _(act):
            def step(s, u, has):
                if has(LEAD + 1):
                    v, _, _ = item(u, LEAD + 1)
                    n = s - LEAD - 1
                    wait(act, masked, n + 1)
                    wait(act, turned, n - 1)
                    if v % H == 0:
                        wait(act, o_read, has.per(LEAD + 1, H) - 1)
                    for t in range(2):
                        last = act.activation(prob[v % 2][:, rows_of[t]], neg[v % 2][:, rows_of[t]], ACT.Exp,
                                              bias=nmax[v % 2][:, t:t + 1], scale=-1.0,
                                              accum_out=rsum[v // H][:, t, v % H:v % H + 1])
                    last.then_inc(exped, 1)
                if has(LEAD + 2):
                    v, _, _ = item(u, LEAD + 2)
                    n = s - LEAD - 2
                    wait(act, turned, n + 1)
                    wait(act, pv_done, n - 3)
                    act.copy(pT[v % 4][:, 0, :], tp[v % 2][:, 0:W]).then_inc(hi_done, 1)
                if pd is not None and has(PRE) and u % 2 == 0:
                    v, _, _ = item(u, PRE)
                    take_pos(act, act.copy, s, v, has)
            steps(act, NH, LAG, step, U)

        @block.vector
        def _(dve):
            dve.wait_ge(setup2, 3 if causal else 1)

            def step(s, u, has):
                if has(LEAD):
                    v, n = item(u, LEAD)[0], s - LEAD
                    wait(dve, s_ready, n + 1)
                    wait(dve, exped, n - 1)
                    if pd is not None:
                        dve.wait_ge(p_in[v % 4], has.per(LEAD, 4) * 16 + 16)
                if has(LEAD + 3):
                    v, _, _ = item(u, LEAD + 3)
                    n = s - LEAD - 3
                    wait(dve, hi_done, n + 1)
                    dve.tensor_tensor(pT[v % 4][:, 1, :], tp[v % 2][:, 0:W], pT[v % 4][:, 0, :], ALU.subtract).then_inc(lo_done, 1)
                if has(LEAD):
                    v = item(u, LEAD)[0]
                    other = mask if causal else pos[v % 4]
                    for t in range(2):
                        last = dve.tensor_tensor_reduce(out=neg[v % 2][:, rows_of[t]], in0=sc[v % 2][:, rows_of[t]],
                                                        in1=other[:, rows_of[t]], scale=-DH ** -0.5, scalar=1e38,
                                                        op0=ALU.add, op1=ALU.min, accum_out=nmax[v % 2][:, t:t + 1])
                    last.then_inc(masked, 1)
                if pd is not None and has(PRE) and u % 2 == 1:
                    take_pos(dve, dve.tensor_copy, s, item(u, PRE)[0], has)
                if has(LEAD + 5) and (u - LEAD - 5) % H == H - 1:
                    v = (u - LEAD - 5) % U
                    n = s - LEAD - 5
                    b = has.per(LEAD + 5, H)
                    wait(dve, pv_done, n + 1)
                    wait(dve, exped, n + 1)
                    dve.reciprocal(rinv[:, :, :], rsum[v // H][:, :, :])
                    dve.tensor_copy(lows[:, :, :, :], ob[:, :, :, 1, :]).then_inc(norm_done, 1)
                    dve.wait_ge(norm_done, b * 2 + 1)
                    dve.tensor_tensor(lows[:, :, :, :], lows[:, :, :, :], ob[:, :, :, 0, :], ALU.add).then_inc(norm_done, 1)
                    dve.wait_ge(norm_done, b * 2 + 2)
                    dve.tensor_tensor(ao[:, bass.ds(b * 2, 2), :].rearrange("p t (h d) -> p t h d", h=H), lows[:, :, :, :],
                                      rinv[:, :, :].unsqueeze(3).to_broadcast([P, 2, H, DH]), ALU.mult).then_inc(o_read, 1)
            steps(dve, NH, LAG, step, U)


WSCALE = 64.0


def split_norm_T(nc, stage, h, ident, xhT, xlT, affine=None, gain=None, shift=None, keep=None):
    with ExitStack() as outer:
        oroom = Room(nc, outer, stage)
        if keep:
            xh, xl = keep
        else:
            xh = oroom.sb("xh", [P, NT, C], FP16)
            xl = oroom.sb("xl", [P, NT, C], FP16)
        with ExitStack() as ctx:
            room = Room(nc, ctx, stage + "n")
            xn = room.sb("xn", [P, NT, C])
            gb = room.sb("gb", [P, 2, C])
            dve_done = room.sem("dve_done")
            var_ready = room.sem("var_ready")
            root_ready = room.sem("root_ready")
            var_ready2 = room.sem("var_ready2")
            root_ready2 = room.sem("root_ready2")
            loaded = room.sem("loaded")
            x_ready = room.sem("x_ready")
            xh_ready = room.sem("xh_ready")
            count = Count(dve_done)
            mean, rstd, ln_vector, ln_scalar = layernorm_stats(nc.vector, count, h, room, var_ready, root_ready)
            if affine:
                room.stage += "b"
                mean2, rstd2, ln_vector2, ln_scalar2 = layernorm_stats(nc.vector, count, xn, room, var_ready2, root_ready2)
            block = ctx.enter_context(nc.Block())

            @block.sync
            def _(sp):
                if affine:
                    sp.dma_start(gb[:, 0, :], gain).then_inc(loaded, 16)
                    sp.dma_start(gb[:, 1, :], shift).then_inc(loaded, 16)

            @block.scalar
            def _(act):
                ln_scalar(act)
                if affine:
                    ln_scalar2(act)
                for q in range(4):
                    r = slice(q * NT // 4, (q + 1) * NT // 4)
                    act.wait_ge(x_ready, q + 1)
                    act.copy(xh[:, r, :], xn[:, r, :]).then_inc(xh_ready, 1)

            @block.vector
            def _(dve):
                def apply(dst, src, m, r):
                    with dve.Fori(0, NT) as n:
                        dve.tensor_scalar(dst[:, n, :], src[:, n, :], m[:, bass.ds(n, 1)], r[:, bass.ds(n, 1)],
                                          ALU.subtract, ALU.mult).then_inc(dve_done, 1)
                    count.n += NT
                    count.wait(dve)

                ln_vector()
                apply(xn, h, mean, rstd)
                if affine:
                    ln_vector2()
                    apply(xn, xn, mean2, rstd2)
                    dve.wait_ge(loaded, 32)
                for q in range(4):
                    r = slice(q * NT // 4, (q + 1) * NT // 4)
                    if affine:
                        shape = [P, NT // 4, C]
                        link(dve, count, dve.tensor_tensor(xn[:, r, :], xn[:, r, :], gb[:, 0, :].unsqueeze(1).to_broadcast(shape), ALU.mult))
                        link(dve, count, dve.tensor_tensor(xn[:, r, :], xn[:, r, :], gb[:, 1, :].unsqueeze(1).to_broadcast(shape), ALU.add))
                    dve.sem_inc(x_ready, 1)
                    dve.wait_ge(xh_ready, q + 1)
                    dve.tensor_tensor(xl[:, r, :], xn[:, r, :], xh[:, r, :], ALU.subtract)

        split_tokens_T(nc, stage + "t", [(xh, xhT), (xl, xlT)], ident)


def split_weights(nc, stage, items):
    with ExitStack() as ctx:
        room = Room(nc, ctx, stage)
        raws = [room.sb(f"raw{i}", [P, hi.shape[1], hi.shape[2]]) for i, (_, hi, _) in enumerate(items)]
        loaded = [room.sem(f"loaded{i}") for i in range(len(items))]
        hi_ready = room.sem("hi_ready")
        block = ctx.enter_context(nc.Block())

        @block.sync
        def _(sp):
            for i, (src, hi, _) in enumerate(items):
                sp.dma_start(raws[i][:, :, :], src.rearrange("(k p) n -> p k n", p=P)).then_inc(loaded[i], 16)

        @block.scalar
        def _(act):
            for i, (_, hi, _) in enumerate(items):
                act.wait_ge(loaded[i], 16)
                act.activation(hi[:, :, :], raws[i][:, :, :], ACT.Copy, scale=WSCALE).then_inc(hi_ready, 1)

        @block.vector
        def _(dve):
            for i, (_, hi, lo) in enumerate(items):
                dve.wait_ge(loaded[i], 16)
                dve.wait_ge(hi_ready, i + 1)
                dve.scalar_tensor_tensor(lo[:, :, :], raws[i][:, :, :], WSCALE, hi[:, :, :], ALU.mult, ALU.subtract)


PH, PK, TOP = 8, 32, 4
PG = 4
SEG = 2 * PH
PE_TOP = 8


def experts0_stage(nc, a, h, ident):
    with ExitStack() as outer:
        oroom = Room(nc, outer, "f0")
        NE = PE_TOP * PK
        xhT = oroom.sb("xhT", [P, CK, NT * P], FP16)
        xlT = oroom.sb("xlT", [P, CK, NT * P], FP16)
        split_norm_T(nc, "f0x", h, ident, xhT, xlT)
        xT = (xhT, xlT)
        wq = [oroom.sb(f"wq{i}", [P, CK, PG * P], FP16) for i in range(2)]
        down = [oroom.sb(f"down{i}", [P, CK, NE], FP16) for i in range(2)]
        up = [oroom.sb(f"up{i}", [P, CK, C], FP16) for i in range(2)]
        split_weights(nc, "f0w", [(a["f0_wq"], *wq), (a["f0_down"], *down), (a["f0_up"], *up)])
        qT = oroom.sb("qT", [P, PG, NT * P])
        gel = oroom.sb("gel", [P, NT, NE])
        rnorm = oroom.sb("rnorm", [P, NT, SEG])
        keys = oroom.sb("keys", [P, P])
        qa = oroom.sb("qa", [P, 2])
        blocks = oroom.sb("blocks", [P, SEG // PG])

        TB = 512
        NB = NT * P // TB
        with ExitStack() as ctx:
            room = Room(nc, ctx, "f0q")
            bq = room.sb("bq", [P, PG])
            ps = [room.ps(f"q{i}", [P, TB]) for i in range(4)]
            pg = [room.ps(f"g{i}", [P, 2, NE]) for i in range(2)]
            st = room.sb("st", [P, PG * NB, 6])
            mv = room.sb("mv", [P, PG, 2])
            agg = room.sb("agg", [P, P])
            gnb = room.sb("gnb", [P, 2])
            gm = room.sb("gm", [P, 8])
            key2 = room.sb("key2", [P, P])
            ones = room.sb("ones", [P, P])
            loaded = room.sem("loaded")
            q_in_psum = room.sem("q_in_psum")
            q_done = room.sem("q_done")
            e_in_psum = room.sem("e_in_psum")
            e_done = room.sem("e_done")
            m_ready = room.sem("m_ready")
            m_summed = room.sem("m_summed")
            v_ready = room.sem("v_ready")
            roots = room.sem("roots")
            dve_done = room.sem("dve_done")
            psm = ps[0][:, 0:PG]
            psv = ps[1][:, 0:PG]
            psk = ps[2][:, 0:P]
            block = ctx.enter_context(nc.Block())

            @block.sync
            def _(sp):
                for dst, name in ((bq, "f0_bq"), (gnb, "f0_gnb"), (keys, "f0_keys"), (agg, "f0_agg"), (ones, "f0_ones"),
                                  (blocks, "f0_blocks")):
                    sp.dma_start(dst[:, :], a[name]).then_inc(loaded, 16)

            @block.tensor
            def _(pe):
                with pe.Fori(0, NB) as b:
                    for g in range(PG):
                        pe.wait_ge(q_done, b * PG + g + 1)
                        matmul3(pe, ps[g][:, :], lambda s, k: wq[s][:, k, g * P:(g + 1) * P],
                                lambda m, k: xT[m][:, k, bass.ds(b * TB, TB)]).then_inc(q_in_psum, 1)
                with pe.Fori(0, NT // 4) as i:
                    for u in range(2):
                        pe.wait_ge(e_done, i * 2 + u + 1)
                        for t in range(2):
                            last = matmul3(pe, pg[u][:, t, :], lambda s, k: xT[s][:, k, bass.ds((i * 4 + u * 2 + t) * P, P)],
                                           lambda m, k: down[m][:, k, :])
                        last.then_inc(e_in_psum, 1)
                pe.wait_ge(loaded, 96)
                pe.wait_ge(m_ready, 1)
                pe.matmul(psm, agg[:, :], mv[:, :, 0], start=True, stop=True).then_inc(m_summed, 1)
                pe.wait_ge(m_ready, 2)
                pe.matmul(psv, agg[:, :], mv[:, :, 1], start=True, stop=True).then_inc(m_summed, 1)
                pe.matmul(psk, ones[:, :], key2[:, :], start=True, stop=True).then_inc(m_summed, 1)

            @block.scalar
            def _(act):
                act.sem_inc(q_done, PG)
                act.sem_inc(e_done, 2)
                act.wait_ge(loaded, 96)
                with act.Fori(0, NB) as b:
                    for g in range(PG):
                        act.wait_ge(q_in_psum, b * PG + g + 1)
                        act.activation(qT[:, g, bass.ds(b * TB, TB)], ps[g][:, :], ACT.Identity, bias=bq[:, g:g + 1],
                                       scale=1.0 / WSCALE).then_inc(q_done, 1)
                with act.Fori(0, NT // 4) as i:
                    for u in range(2):
                        act.wait_ge(e_in_psum, i * 2 + u + 1)
                        act.activation(gel[:, bass.ds(i * 4 + u * 2, 2), :], pg[u][:, :, :], ACT.Gelu,
                                       scale=1.0 / WSCALE).then_inc(e_done, 1)
                act.wait_ge(v_ready, 1)
                act.activation(gm[:, 3:4], gm[:, 2:3], ACT.Sqrt)
                act.activation(key2[:, :], psk, ACT.Sqrt).then_inc(roots, 1)

            @block.vector
            def _(dve):
                count = Count(dve_done)
                with dve.Fori(0, NB) as b:
                    for g in range(PG):
                        dve.wait_ge(q_done, b * PG + g + PG + 1)
                        dve.bn_stats(st[:, bass.ds(b + g * NB, 1), :], qT[:, g, bass.ds(b * TB, TB)]).then_inc(dve_done, 1)
                count.n += NB * PG
                count.wait(dve)
                for g in range(PG):
                    link(dve, count, dve.bn_aggr(mv[:, g, :], st[:, g * NB:(g + 1) * NB, :].rearrange("p n s -> p (n s)")))
                dve.sem_inc(m_ready, 1)
                dve.wait_ge(m_summed, 1)
                link(dve, count, dve.tensor_reduce(gm[:, 0:1], psm, AX.X, ALU.add))
                link(dve, count, dve.tensor_scalar(mv[:, :, 0], mv[:, :, 0], gm[:, 0:1], None, ALU.subtract))
                link(dve, count, dve.tensor_tensor(mv[:, :, 0], mv[:, :, 0], mv[:, :, 0], ALU.mult))
                link(dve, count, dve.tensor_tensor(mv[:, :, 1], mv[:, :, 0], mv[:, :, 1], ALU.add))
                dve.wait_ge(loaded, 96)
                link(dve, count, dve.tensor_tensor(key2[:, :], keys[:, :], keys[:, :], ALU.mult))
                dve.sem_inc(m_ready, 1)
                dve.wait_ge(m_summed, 3)
                link(dve, count, dve.tensor_reduce(gm[:, 1:2], psv, AX.X, ALU.add))
                dve.tensor_scalar(gm[:, 2:3], gm[:, 1:2], EPS, None, ALU.add).then_inc(v_ready, 1)
                dve.wait_ge(roots, 1)
                link(dve, count, dve.reciprocal(gm[:, 4:5], gm[:, 3:4]))
                link(dve, count, dve.tensor_tensor(qa[:, 0:1], gm[:, 4:5], gnb[:, 0:1], ALU.mult))
                link(dve, count, dve.tensor_tensor(gm[:, 5:6], gm[:, 0:1], qa[:, 0:1], ALU.mult))
                link(dve, count, dve.tensor_tensor(qa[:, 1:2], gnb[:, 1:2], gm[:, 5:6], ALU.subtract))
                link(dve, count, dve.tensor_scalar(key2[:, :], key2[:, :], 1e-12, None, ALU.max))
                link(dve, count, dve.reciprocal(key2[:, :], key2[:, :]))
                link(dve, count, dve.tensor_tensor(keys[:, :], keys[:, :], key2[:, :], ALU.mult))

        with ExitStack() as ctx:
            room = Room(nc, ctx, "f0n")
            sq = [room.sb(f"sq{i}", [P, PG, P]) for i in range(2)]
            ps = [room.ps(f"n{i}", [P, SEG]) for i in range(2)]
            squared = room.sem("squared")
            summed = room.sem("summed")
            taken = room.sem("taken")
            root = room.sem("root")
            dve_done = room.sem("dve_done")
            block = ctx.enter_context(nc.Block())

            @block.scalar
            def _(act):
                def step(s, u, has):
                    wait(act, summed, s - 1)
                    act.activation(sq[u][:, :, :], qT[:, :, bass.ds(s * P, P)], ACT.Square, bias=qa[:, 1:2],
                                   scale=qa[:, 0:1]).then_inc(squared, 1)
                steps(act, NT, 2, lambda s, u, has: step(s, u, has) if has(0) else None)
                act.wait_ge(taken, NT)
                act.activation(rnorm[:, :, :], rnorm[:, :, :], ACT.Sqrt).then_inc(root, 1)

            @block.tensor
            def _(pe):
                def step(s, u, has):
                    wait(pe, squared, s + 1)
                    wait(pe, taken, s - 1)
                    for g in range(PG):
                        last = pe.matmul(ps[u][:, g * 4:(g + 1) * 4], sq[u][:, g, :], blocks[:, :], start=True, stop=True)
                    last.then_inc(summed, 1)
                steps(pe, NT, 2, lambda s, u, has: step(s, u, has) if has(0) else None)

            @block.vector
            def _(dve):
                def step(s, u, has):
                    wait(dve, summed, s + 1)
                    dve.tensor_copy(rnorm[:, bass.ds(s, 1), :], ps[u][:, :]).then_inc(taken, 1)
                steps(dve, NT, 2, lambda s, u, has: step(s, u, has) if has(0) else None)
                count = Count(dve_done)
                dve.wait_ge(root, 1)
                link(dve, count, dve.tensor_scalar(rnorm[:, :, :], rnorm[:, :, :], 1e-12, None, ALU.max))
                link(dve, count, dve.reciprocal(rnorm[:, :, :], rnorm[:, :, :]))

        with ExitStack() as ctx:
            room = Room(nc, ctx, "f0s")
            PAD = PK + TOP
            SENT, GONE = 9.0, -9.0
            qn = [room.sb(f"qn{i}", [P, PG, P]) for i in range(2)]
            s36 = [room.sb(f"s36_{i}", [P, SEG, PAD]) for i in range(2)]
            left = [room.sb(f"left{i}", [P, SEG, PAD]) for i in range(2)]
            top8 = [room.sb(f"top8_{i}", [P, SEG, 8]) for i in range(2)]
            gap = [room.sb(f"gap{i}", [P, SEG, PK]) for i in range(2)]
            ex = gap
            wt = [room.sb(f"wt{i}", [P, SEG, PK]) for i in range(2)]
            total = [room.sb(f"total{i}", [P, SEG]) for i in range(2)]
            tail = [room.sb(f"tail{i}", [P, 1]) for i in range(2)]
            prod = room.sb("prod", [P, PH, PE_TOP, PK])
            coef = [room.sb(f"coef{i}", [P, NE]) for i in range(2)]
            ch = [room.sb(f"ch{i}", [P, NE], FP16) for i in range(2)]
            cl = [room.sb(f"cl{i}", [P, NE], FP16) for i in range(2)]
            chT = [room.sb(f"chT{i}", [P, 2, CK, P], FP16) for i in range(2)]
            ps_s = [room.ps(f"s{i}", [P, PG * P]) for i in range(2)]
            ps_t = [room.ps(f"t{i}", [P, 2, CK, P]) for i in range(2)]
            ps_o = [room.ps(f"o{i}", [P, C]) for i in range(2)]
            qn_ready, s_ready, s_taken = room.sem("qn_ready"), room.sem("s_ready"), room.sem("s_taken")
            gap_ready, ex_ready, coef_ready = room.sem("gap_ready"), room.sem("ex_ready"), room.sem("coef_ready")
            t_ready, cT_ready, o_ready, o_taken = room.sem("t_ready"), room.sem("cT_ready"), room.sem("o_ready"), room.sem("o_taken")
            wt_ready, cf_ready, ch_ready = room.sem("wt_ready"), room.sem("cf_ready"), room.sem("ch_ready")
            pool_done, one_ready = room.sem("pool_done"), room.sem("one_ready")
            one, gel_last = room.sb("one", [P, 1]), [room.sb(f"gel_last{i}", [P, 1]) for i in range(2)]
            sent_ready = room.sem("sent_ready")
            dve_done = room.sem("dve_done")
            block = ctx.enter_context(nc.Block())

            @block.scalar
            def _(act):
                def step(s, u, has):
                    if has(0):
                        wait(act, s_ready, s - 1)
                        act.activation(qn[u][:, :, :], qT[:, :, bass.ds(s * P, P)], ACT.Identity, bias=qa[:, 1:2],
                                       scale=qa[:, 0:1]).then_inc(qn_ready, 1)
                    if has(2):
                        wait(act, gap_ready, s - 1)
                        act.activation(ex[u][:, :, :], gap[u][:, :, :], ACT.Exp).then_inc(ex_ready, 1)
                    if has(5):
                        wait(act, t_ready, s - 4)
                        act.copy(chT[1 - u][:, :, :, :], ps_t[1 - u][:, :, :, :]).then_inc(cT_ready, 1)
                    if has(4):
                        wait(act, cf_ready, s - 3)
                        wait(act, t_ready, s - 5)
                        act.copy(ch[u][:, :], coef[u][:, :]).then_inc(ch_ready, 1)
                steps(act, NT, 6, step)

            @block.tensor
            def _(pe):
                def step(s, u, has):
                    if has(0):
                        wait(pe, qn_ready, s + 1)
                        wait(pe, s_taken, s - 1)
                        for g in range(PG):
                            last = pe.matmul(ps_s[u][:, g * P:(g + 1) * P], qn[u][:, g, :], keys[:, :], start=True, stop=True)
                        last.then_inc(s_ready, 1)
                    if has(4):
                        wait(pe, coef_ready, s - 3)
                        wait(pe, cT_ready, s - 5)
                        for part, c in enumerate((ch[u], cl[u])):
                            for k in range(CK):
                                last = pe.matmul(ps_t[u][:, part, k, :], c[:, k * P:(k + 1) * P], ident, start=True, stop=True)
                        last.then_inc(t_ready, 1)
                    if has(5):
                        v = 1 - u
                        wait(pe, cT_ready, s - 4)
                        wait(pe, o_taken, s - 6)
                        matmul3(pe, ps_o[v][:, :], lambda p, k: chT[v][:, p, k, :], lambda m, k: up[m][:, k, :]).then_inc(o_ready, 1)
                steps(pe, NT, 6, step)

            @block.gpsimd
            def _(pool):
                PCH = 7

                pool.memset(one[:, :], 1.0).then_inc(one_ready, 1)
                pool.wait_ge(one_ready, 1)

                def step(s, u, has):
                    if has(1):
                        v = 1 - u
                        count = Count(pool_done, (s - 1) * PCH)
                        w4 = wt[v][:, :, :].rearrange("p (h two) k -> p h two k", two=2)
                        w0, w1 = w4[:, :, 0, 0:PE_TOP], w4[:, :, 1, :]
                        shape = [P, PH, PE_TOP, PK]
                        gel_n = gel[:, bass.ds(s - 1, 1), :].rearrange("p o e -> p (o e)")
                        count.then(pool.tensor_tensor(gel_last[v][:, :], gel_n[:, NE - 1:], one[:, :], ALU.mult))
                        wait(pool, coef_ready, s - 2)
                        wait(pool, wt_ready, s)
                        link(pool, count, pool.tensor_tensor(prod[:, :, :, :], w0.unsqueeze(3).to_broadcast(shape),
                                                             w1.unsqueeze(2).to_broadcast(shape), ALU.mult))
                        link(pool, count, pool.tensor_tensor(prod[:, 0:4, :, :], prod[:, 0:4, :, :], prod[:, 4:8, :, :], ALU.add))
                        link(pool, count, pool.tensor_tensor(prod[:, 0:2, :, :], prod[:, 0:2, :, :], prod[:, 2:4, :, :], ALU.add))
                        cf = coef[v][:, :]
                        link(pool, count, pool.tensor_tensor(cf, prod[:, 0, :, :], prod[:, 1, :, :], ALU.add))
                        count.then(pool.tensor_tensor(cf[:, NE - 1:], cf[:, NE - 1:], tail[v][:, :], ALU.add))
                        link(pool, count, pool.tensor_tensor(cf[:, :NE - 1], cf[:, :NE - 1], gel_n[:, :NE - 1], ALU.mult))
                        pool.tensor_tensor(cf[:, NE - 1:], cf[:, NE - 1:], gel_last[v][:, :], ALU.mult).then_inc(cf_ready, 1)
                steps(pool, NT, 1, step)

            @block.vector
            def _(dve):
                KCH = 7

                def step(s, u, has):
                    count = Count(dve_done, s * KCH)

                    if has(1):
                        wait(dve, s_ready, s)
                        dve.tensor_tensor(s36[1 - u][:, :, 0:PK], ps_s[1 - u][:, :].rearrange("p (s k) -> p s k", k=PK),
                                          rnorm[:, bass.ds(s - 1, 1), :].rearrange("p o s -> p (o s)").unsqueeze(2).to_broadcast([P, SEG, PK]),
                                          ALU.mult).then_inc(s_taken, 1)
                        dve.wait_ge(sent_ready, 2)
                        dve.wait_ge(s_taken, s)
                        for j in range(SEG):
                            last = dve.max(top8[1 - u][:, j, :], s36[1 - u][:, j, 0:PK])
                        link(dve, count, last)
                        link(dve, count, dve.memset(top8[1 - u][:, :, TOP:], SENT))
                        dve.tensor_tensor(gap[1 - u][:, :, :], s36[1 - u][:, :, 0:PK], top8[1 - u][:, :, 0:1].to_broadcast([P, SEG, PK]),
                                          ALU.subtract).then_inc(gap_ready, 1)
                        for j in range(SEG):
                            last = dve.match_replace(left[1 - u][:, j, :], top8[1 - u][:, j, :], s36[1 - u][:, j, :], GONE)
                        link(dve, count, last)
                    else:
                        dve.sem_inc(dve_done, 3)
                        count.n = 3
                    if has(2):
                        v = u
                        wait(dve, ex_ready, s - 1)
                        keep = left[v][:, :, 0:PK]
                        link(dve, count, dve.scalar_tensor_tensor(ex[v][:, :, :], keep, GONE, ex[v][:, :, :], ALU.is_equal, ALU.mult))
                        link(dve, count, dve.tensor_reduce(total[v][:, :], ex[v][:, :, :], AX.X, ALU.add))
                        link(dve, count, dve.reciprocal(total[v][:, :], total[v][:, :]))
                        wait(dve, cf_ready, s - 3)
                        link(dve, count, dve.tensor_tensor(wt[v][:, :, :], ex[v][:, :, :],
                                                           total[v][:, :].unsqueeze(2).to_broadcast([P, SEG, PK]), ALU.mult))
                        w0 = wt[v][:, :, :].rearrange("p (h two) k -> p h two k", two=2)[:, :, 0, PE_TOP:]
                        dve.tensor_reduce(tail[v][:, :], w0, AX.XY, ALU.add).then_inc(wt_ready, 1)
                    else:
                        dve.sem_inc(dve_done, 4)
                        count.n += 4
                    if has(4):
                        v = u
                        wait(dve, ch_ready, s - 3)
                        dve.tensor_tensor(cl[v][:, :], coef[v][:, :], ch[v][:, :], ALU.subtract).then_inc(coef_ready, 1)
                    if has(6):
                        v = u
                        row = h[:, bass.ds(s - 6, 1), :].rearrange("p o c -> p (o c)")
                        wait(dve, o_ready, s - 5)
                        dve.scalar_tensor_tensor(row, ps_o[v][:, :], 1.0 / WSCALE, row, ALU.mult, ALU.add).then_inc(o_taken, 1)
                    assert count.n == KCH

                for i in range(2):
                    dve.memset(s36[i][:, :, PK:], SENT).then_inc(sent_ready, 1)
                steps(dve, NT, 6, step)


def attention1_stage(nc, a, h, ident):
    with ExitStack() as outer:
        oroom = Room(nc, outer, "a1")
        ao = oroom.sb("ao", [P, NT, C])
        wo = [oroom.sb(f"wo{i}", [P, CK, C], FP16) for i in range(2)]
        dram = {n: nc.dram_tensor(f"a1_{n}", [2, C, t], FP16, kind="Internal").ap()
                for n, t in (("q", NT * P), ("qv", NT * P), ("k", NT * P), ("p", T))}
        pos = nc.dram_tensor("a1_pos", [2 * H, T * (T + 1)], FP32, kind="Internal").ap()
        with ExitStack() as mid:
            vs = Room(nc, mid, "a1m").sb("vs", [P, NT, H, 2, DH], FP16)
            with ExitStack() as ctx:
                room = Room(nc, ctx, "a1x")
                xT = [room.sb(f"xT{i}", [P, CK, NT * P], FP16) for i in range(2)]
                split_norm_T(nc, "a1n", h, ident, *xT, affine=True, gain=a["a1_g"], shift=a["a1_b"])
                w = {n: [room.sb(f"w{n}{i}", [P, CK, C], FP16) for i in range(2)] for n in ("q", "k", "v", "p")}
                pe_parts = [room.sb(f"pe{i}", [P, CK, T], FP16) for i in range(2)]
                split_weights(nc, "a1w", [(a[f"a1_w{n}"], *w[n]) for n in ("q", "k", "v", "p")]
                              + [(a["a1_wo"], *wo), (a["a1_pe"], *pe_parts)])
                bias = room.sb("bias", [P, 5, CK])
                v_bias = room.sb("v_bias", [P, C])
                full = room.sb("full", [P, CK, T])
                part = room.sb("part", [P, 2, CK, T], FP16)
                loaded, summed, taken, hi_done, split, stored, biased = (
                    room.sem(n) for n in ("loaded", "summed", "taken", "hi_done", "split", "stored", "biased"))
                with ExitStack() as pctx:
                    ps = Room(nc, pctx, "a1p").ps("p", [P, CK, T])
                    block = pctx.enter_context(nc.Block())

                    @block.sync
                    def _(sp):
                        sp.dma_start(bias[:, 0:4, :], a["a1_qkuv"]).then_inc(loaded, 16)
                        sp.dma_start(v_bias[:, :], a["a1_bv"]).then_inc(loaded, 16)
                        sp.wait_ge(split, 1)
                        for ck in range(CK):
                            sp.dma_start(dram["p"][:, ck * P:(ck + 1) * P, :].rearrange("q p n -> p q n"),
                                         part[:, :, ck, :]).then_inc(stored, 16)
                        sp.wait_ge(stored, 16 * CK)

                    @block.tensor
                    def _(pe):
                        for ck in range(CK):
                            last = matmul3(pe, ps[:, ck, :], lambda q, k: w["p"][q][:, k, ck * P:(ck + 1) * P],
                                           lambda m, k: pe_parts[m][:, k, :])
                        last.then_inc(summed, 1)

                    @block.scalar
                    def _(act):
                        act.wait_ge(summed, 1)
                        act.activation(full[:, :, :], ps[:, :, :], ACT.Copy, scale=WSCALE ** -2).then_inc(taken, 1)

                    @block.vector
                    def _(dve):
                        dve.wait_ge(loaded, 32)
                        dve.tensor_tensor(bias[:, 2, :], bias[:, 2, :], bias[:, 0, :], ALU.add)
                        dve.tensor_tensor(bias[:, 3, :], bias[:, 3, :], bias[:, 0, :], ALU.add)
                        dve.wait_ge(taken, 1)
                        dve.tensor_copy(part[:, 0, :, :], full[:, :, :]).then_inc(hi_done, 1)
                        dve.wait_ge(hi_done, 1)
                        dve.tensor_tensor(part[:, 1, :, :], full[:, :, :], part[:, 0, :, :], ALU.subtract).then_inc(split, 1)

                s = 1.0 / WSCALE
                project_stage(nc, "a1j", xT, [(w["q"], 0, s, bias[:, 2, :], dram["q"]),
                                              (w["q"], 0, s, bias[:, 3, :], dram["qv"]),
                                              (w["k"], 0, s, bias[:, 1, :], dram["k"])],
                              (w["v"], 0), v_bias, s, vs, matmul3)
            attend_stage(nc, "a1a", dram["q"], dram["k"], vs, ao, causal=False, pd=dram["p"], qvd=dram["qv"], posd=pos)

        with ExitStack() as ctx:
            room = Room(nc, ctx, "a1o")
            x = [room.sb(f"x{i}", [P, NT, C], FP16) for i in range(2)]
            xT = [room.sb(f"xT{i}", [P, CK, NT * P], FP16) for i in range(2)]
            o_bias = room.sb("o_bias", [P, C])
            hi_done, loaded, pr_ready, added = (room.sem(n) for n in ("hi_done", "loaded", "pr_ready", "added"))
            with nc.Block() as block:
                quarter = [slice(q * NT // 4, (q + 1) * NT // 4) for q in range(4)]

                @block.sync
                def _(sp):
                    sp.dma_start(o_bias[:, :], a["a1_bo"]).then_inc(loaded, 16)
                    sp.wait_ge(loaded, 16)

                @block.scalar
                def _(act):
                    for r in quarter:
                        act.copy(x[0][:, r, :], ao[:, r, :]).then_inc(hi_done, 1)

                @block.vector
                def _(dve):
                    for q, r in enumerate(quarter):
                        dve.wait_ge(hi_done, q + 1)
                        dve.tensor_tensor(x[1][:, r, :], ao[:, r, :], x[0][:, r, :], ALU.subtract)

            split_tokens_T(nc, "a1ot", [(x[0], xT[0]), (x[1], xT[1])], ident)
            pr = [room.ps(f"pr{i}", [P, 2, C]) for i in range(2)]
            with nc.Block() as block:

                @block.tensor
                def _(pe):
                    def step(s, u, has):
                        if has(0):
                            wait(pe, added, s - 1)
                            for t in range(2):
                                last = matmul3(pe, pr[u][:, t, :], lambda q, k: xT[q][:, k, bass.ds((s * 2 + t) * P, P)],
                                               lambda m, k: wo[m][:, k, :])
                            last.then_inc(pr_ready, 1)
                    steps(pe, NT // 2, 2, step)

                @block.vector
                def _(dve):
                    def step(s, u, has):
                        if has(0):
                            rows2 = h[:, bass.ds(s * 2, 2), :]
                            wait(dve, pr_ready, s + 1)
                            dve.scalar_tensor_tensor(rows2, pr[u][:, :, :], 1.0 / WSCALE, rows2, ALU.mult, ALU.add).then_inc(added, 1)
                    steps(dve, NT // 2, 2, step)
                    dve.wait_ge(added, NT // 2)
                    dve.tensor_tensor(h[:, :, :], h[:, :, :], o_bias[:, :].unsqueeze(1).to_broadcast([P, NT, C]), ALU.add)


ER = 7
E8 = 8
F = 1024
FC = F // P
TT = 256
TK = TT // P
PAIRS = 2 * NT * P
RT = (PAIRS + ER * (TT - 1)) // TT
GU, DN = 2 * CK * F, FC * C


def split_experts(nc, src, dst):
    CUTS = 3
    CUT = (GU + DN) // CUTS
    ITEMS = E8 * CUTS

    def side(room):
        raw = [room.sb(f"raw{i}", [P, CUT]) for i in range(2)]
        part = [room.sb(f"part{i}", [P, 2, CUT], FP16) for i in range(2)]
        w_loaded = [room.dma_sem(f"w_loaded{i}") for i in range(2)]
        w_stored = [room.dma_sem(f"w_stored{i}") for i in range(2)]
        w_scaled, w_split = room.sem("w_scaled"), room.sem("w_split")
        factor = room.sb("factor", [P, 1])

        def work(pool):
            pool.memset(factor[:, :], WSCALE).then_inc(w_scaled, 1)
            pool.wait_ge(w_scaled, 1)

            def step(s, u, has):
                if has(0):
                    wait(pool, w_split, s - 1)
                    cut = slice(u % CUTS * CUT, (u % CUTS + 1) * CUT)
                    pool.dma_start(raw[u % 2][:, :], src[bass.ds(has.per(0, CUTS), 1), :, cut]
                                   .rearrange("e p n -> p (e n)")).then_inc(w_loaded[u % 2], 16)
                if has(1):
                    v = (u - 1) % (2 * CUTS)
                    cut = slice(v % CUTS * CUT, (v % CUTS + 1) * CUT)
                    pool.wait_ge(w_loaded[v % 2], has.per(1, 2) * 16 + 16)
                    if not isinstance(s, int) or s >= 3:
                        pool.wait_ge(w_stored[v % 2], has.per(1, 2) * 16)
                    by = factor[:, 0:1].to_broadcast([P, CUT])
                    pool.tensor_tensor(part[v % 2][:, 0, :], raw[v % 2][:, :], by, ALU.mult).then_inc(w_scaled, 1)
                    pool.tensor_tensor(raw[v % 2][:, :], raw[v % 2][:, :], by, ALU.mult).then_inc(w_scaled, 1)
                    pool.wait_ge(w_scaled, s * 2 + 1)
                    pool.tensor_tensor(part[v % 2][:, 1, :], raw[v % 2][:, :], part[v % 2][:, 0, :],
                                       ALU.subtract).then_inc(w_split, 1)
                    pool.wait_ge(w_split, s)
                    pool.dma_start(dst[bass.ds(has.per(1, CUTS), 1), :, :, cut].rearrange("e p q n -> p (e q) n"),
                                   part[v % 2][:, :, :]).then_inc(w_stored[v % 2], 16)
            steps(pool, ITEMS, 1, step, 2 * CUTS)
            for i in range(2):
                pool.wait_ge(w_stored[i], ITEMS // 2 * 16)

        return work

    return side


def route_stage(nc, a, xT, slots, coef, tile_expert, x_sorted):
    with ExitStack() as ctx:
        room = Room(nc, ctx, "rt")
        wr = [room.sb(f"wr{i}", [P, CK, E8], FP16) for i in range(2)]
        raw = room.sb("raw", [P, CK, E8])
        zero = room.sb("zero", [P, 2 * C], FP16)
        before = room.sb("before", [P, P])
        ones = room.sb("ones", [P, P])
        lane = room.sb("lane", [P, E8])
        tile_no = room.sb("tile_no", [1, RT, E8])
        big = lambda n, dt=FP32: room.sb(n, [P, NT, E8], dt)
        logit, prob, top, hot1, hot2, hot, scan0, scan1, rank, pick = (
            big(n) for n in ("logit", "prob", "top", "hot1", "hot2", "hot", "scan0", "scan1", "rank", "pick"))
        index = big("index", mybir.dt.uint32)
        indexf = big("indexf")
        small = room.sb("small", [P, 4, NT])
        slotf = room.sb("slotf", [P, NT, 2])
        per_e = room.sb("per_e", [P, 6, E8])
        ge = room.sb("ge", [1, RT, E8])
        texp = room.sb("texp", [1, RT])
        ps = room.ps("l", [P, NT, E8])
        pp = room.ps("p", [P, 2, NT, E8])
        loaded, zeroed, hi_done, w_split, l_ready, gap_ready, e_ready, hot_ready, p_ready, z_stored, dve_done = (
            room.sem(n) for n in ("loaded", "zeroed", "hi_done", "w_split", "l_ready", "gap_ready", "e_ready",
                                  "hot_ready", "p_ready", "z_stored", "dve_done"))
        block = ctx.enter_context(nc.Block())

        @block.sync
        def _(sp):
            sp.dma_start(raw[:, :, :], a["m_router"].rearrange("(k p) e -> p k e", p=P)).then_inc(loaded, 16)
            for dst, name in ((before, "m_before"), (ones, "m_ones"), (lane, "m_lane")):
                sp.dma_start(dst[:, :], a[name]).then_inc(loaded, 16)
            sp.dma_start(tile_no[:, :, :], a["m_tile_no"]).then_inc(loaded, 16)
            sp.wait_ge(zeroed, 1)
            sp.dma_start(x_sorted.rearrange("(t p) c -> p t c", p=P),
                         zero[:, :].unsqueeze(1).to_broadcast([P, RT * TK, 2 * C])).then_inc(z_stored, 16)
            sp.wait_ge(z_stored, 16)

        @block.gpsimd
        def _(pool):
            pool.memset(zero[:, :], 0.0).then_inc(zeroed, 1)

        @block.tensor
        def _(pe):
            pe.wait_ge(w_split, 1)
            with pe.Fori(0, NT) as n:
                for k, (s, m) in enumerate([(0, 0), (0, 1), (1, 0)] * CK):
                    ck = k // 3
                    last = pe.matmul(ps[:, bass.ds(n, 1), :].rearrange("p o e -> p (o e)"), xT[s][:, ck, bass.ds(n * P, P)],
                                     wr[m][:, ck, :], start=k == 0, stop=k == 3 * CK - 1)
                last.then_inc(l_ready, 1)
            pe.wait_ge(loaded, 80)
            pe.wait_ge(hot_ready, 1)
            pe.matmul(pp[:, 0, :, :], before[:, :], hot[:, :, :], start=True, stop=True)
            pe.matmul(pp[:, 1, :, :], ones[:, :], hot[:, :, :], start=True, stop=True).then_inc(p_ready, 1)

        @block.scalar
        def _(act):
            act.wait_ge(loaded, 80)
            act.activation(wr[0][:, :, :], raw[:, :, :], ACT.Copy, scale=WSCALE).then_inc(hi_done, 1)
            act.wait_ge(gap_ready, 1)
            act.activation(prob[:, :, :], prob[:, :, :], ACT.Exp).then_inc(e_ready, 1)

        @block.vector
        def _(dve):
            count = Count(dve_done)
            wide = [P, NT, E8]

            def tt(out, x, y, op):
                link(dve, count, dve.tensor_tensor(out, x, y, op))

            dve.wait_ge(hi_done, 1)
            dve.scalar_tensor_tensor(wr[1][:, :, :], raw[:, :, :], WSCALE, wr[0][:, :, :], ALU.mult, ALU.subtract).then_inc(w_split, 1)
            dve.wait_ge(l_ready, NT)
            link(dve, count, dve.tensor_scalar(logit[:, :, :], ps[:, :, :], 1.0 / WSCALE, None, ALU.mult))
            link(dve, count, dve.memset(logit[:, :, ER:], -1e30))
            link(dve, count, dve.tensor_reduce(small[:, 0, :], logit[:, :, :], AX.X, ALU.max))
            dve.tensor_tensor(prob[:, :, :], logit[:, :, :], small[:, 0, :].unsqueeze(2).to_broadcast(wide), ALU.subtract).then_inc(gap_ready, 1)
            dve.wait_ge(e_ready, 1)
            link(dve, count, dve.tensor_reduce(small[:, 1, :], prob[:, :, :], AX.X, ALU.add))
            link(dve, count, dve.reciprocal(small[:, 1, :], small[:, 1, :]))
            tt(prob[:, :, :], prob[:, :, :], small[:, 1, :].unsqueeze(2).to_broadcast(wide), ALU.mult)
            for n in range(NT):
                last = dve.max(top[:, n, :], prob[:, n, :])
            link(dve, count, last)
            for n in range(NT):
                last = dve.max_index(index[:, n, :], top[:, n, :], prob[:, n, :])
            link(dve, count, last)
            link(dve, count, dve.tensor_copy(indexf[:, :, :], index[:, :, :]))
            lanes = lane[:, :].unsqueeze(1).to_broadcast(wide)
            dve.tensor_tensor(hot1[:, :, :], indexf[:, :, 0:1].to_broadcast(wide), lanes, ALU.is_equal)
            tt(hot2[:, :, :], indexf[:, :, 1:2].to_broadcast(wide), lanes, ALU.is_equal)
            dve.tensor_tensor(hot[:, :, :], hot1[:, :, :], hot2[:, :, :], ALU.add).then_inc(hot_ready, 1)
            tt(small[:, 2, :], top[:, :, 0], top[:, :, 1], ALU.add)
            link(dve, count, dve.tensor_scalar(small[:, 2, :], small[:, 2, :], 1e-9, None, ALU.add))
            link(dve, count, dve.reciprocal(small[:, 2, :], small[:, 2, :]))
            tt(coef[:, :, :], top[:, :, 0:2], small[:, 2, :].unsqueeze(2).to_broadcast([P, NT, 2]), ALU.mult)
            dve.wait_ge(p_ready, 1)
            link(dve, count, dve.tensor_copy(scan0[:, :, :], pp[:, 1, :, :]))
            x, y, d = scan0, scan1, 1
            while d < NT:
                dve.tensor_copy(y[:, 0:d, :], x[:, 0:d, :])
                tt(y[:, d:, :], x[:, d:, :], x[:, 0:NT - d, :], ALU.add)
                x, y, d = y, x, 2 * d
            need, end, end2, first = (per_e[:, i, :] for i in range(4))
            link(dve, count, dve.tensor_scalar(need, x[:, NT - 1, :], TT - 1.0, 1.0 / TT, ALU.add, ALU.mult))
            link(dve, count, dve.tensor_scalar(need, need, -(0.5 - 0.5 / TT), MAGIC, ALU.add, ALU.add))
            link(dve, count, dve.tensor_scalar(need, need, MAGIC, None, ALU.subtract))
            link(dve, count, dve.tensor_copy(end, need))
            u, w, d = end, end2, 1
            while d < E8:
                dve.tensor_copy(w[:, 0:d], u[:, 0:d])
                tt(w[:, d:], u[:, d:], u[:, 0:E8 - d], ALU.add)
                u, w, d = w, u, 2 * d
            tt(first, u, need, ALU.subtract)
            link(dve, count, dve.tensor_scalar(first, first, float(TT), None, ALU.mult))
            tt(y[:, :, :], x[:, :, :], pp[:, 1, :, :], ALU.subtract)
            tt(rank[:, :, :], y[:, :, :], pp[:, 0, :, :], ALU.add)
            tt(rank[:, :, :], rank[:, :, :], first.unsqueeze(1).to_broadcast(wide), ALU.add)
            for i, hot_i in enumerate((hot1, hot2)):
                tt(pick[:, :, :], rank[:, :, :], hot_i[:, :, :], ALU.mult)
                link(dve, count, dve.tensor_reduce(slotf[:, :, i], pick[:, :, :], AX.X, ALU.add))
            link(dve, count, dve.tensor_copy(slots[:, :, :], slotf[:, :, :]))
            tt(ge[:, :, :], tile_no[:, :, :], u[0:1, :].unsqueeze(1).to_broadcast([1, RT, E8]), ALU.is_ge)
            link(dve, count, dve.tensor_reduce(texp[:, :], ge[:, :, 0:ER], AX.X, ALU.add))
            link(dve, count, dve.tensor_scalar(texp[:, :], texp[:, :], ER - 1.0, None, ALU.min))
            link(dve, count, dve.tensor_copy(tile_expert[:, :], texp[:, :]))


def expert_tiles(nc, stage, tiles, weights, ident=None, xT=None, first=0, h=None, tile_expert=None, x_sorted=None,
                 y_sorted=None, side=None):
    routed = h is None
    WS = 2 if routed else 1
    with ExitStack() as ctx:
        room = Room(nc, ctx, stage)
        wgu = [room.sb(f"wgu{i}", [P, 2, GU], FP16) for i in range(WS)]
        wdn = [room.sb(f"wdn{i}", [P, 2, FC, C], FP16) for i in range(WS)]
        sg = [room.sb(f"sg{i}", [P, 2, TT]) for i in range(2)]
        full = [room.sb(f"full{i}", [P, 2, TT]) for i in range(2)]
        act_p = [room.sb(f"act{i}", [P, 2, FC, TT], FP16) for i in range(2)]
        pg = [room.ps(f"g{i}", [P, 2, TT]) for i in range(2)]
        pu = [room.ps(f"u{i}", [P, 2, TT]) for i in range(2)]
        py = [room.ps(f"y{i}", [P, TK, C]) for i in range(2)]
        if routed:
            xs = [room.sb(f"xs{i}", [P, TK, 2, CK, P], FP16) for i in range(2)]
            xt = [room.sb(f"xt{i}", [P, TK, 2, CK, P], FP16) for i in range(2)]
            pt = [room.ps(f"t{i}", [P, 2, CK, P]) for i in range(2)]
            ysb = [room.sb(f"ysb{i}", [P, TK, C]) for i in range(2)]
            x_in = [room.sem(f"x_in{i}") for i in range(2)]
            turned, xt_done = room.sem("turned"), room.sem("xt_done")
            y_out = [room.sem(f"y_out{i}") for i in range(2)]
        gu_in = [room.sem(f"gu_in{i}") for i in range(WS)]
        dn_in = [room.sem(f"dn_in{i}") for i in range(WS)]
        g_ready = room.sem("g_ready")
        sg_done = room.sem("sg_done")
        a_done = room.sem("a_done")
        hi_done = room.sem("hi_done")
        lo_done = room.sem("lo_done")
        y_ready = room.sem("y_ready")
        y_taken = room.sem("y_taken")
        block = ctx.enter_context(nc.Block())
        PR = FC // 2
        if side:
            side(block)

        @block.sync
        def _(sp):
            def step(s, u, has):
                if has(0):
                    if routed:
                        e = sp.value_load(tile_expert[0:1, bass.ds(s, 1) if not isinstance(s, int) else slice(s, s + 1)],
                                          min_val=0, max_val=ER - 1)
                        wait(sp, turned, (s - 1) * TK if isinstance(s, int) else s * TK - TK)
                        at = s * TT
                        for t in range(TK):
                            sp.dma_start(xs[u][:, t, :, :, :].rearrange("p q k c -> p (q k c)"),
                                         x_sorted[bass.ds(at + t * P, P), :]).then_inc(x_in[u], 16)
                    else:
                        e = ER
                    if routed or (isinstance(s, int) and s == 0):
                        wait(sp, g_ready, (s - 1) * PR)
                        sp.dma_start(wgu[u % WS][:, :, :], weights[bass.ds(e, 1), :, :, 0:GU].rearrange("e p q n -> p (e q) n"))\
                            .then_inc(gu_in[u % WS], 16)
                        wait(sp, y_ready, s - 1)
                        sp.dma_start(wdn[u % WS][:, :, :, :].rearrange("p q f c -> p q (f c)"),
                                     weights[bass.ds(e, 1), :, :, GU:].rearrange("e p q n -> p (e q) n")).then_inc(dn_in[u % WS], 16)
                if routed and has(2):
                    wait(sp, y_taken, s - 1)
                    sp.dma_start(y_sorted[bass.ds((s - 2) * TT, TT), :].rearrange("(t p) c -> p t c", p=P),
                                 ysb[u][:, :, :]).then_inc(y_out[u], 16)
            steps(sp, tiles, 2, step)
            if routed:
                for i in range(2):
                    sp.wait_ge(y_out[i], tiles // 2 * 16)

        @block.tensor
        def _(pe):
            def turn(s, u, n_of):
                pe.wait_ge(x_in[u], n_of * 16 * TK + 16 * TK)
                for t in range(TK):
                    wait(pe, xt_done, s * TK + t - 1)
                    for q in range(2):
                        for k in range(CK):
                            last = pe.matmul(pt[t][:, q, k, :], xs[u][:, t, q, k, :], ident, start=True, stop=True)
                    last.then_inc(turned, 1)

            def step(s, u, has):
                if has(0):
                    if routed:
                        turn(s, u, has.per(0, 2))
                        wait(pe, xt_done, s * TK + TK)
                        pe.wait_ge(gu_in[u], has.per(0, 2) * 16 + 16)
                        moving = lambda m, k: xt[u][:, :, m, k, :]
                    else:
                        if isinstance(s, int) and s == 0:
                            pe.wait_ge(gu_in[0], 16)
                        moving = lambda m, k: xT[m][:, k, bass.ds((s + first) * TT, TT)]
                    w = wgu[u % WS][:, :, :].rearrange("p q (b k f) -> p q b k f", b=2, k=CK)
                    for j in range(PR):
                        wait(pe, a_done, s * PR + j - 1)
                        for b, bank in ((0, pg[j % 2]), (1, pu[j % 2])):
                            for c in range(2):
                                f = slice((2 * j + c) * P, (2 * j + c + 1) * P)
                                last = matmul3(pe, bank[:, c, :], lambda q, k: w[:, q, b, k, f], moving)
                        last.then_inc(g_ready, 1)
                if has(1):
                    v = 1 - u
                    pe.wait_ge(dn_in[v % WS], has.per(1, 2) * 16 + 16 if routed else 16)
                    wait(pe, lo_done, s * PR)
                    wait(pe, y_taken, s - 2)
                    for t in range(TK):
                        last = matmul3(pe, py[v][:, t, :], lambda q, f: act_p[v][:, q, f, t * P:(t + 1) * P],
                                       lambda m, f: wdn[v % WS][:, m, f, :], chunks=FC)
                    last.then_inc(y_ready, 1)
            steps(pe, tiles, 2, step)

        @block.scalar
        def _(act):
            def step(s, u, has):
                if has(0):
                    if routed:
                        for t in range(TK):
                            wait(act, turned, s * TK + t + 1)
                            wait(act, g_ready, (s - 1) * PR) if t == 0 else None
                            act.copy(xt[u][:, t, :, :, :], pt[t][:, :, :, :]).then_inc(xt_done, 1)
                    for j in range(PR):
                        n = s * PR + j
                        wait(act, g_ready, n + 1)
                        wait(act, a_done, n - 1)
                        act.activation(sg[j % 2][:, :, :], pg[j % 2][:, :, :], ACT.Silu, scale=1.0 / WSCALE).then_inc(sg_done, 1)
                        wait(act, a_done, n + 1)
                        if j == 0:
                            wait(act, y_ready, s - 1)
                        act.copy(act_p[u][:, 0, 2 * j:2 * j + 2, :], full[j % 2][:, :, :]).then_inc(hi_done, 1)
                if routed and has(1):
                    v = 1 - u
                    wait(act, y_ready, s)
                    if not isinstance(s, int) or s >= 3:
                        act.wait_ge(y_out[v], has.per(1, 2) * 16)
                    act.activation(ysb[v][:, :, :], py[v][:, :, :], ACT.Copy, scale=1.0 / WSCALE).then_inc(y_taken, 1)
            steps(act, tiles, 2, step)

        @block.vector
        def _(dve):
            def step(s, u, has):
                if has(0):
                    for j in range(PR):
                        n = s * PR + j
                        wait(dve, sg_done, n + 1)
                        wait(dve, lo_done, n - 1)
                        dve.scalar_tensor_tensor(full[j % 2][:, :, :], pu[j % 2][:, :, :], 1.0 / WSCALE, sg[j % 2][:, :, :],
                                                 ALU.mult, ALU.mult).then_inc(a_done, 1)
                        wait(dve, hi_done, n + 1)
                        dve.tensor_tensor(act_p[u][:, 1, 2 * j:2 * j + 2, :], full[j % 2][:, :, :],
                                          act_p[u][:, 0, 2 * j:2 * j + 2, :], ALU.subtract).then_inc(lo_done, 1)
                if not routed and has(1):
                    v = 1 - u
                    rows2 = h[:, bass.ds((s - 1 + first) * TK, TK), :]
                    wait(dve, y_ready, s)
                    dve.scalar_tensor_tensor(rows2, py[v][:, :, :], 1.0 / WSCALE, rows2, ALU.mult, ALU.add).then_inc(y_taken, 1)
            steps(dve, tiles, 2, step)


def moe_stage(nc, a, h, ident, w_dram, room):
    x_sorted = nc.dram_tensor("m_x_sorted", [RT * TT, 2 * C], FP16, kind="Internal").ap()
    y_sorted = nc.dram_tensor("m_y_sorted", [RT * TT, C], FP32, kind="Internal").ap()
    slots = room.sb("slots", [P, NT, 2], I32)
    coef = room.sb("coef", [P, NT, 2])
    tile_expert = room.sb("tile_expert", [1, RT], I32)
    xT = [room.sb(f"xT{i}", [P, CK, NT * P], FP16) for i in range(2)]
    scattered = room.dma_sem("scattered")
    gathered = room.dma_sem("gathered")
    half = NT // TK // 2
    with ExitStack() as ctx:
        x = Room(nc, ctx, "mx").sb("x", [P, NT, 2, C], FP16)
        split_norm_T(nc, "mn", h, ident, *xT, keep=(x[:, :, 0, :], x[:, :, 1, :]))
        route_stage(nc, a, xT, slots, coef, tile_expert, x_sorted)

        def scatter(block):
            @block.gpsimd
            def _(pool):
                for n in range(NT):
                    for i in range(2):
                        pool.indirect_dma_start(x_sorted[:, :], bass.IndirectOffsetOnAxis(ap=slots[:, n, i:i + 1], axis=0),
                                                x[:, n, :, :].rearrange("p q c -> p (q c)"), None).then_inc(scattered, 16)
                pool.wait_ge(scattered, NT * 2 * 16)

        expert_tiles(nc, "ma", half, w_dram, xT=xT, first=0, h=h, side=scatter)
    expert_tiles(nc, "mb", RT, w_dram, ident=ident, tile_expert=tile_expert, x_sorted=x_sorted, y_sorted=y_sorted)
    y = [room.sb(f"y{i}", [P, NT, C]) for i in range(2)]

    def gather(block):
        @block.gpsimd
        def _(pool):
            for n in range(NT):
                for i in range(2):
                    pool.indirect_dma_start(y[i][:, n, :], None, y_sorted[:, :],
                                            bass.IndirectOffsetOnAxis(ap=slots[:, n, i:i + 1], axis=0)).then_inc(gathered, 16)
            pool.wait_ge(gathered, NT * 2 * 16)
            for q in range(4):
                r = slice(q * NT // 4, (q + 1) * NT // 4)
                for i in range(2):
                    pool.tensor_tensor(y[i][:, r, :], y[i][:, r, :], coef[:, r, i:i + 1].to_broadcast([P, NT // 4, C]),
                                       ALU.mult).then_inc(weighted, 1)
                pool.wait_ge(weighted, q * 2 + 2)
                pool.tensor_tensor(y[0][:, r, :], y[0][:, r, :], y[1][:, r, :], ALU.add)

    weighted = room.sem("weighted")
    expert_tiles(nc, "mc", half, w_dram, xT=xT, first=half, h=h, side=gather)
    return y[0]


def program(nc, a, out):
    with ExitStack() as ctx:
        h = ctx.enter_context(nc.sbuf_tensor("h", [P, NT, C], FP32))
        identb = ctx.enter_context(nc.sbuf_tensor("identb", [P, P], BF16))
        identh = ctx.enter_context(nc.sbuf_tensor("identh", [P, P], FP16))
        constants_stage(nc, identb, identh)
        w_dram = nc.dram_tensor("m_w_parts", [E8, P, 2, GU + DN], FP16, kind="Internal").ap()
        embed_stage(nc, a["ids"], a["table"], h)
        attention0_stage(nc, a, h, identb[:, :], split_experts(nc, a["m_w"], w_dram))
        experts0_stage(nc, a, h, identh[:, :])
        attention1_stage(nc, a, h, identh[:, :])
        y = moe_stage(nc, a, h, identh[:, :], w_dram, Room(nc, ctx, "m"))
        write_stage(nc, h, y, out)


def rows(v):
    return v.reshape(-1, P).T


def spread(v):
    return np.broadcast_to(v, (P, v.shape[0]))


def sinusoids(length, width):
    at = np.arange(length, dtype=np.float32)[:, None]
    rate = np.exp(np.arange(0, width, 2, dtype=np.float32) * np.float32(-np.log(10000.0) / width))
    return np.stack([np.sin(at * rate), np.cos(at * rate)], -1).reshape(length, width).astype(np.float32)


def kernel(**inputs):
    import concourse.bacc as bacc
    from concourse.bass_utils import run_bass_kernel_spmd

    f = {k: np.asarray(v) for k, v in inputs.items()}
    wqkv, bqkv = f["L0_attn_Wqkv"], f["L0_attn_bqkv"]
    laid = {
        "ids": f["x"].reshape(NT, P).T,
        "table": f["L0_tok_weight"],
        "a0_wqkv": wqkv.T,
        "a0_qkb": rows(bqkv[:2 * C]),
        "a0_vb": spread(bqkv[2 * C:]),
        "a0_wo": f["L0_attn_Wproj"].T,
        "a0_ob": spread(f["L0_attn_bproj"]),
    }
    pair = np.zeros((P, P), f["L0_ffn_sub_key0"].dtype)
    for b in range(4):
        pair[b * PK:(b + 1) * PK, b * PK:(b + 1) * PK] = f[f"L0_ffn_sub_key{b % 2}"].T
    laid.update({
        "f0_wq": f["L0_ffn_Wq"],
        "f0_down": f["L0_ffn_expert_down"].T,
        "f0_up": f["L0_ffn_expert_up"],
        "f0_bq": rows(f["L0_ffn_bq"]),
        "f0_gnb": np.stack([np.tile(f["L0_ffn_bn_gamma"], 2), np.tile(f["L0_ffn_bn_beta"], 2)], 1),
        "f0_keys": pair,
        "f0_agg": (np.tile(np.eye(P // 2), (2, 2)) / PH).astype(np.float32),
        "f0_ones": np.ones((P, P), np.float32),
        "f0_blocks": np.repeat(np.eye(4), P // 4, 0).astype(np.float32),
    })
    laid.update({f"a1_w{n}": f[f"L1_attn_W{n}"] for n in "qkvpo"})
    laid.update({
        "a1_pe": sinusoids(T, C).T,
        "a1_g": spread(f["L1_attn_ln_g"]),
        "a1_b": spread(f["L1_attn_ln_b"]),
        "a1_qkuv": np.stack([rows(f[f"L1_attn_{n}"].reshape(C)) for n in ("bq", "bk", "u_bias", "v_bias")], 1),
        "a1_bv": spread(f["L1_attn_bv"]),
        "a1_bo": spread(f["L1_attn_bo"]),
    })
    gate, up, down = (np.concatenate([f[f"L1_ffn_routed_{n}"], f[f"L1_ffn_shared_{n}"][None]]) for n in ("gate", "up", "down"))
    laid.update({
        "m_w": np.concatenate([w.transpose(0, 2, 1).reshape(E8, -1, P, w.shape[1]).transpose(0, 2, 1, 3).reshape(E8, P, -1)
                               for w in (gate, up, down)], 2),
        "m_router": np.concatenate([f["L1_ffn_router_w"], np.zeros((1, C), np.float32)]).T,
        "m_before": np.triu(np.ones((P, P), np.float32), 1),
        "m_ones": np.ones((P, P), np.float32),
        "m_lane": spread(np.arange(E8, dtype=np.float32)),
        "m_tile_no": np.repeat(np.arange(RT, dtype=np.float32)[None, :, None], E8, 2),
    })
    nc = bacc.Bacc("TRN2", target_bir_lowering=False, num_devices=1)
    arrays, args = {}, {}
    for name, a in laid.items():
        a = np.ascontiguousarray(a)
        arrays["in_" + name] = a
        args[name] = nc.dram_tensor("in_" + name, a.shape, mybir.dt.from_np(a.dtype), kind="ExternalInput").ap()
    out = nc.dram_tensor("out", (B, T, C), FP32, kind="ExternalOutput").ap()
    program(nc, args, out)
    r = run_bass_kernel_spmd(nc, [arrays], core_ids=[0])
    return r.results[0]["out"]
```

```python
import numpy as np
import concourse.bass as bass
from concourse import mybir
from contextlib import ExitStack

FP32 = mybir.dt.float32
BF16 = mybir.dt.bfloat16
FP16 = mybir.dt.float16
I32 = mybir.dt.int32
ALU = mybir.AluOpType
ACT = mybir.ActivationFunctionType
AX = mybir.AxisListType

P = 128
B, T, C = 16, 256, 256
NT = B * T // P
CK = C // P
V = 50257


class Count:

    def __init__(self, sem, base=0):
        self.sem, self.base, self.n = sem, base, 0

    def then(self, instruction, by=1):
        instruction.then_inc(self.sem, by)
        self.n += by
        return instruction

    def wait(self, engine):
        engine.wait_ge(self.sem, self.base + self.n)


def link(engine, count, instruction):
    count.then(instruction)
    count.wait(engine)


class Room:

    def __init__(self, nc, ctx, stage):
        self.nc, self.ctx, self.stage, self.sems = nc, ctx, stage, []
        ctx.callback(self.close)

    def close(self):
        for sem in self.sems:
            self.nc.gpsimd.sem_clear(sem)
            self.nc.release_semaphore(sem)

    def sb(self, name, shape, dt=FP32):
        return self.ctx.enter_context(self.nc.sbuf_tensor(f"{self.stage}_{name}", shape, dt))

    def ps(self, name, shape, dt=FP32):
        return self.ctx.enter_context(self.nc.psum_tensor(f"{self.stage}_{name}", shape, dt))

    def dma_sem(self, name):
        return self.nc.alloc_semaphore(f"{self.stage}_{name}")

    def sem(self, name):
        self.sems.append(self.nc.alloc_semaphore(f"{self.stage}_{name}"))
        return self.sems[-1]


def embed_stage(nc, ids, table, h):
    WHOLE = V * C // P
    CH = WHOLE // 58
    LOADS = WHOLE // CH
    RING = 6
    with ExitStack() as ctx:
        room = Room(nc, ctx, "emb")
        ring = room.sb("ring", [P, RING, CH])
        idsb = room.sb("ids", [P, NT], I32)
        part = room.sb("part", [P, LOADS])
        top = room.sb("top", [P, 1])
        maxw = room.sb("maxw", [P, 1])
        max2 = room.sb("max2", [P, 1])
        inv = room.sb("inv", [P, 1])
        half_inv = room.sb("half_inv", [P, 1])
        QS = 8

        def part_of(q):
            return slice(q * NT // QS, (q + 1) * NT // QS)

        scales_ready, scaled = room.sem("scales_ready"), room.sem("scaled")
        ids_in = room.sem("ids_in")
        rows_in = room.dma_sem("rows_in")
        slot_in = [room.sem(f"slot_in{r}") for r in range(RING)]
        reduced = room.sem("reduced")
        top_ready = room.sem("top_ready")
        max_ready = room.sem("max_ready")
        dve_done = room.sem("dve_done")
        block = ctx.enter_context(nc.Block())
        flat = table.rearrange("v c -> (v c)").rearrange("(p n) -> p n", p=P)

        @block.sync
        def _(sp):
            sp.dma_start(idsb[:, :], ids).then_inc(ids_in, 16)
            for n in range(LOADS):
                if n >= RING:
                    sp.wait_ge(reduced, n - RING + 1)
                sp.dma_start(ring[:, n % RING, :], flat[:, n * CH:(n + 1) * CH]).then_inc(slot_in[n % RING], 16)

        @block.gpsimd
        def _(pool):
            pool.wait_ge(ids_in, 16)
            for n in range(NT):
                pool.indirect_dma_start(h[:, n, :], None, table[:, :],
                                        bass.IndirectOffsetOnAxis(ap=idsb[:, n:n + 1], axis=0)).then_inc(rows_in, 16)
            pool.wait_ge(top_ready, 1)
            pool.partition_all_reduce(maxw[:, :], top[:, :], P, bass.bass_isa.ReduceOp.max).then_inc(max_ready, 1)

        @block.vector
        def _(dve):
            done = Count(dve_done)
            for n in range(LOADS):
                dve.wait_ge(slot_in[n % RING], 16 * (n // RING + 1))
                dve.tensor_reduce(part[:, n:n + 1], ring[:, n % RING, :], AX.X, ALU.max,
                                  apply_absolute_value=True).then_inc(reduced, 1)
            dve.wait_ge(reduced, LOADS)
            dve.tensor_reduce(top[:, :], part[:, :], AX.X, ALU.max).then_inc(top_ready, 1)
            dve.wait_ge(max_ready, 1)
            dve.wait_ge(rows_in, 16 * NT)
            link(dve, done, dve.tensor_scalar(max2[:, :], maxw[:, :], 2.0, None, ALU.mult))
            link(dve, done, dve.reciprocal(inv[:, :], maxw[:, :]))
            dve.tensor_scalar(half_inv[:, :], inv[:, :], 0.5, None, ALU.mult).then_inc(scales_ready, 1)
            for q in range(QS):
                dve.wait_ge(scaled, q + 1)
                hq = h[:, part_of(q), :]
                link(dve, done, dve.tensor_scalar(hq, hq, 0.5, 0.5, ALU.add, ALU.is_gt))
                dve.tensor_scalar(hq, hq, max2[:, 0:1], maxw[:, 0:1], ALU.mult, ALU.subtract)

        @block.scalar
        def _(act):
            act.wait_ge(scales_ready, 1)
            for q in range(QS):
                hq = h[:, part_of(q), :]
                act.activation(hq, hq, ACT.Copy, scale=half_inv[:, 0:1]).then_inc(scaled, 1)


def write_stage(nc, h, y, out):
    with ExitStack() as ctx:
        room = Room(nc, ctx, "wr")
        added = room.sem("added")
        out_done = room.sem("out_done")
        block = ctx.enter_context(nc.Block())
        quarter = [slice(q * NT // 4, (q + 1) * NT // 4) for q in range(4)]

        @block.vector
        def _(dve):
            for r in quarter:
                dve.tensor_tensor(h[:, r, :], h[:, r, :], y[:, r, :], ALU.add).then_inc(added, 1)

        @block.sync
        def _(sp):
            tiles = out.rearrange("b (t p) c -> p (b t) c", p=P)
            for q, r in enumerate(quarter):
                sp.wait_ge(added, q + 1)
                sp.dma_start(tiles[:, r, :], h[:, r, :]).then_inc(out_done, 16)
            sp.wait_ge(out_done, 64)


MAGIC = 1.5 * 2.0 ** 23
QMAX = 127.0
EPS = 1e-5
H, DH = 16, 16
VW = 2 * DH + 2


def layernorm_stats(dve, count, h, room, sqrt_in, sqrt_out):
    st = room.sb("ln_st", [P, NT, 6])
    mean = room.sb("ln_mean", [P, NT])
    gap = room.sb("ln_gap", [P, NT])
    gap2 = room.sb("ln_gap2", [P, NT])
    var = room.sb("ln_var", [P, NT])
    root = room.sb("ln_root", [P, NT])
    rstd = room.sb("ln_rstd", [P, NT])
    mean_e, mean_o, m2_e, m2_o = st[:, :, 1], st[:, :, 4], st[:, :, 2], st[:, :, 5]

    def on_vector():
        with dve.Fori(0, NT // 8) as i:
            for n in (i * 8 + k for k in range(8)):
                dve.bn_stats(st[:, n, :], h[:, n, :]).then_inc(count.sem, 1)
        count.n += NT
        count.wait(dve)
        link(dve, count, dve.tensor_tensor(gap[:, :], mean_e, mean_o, ALU.subtract))
        link(dve, count, dve.tensor_tensor(mean[:, :], mean_e, mean_o, ALU.add))
        link(dve, count, dve.tensor_tensor(var[:, :], m2_e, m2_o, ALU.add))
        link(dve, count, dve.tensor_tensor(gap2[:, :], gap[:, :], gap[:, :], ALU.mult))
        link(dve, count, dve.tensor_scalar(mean[:, :], mean[:, :], 0.5, None, ALU.mult))
        link(dve, count, dve.tensor_scalar(gap2[:, :], gap2[:, :], 0.25, EPS, ALU.mult, ALU.add))
        dve.scalar_tensor_tensor(var[:, :], var[:, :], 1.0 / C, gap2[:, :], ALU.mult, ALU.add).then_inc(sqrt_in, 1)
        dve.wait_ge(sqrt_out, 1)
        link(dve, count, dve.reciprocal(rstd[:, :], root[:, :]))

    def on_scalar(act):
        act.wait_ge(sqrt_in, 1)
        act.activation(root[:, :], var[:, :], ACT.Sqrt).then_inc(sqrt_out, 1)

    return mean, rstd, on_vector, on_scalar


GRP = 4
G = NT // GRP


def group(n):
    return slice(n * GRP, (n + 1) * GRP)


class Turn:

    def __init__(self, room, parts, ident, slots):
        self.parts, self.ident, self.slots = parts, ident, slots
        self.bank = [[room.ps(f"bank{p}_{i}", [P, CK, GRP * P]) for i in range(slots[p])] for p in range(len(parts))]
        self.turned = [room.sem(f"turned{p}") for p in range(len(parts))]
        self.copied = [room.sem(f"copied{p}") for p in range(len(parts))]

    def turn(self, pe, p, n):
        src, _, ready = self.parts[p]
        wait(pe, self.copied[p], n + 1 - self.slots[p])
        pe.wait_ge(ready, n + 1)
        for ck in range(CK):
            for k in range(GRP):
                last = pe.matmul(self.bank[p][n % self.slots[p]][:, ck, k * P:(k + 1) * P],
                                 src[:, n * GRP + k, ck * P:(ck + 1) * P], self.ident, start=True, stop=True)
        last.then_inc(self.turned[p], 1)

    def copy(self, engine, copy, p, n):
        engine.wait_ge(self.turned[p], n + 1)
        copy(self.parts[p][1][:, :, n * GRP * P:(n + 1) * GRP * P], self.bank[p][n % self.slots[p]][:, :, :])\
            .then_inc(self.copied[p], 1)


class Quantise:

    def __init__(self, room, items, inv_ready, own):
        self.items, self.inv_ready, self.own = items, inv_ready, own
        self.magic = room.sb("magic", [P, 1])
        self.magic_ready = room.sem("magic_ready")
        self.shifted = room.sem("shifted")
        self.own_shifted = room.sem("own_shifted")
        self.clipped = room.sem("clipped")
        self.quantised = room.sem("quantised")

    def constants(self, pool):
        pool.memset(self.magic[:, :], -MAGIC).then_inc(self.magic_ready, 1)

    def shift(self, engine, n):
        if n == 0:
            engine.wait_ge(self.inv_ready, 1)
        x, _, inv = self.items[n]
        engine.tensor_scalar(x, x, inv, MAGIC, ALU.mult, ALU.add).then_inc(self.shifted if n < self.own else self.own_shifted, 1)

    def clip(self, dve, n):
        x = self.items[n][0]
        if n < self.own:
            dve.wait_ge(self.shifted, n + 1)
        else:
            dve.wait_ge(self.own_shifted, n + 1 - self.own)
        dve.tensor_scalar(x, x, MAGIC - QMAX, MAGIC + QMAX, ALU.max, ALU.min).then_inc(self.clipped, 1)

    def finish(self, act, n):
        x, out, _ = self.items[n]
        if n == 0:
            act.wait_ge(self.magic_ready, 1)
        act.wait_ge(self.clipped, n + 1)
        act.activation(out, x, ACT.Identity, bias=self.magic[:, 0:1]).then_inc(self.quantised, 1)


def attention0_stage(nc, a, h, ident, side):
    with ExitStack() as outer:
        oroom = Room(nc, outer, "a0")
        xn = oroom.sb("xn", [P, NT, C])
        xT = oroom.sb("xT", [P, CK, NT * P], BF16)
        qk_w = oroom.sb("qk_w", [P, CK, 2 * C], BF16)
        v_w = oroom.sb("v_w", [P, CK, C], BF16)
        o_w = oroom.sb("o_w", [P, CK, C], BF16)
        qk_bias = oroom.sb("qk_bias", [P, 2 * CK])
        v_bias = oroom.sb("v_bias", [P, C])
        o_bias = oroom.sb("o_bias", [P, C])
        scale = oroom.sb("scale", [P, 8])
        S_X, S_QKV, S_O, S_K, S_AO, S_OUT = range(6)

        def col(i):
            return scale[:, i:i + 1]

        with ExitStack() as ctx:
            room = Room(nc, ctx, "a0q")
            xi = room.sb("xi", [P, NT, C], BF16)
            raw = room.sb("raw", [P, CK, 3 * C])
            raw_o = room.sb("raw_o", [P, CK, C])
            top = room.sb("top", [P, 3])
            maxs = room.sb("maxs", [P, 3])
            inv = room.sb("inv", [P, 3])
            inv_ready = room.sem("inv_ready")
            q = Quantise(room, [(xn[:, group(n), :], xi[:, group(n), :], inv[:, 0:1]) for n in range(G)]
                         + [(raw[:, :, 0:2 * C], qk_w[:, :, :], inv[:, 1:2]), (raw[:, :, 2 * C:], v_w[:, :, :], inv[:, 1:2]),
                            (raw_o[:, :, :], o_w[:, :, :], inv[:, 2:3])], inv_ready, G)
            turn = Turn(room, [(xi, xT, q.quantised)], ident, [2])
            loaded = room.sem("loaded")
            tops = room.sem("tops")
            maxed = room.sem("maxed")
            var_ready = room.sem("var_ready")
            root_ready = room.sem("root_ready")
            dve_done = room.sem("dve_done")
            count = Count(dve_done)
            mean, rstd, ln_vector, ln_scalar = layernorm_stats(nc.vector, count, h, room, var_ready, root_ready)
            with nc.Block() as block:

                @block.sync
                def _(sp):
                    sp.dma_start(raw[:, :, :], a["a0_wqkv"].rearrange("(k p) n -> p k n", p=P)).then_inc(loaded, 16)
                    sp.dma_start(raw_o[:, :, :], a["a0_wo"].rearrange("(k p) n -> p k n", p=P)).then_inc(loaded, 16)
                    sp.dma_start(qk_bias[:, :], a["a0_qkb"]).then_inc(loaded, 16)
                    sp.dma_start(v_bias[:, :], a["a0_vb"]).then_inc(loaded, 16)
                    sp.dma_start(o_bias[:, :], a["a0_ob"]).then_inc(loaded, 16)

                @block.scalar
                def _(act):
                    ln_scalar(act)
                    for n in range(G + 3):
                        q.finish(act, n)

                @block.gpsimd
                def _(pool):
                    q.constants(pool)
                    pool.wait_ge(tops, 1)
                    pool.partition_all_reduce(maxs[:, :], top[:, :], P, bass.bass_isa.ReduceOp.max).then_inc(maxed, 1)
                    for n in range(G):
                        q.shift(pool, n)

                @block.tensor
                def _(pe):
                    for n in range(G):
                        turn.turn(pe, 0, n)

                @block.vector
                def _(dve):
                    ln_vector()
                    with dve.Fori(0, NT // 8) as i:
                        for n in (i * 8 + k for k in range(8)):
                            dve.tensor_scalar(xn[:, n, :], h[:, n, :], mean[:, bass.ds(n, 1)], rstd[:, bass.ds(n, 1)],
                                              ALU.subtract, ALU.mult).then_inc(dve_done, 1)
                    count.n += NT
                    count.wait(dve)
                    dve.wait_ge(loaded, 80)
                    for i, x in enumerate((raw, raw_o)):
                        count.then(dve.tensor_reduce(top[:, i + 1:i + 2], x[:, :, :], AX.XY, ALU.max, apply_absolute_value=True))
                    link(dve, count, dve.tensor_reduce(top[:, 0:1], xn[:, :, :], AX.XY, ALU.max, apply_absolute_value=True))
                    dve.sem_inc(tops, 1)
                    dve.wait_ge(maxed, 1)
                    link(dve, count, dve.tensor_scalar(scale[:, 0:3], maxs[:, :], 1.0 / QMAX, 1e-8, ALU.mult, ALU.max))
                    link(dve, count, dve.reciprocal(inv[:, :], scale[:, 0:3]))
                    dve.tensor_tensor(col(S_K), col(S_X), col(S_QKV), ALU.mult).then_inc(inv_ready, 1)
                    dve.wait_ge(inv_ready, 1)
                    for n in range(G, G + 3):
                        q.shift(dve, n)
                    for n in range(G + 3):
                        q.clip(dve, n)
                        if n >= 3:
                            turn.copy(dve, dve.tensor_copy, 0, n - 3)

        q_dram = nc.dram_tensor("a0_q", [2, C, NT * P], FP16, kind="Internal").ap()
        k_dram = nc.dram_tensor("a0_k", [2, C, NT * P], FP16, kind="Internal").ap()
        with ExitStack() as ctx:
            vs = Room(nc, ctx, "a0m").sb("vs", [P, NT, H, VW], FP16)
            project_stage(nc, "a0j", (xT,), [((qk_w,), 0, col(S_K), qk_bias[:, 0:CK], q_dram),
                                             ((qk_w,), C, col(S_K), qk_bias[:, CK:], k_dram)],
                          ((v_w,), 0), v_bias, col(S_K), vs, matmul1)
            attend_stage(nc, "a0a", q_dram, k_dram, vs, xn, causal=True, side=side)

        with ExitStack() as ctx:
            room = Room(nc, ctx, "a0p")
            oi = room.sb("oi", [P, NT, C], BF16)
            top = room.sb("top", [P, 1])
            maxs = room.sb("maxs", [P, 1])
            inv = room.sb("inv", [P, 1])
            tops, maxed, inv_ready = room.sem("tops"), room.sem("maxed"), room.sem("inv_ready")
            dve_done = room.sem("dve_done")
            biased = room.sem("biased")
            pr = [room.ps(f"pr{i}", [P, 2, C]) for i in range(2)]
            pr_ready = room.sem("pr_ready")
            added = room.sem("added")
            q = Quantise(room, [(xn[:, group(n), :], oi[:, group(n), :], inv[:, 0:1]) for n in range(G)], inv_ready, G)
            turn = Turn(room, [(oi, xT, q.quantised)], ident, [2])
            block = ctx.enter_context(nc.Block())

            @block.gpsimd
            def _(pool):
                q.constants(pool)
                pool.wait_ge(tops, 1)
                pool.partition_all_reduce(maxs[:, :], top[:, :], P, bass.bass_isa.ReduceOp.max).then_inc(maxed, 1)
                for n in range(G):
                    q.shift(pool, n)
                for n in range(G):
                    pool.tensor_tensor(h[:, group(n), :], h[:, group(n), :],
                                       o_bias[:, :].unsqueeze(1).to_broadcast([P, GRP, C]), ALU.add).then_inc(biased, 1)

            @block.scalar
            def _(act):
                for n in range(G + 1):
                    if n < G:
                        q.finish(act, n)
                    if n >= 1:
                        turn.copy(act, act.copy, 0, n - 1)

            @block.tensor
            def _(pe):
                for n in range(G + 1):
                    if n < G:
                        turn.turn(pe, 0, n)
                    if n >= 1:
                        project_group(pe, turn.copied, pr, pr_ready, added, n - 1,
                                      lambda out, t: matmul1(pe, out, lambda p, k: xT[:, k, t * P:(t + 1) * P], lambda p, k: o_w[:, k, :]))

            @block.vector
            def _(dve):
                count = Count(dve_done)
                dve.tensor_reduce(top[:, :], xn[:, :, :], AX.XY, ALU.max, apply_absolute_value=True).then_inc(tops, 1)
                dve.wait_ge(maxed, 1)
                link(dve, count, dve.tensor_scalar(col(S_AO), maxs[:, :], 1.0 / QMAX, 1e-8, ALU.mult, ALU.max))
                link(dve, count, dve.reciprocal(inv[:, :], col(S_AO)))
                link(dve, count, dve.tensor_tensor(col(S_OUT), col(S_AO), col(S_O), ALU.mult))
                dve.sem_inc(inv_ready, 1)
                for n in range(G + 4):
                    if n < G:
                        q.clip(dve, n)
                    if n >= 4:
                        add_group(dve, h, pr, pr_ready, added, biased, n - 4, col(S_OUT))


def project_group(pe, copied, pr, pr_ready, added, n, product):
    for sem in copied:
        pe.wait_ge(sem, n + 1)
    for j in range(GRP // 2):
        pair = n * (GRP // 2) + j
        wait(pe, added, pair - 1)
        for t in range(2):
            last = product(pr[pair % 2][:, t, :], pair * 2 + t)
        last.then_inc(pr_ready, 1)


def add_group(dve, h, pr, pr_ready, added, biased, n, scale):
    dve.wait_ge(biased, n + 1)
    for j in range(GRP // 2):
        pair = n * (GRP // 2) + j
        dve.wait_ge(pr_ready, pair + 1)
        dve.scalar_tensor_tensor(h[:, pair * 2:pair * 2 + 2, :], pr[pair % 2][:, :, :], scale,
                                 h[:, pair * 2:pair * 2 + 2, :], ALU.mult, ALU.add).then_inc(added, 1)


def constants_stage(nc, ident16b, ident16f):
    with ExitStack() as ctx:
        room = Room(nc, ctx, "cst")
        zeroed = room.sem("zeroed")
        block = ctx.enter_context(nc.Block())

        @block.gpsimd
        def _(pool):
            for n, m in enumerate((ident16b, ident16f)):
                pool.memset(m[:, :], 0.0).then_inc(zeroed, 1)
                pool.wait_ge(zeroed, n + 1)
                pool.affine_select(out=m[:, :], in_=m[:, :], compare_op=ALU.not_equal, fill=1.0, base=0,
                                   pattern=[[-1, P]], channel_multiplier=1)


class Steps:

    def __init__(self, total, c, i=None, unroll=1):
        self.total, self.c, self.i, self.unroll = total, c, i, unroll

    def __call__(self, k):
        return self.i is not None or 0 <= self.c - k < self.total

    def per(self, k, m):
        if self.i is None:
            return (self.c - k) // m
        assert self.unroll % m == 0
        return self.i * (self.unroll // m) + (self.c - k) // m


def steps(engine, total, lag, step, unroll=2):
    head = -(-lag // unroll) * unroll
    assert total % unroll == 0 and total > head
    for s in range(head):
        step(s, s % unroll, Steps(total, s))
    with engine.Fori(0, (total - head) // unroll) as i:
        for u in range(unroll):
            step(i * unroll + head + u, u, Steps(total, head + u, i, unroll))
    for s in range(total, total + lag):
        step(s, s % unroll, Steps(total, s))


def wait(engine, sem, value):
    if not isinstance(value, int) or value > 0:
        engine.wait_ge(sem, value)


def held(engine, value):
    return value if isinstance(value, int) else engine.snap(value)


def matmul3(pe, out, stationary, moving, chunks=CK):
    pairs = [(k, s, m) for k in range(chunks) for s, m in ((0, 0), (0, 1), (1, 0))]
    for j, (k, s, m) in enumerate(pairs):
        last = pe.matmul(out, stationary(s, k), moving(m, k), start=j == 0, stop=j == len(pairs) - 1)
    return last


def matmul1(pe, out, stationary, moving, chunks=CK):
    for k in range(chunks):
        last = pe.matmul(out, stationary(0, k), moving(0, k), start=k == 0, stop=k == chunks - 1)
    return last


def project_stage(nc, stage, xT, dims, v_w, v_bias, v_scale, vs, mm):
    TB = 512
    NB = NT * P // TB
    D = len(dims)
    with ExitStack() as ctx:
        room = Room(nc, ctx, stage)
        ps = [room.ps(f"d{i}", [P, TB]) for i in range(4)]
        pv = [room.ps(f"v{i}", [P, 2, C]) for i in range(4)]
        full = [room.sb(f"full{i}", [P, TB]) for i in range(4)]
        part = [room.sb(f"part{i}", [P, 2, TB], FP16) for i in range(4)]
        vfull = [room.sb(f"vfull{i}", [P, 2, C]) for i in range(2)]
        summed = room.sem("summed")
        taken = room.sem("taken")
        split = room.sem("split")
        hi_done = room.sem("hi_done")
        hi_act = room.sem("hi_act")
        stored = [room.sem(f"stored{i}") for i in range(4)]
        v_summed = room.sem("v_summed")
        v_taken = room.sem("v_taken")
        v_hi = room.sem("v_hi")
        v_split = room.sem("v_split")
        block = ctx.enter_context(nc.Block())
        shares = [d > 0 and dims[d][0] is dims[d - 1][0] and dims[d][1] == dims[d - 1][1] for d in range(D)]
        runs = [[d] + [d + 1] * (d + 1 < D and shares[d + 1]) for d in range(D) if not shares[d]]
        jobs = [(d, ck) for run in runs for ck in range(CK) for d in run]
        product = [sum(not shares[d] for d, _ in jobs[:j + 1]) - 1 for j in range(len(jobs))]
        J = len(jobs)
        assert product[-1] == 3
        NI = J * NB
        U = J * 2 if J % 4 else J

        def place(u, has):
            d, ck = jobs[u % J]
            return d, ck, has.per(0, J)

        @block.gpsimd
        def _(pool):
            pool.memset(vs[:, :, :, 2 * DH:], 1.0)

        @block.tensor
        def _(pe):
            def step(s, u, has):
                d, ck, b = place(u, has)
                if has(0) and not shares[d]:
                    w, col = dims[d][0], dims[d][1]
                    p = product[u % J]
                    wait(pe, taken, s - J + product.count(p))
                    mm(pe, ps[p][:, :], lambda q, k: w[q][:, k, col + ck * P:col + (ck + 1) * P],
                       lambda m, k: xT[m][:, k, bass.ds(b * TB, TB)]).then_inc(summed, 1)
            steps(pe, NI, 4, step, U)

            def vstep(s, u, has):
                if has(0):
                    wait(pe, v_taken, s - 3)
                    for t in range(2):
                        last = mm(pe, pv[u][:, t, :], lambda q, k: xT[q][:, k, bass.ds((s * 2 + t) * P, P)],
                                  lambda m, k: v_w[0][m][:, k, v_w[1]:v_w[1] + C])
                    last.then_inc(v_summed, 1)
            steps(pe, NT // 2, 4, vstep, 4)

        @block.scalar
        def _(act):
            def step(s, u, has):
                if has(0):
                    d, ck, b = place(u, has)
                    p = product[u % J]
                    wait(act, split, s - 3)
                    wait(act, summed, b * 4 + p + 1)
                    act.activation(full[u % 4][:, :], ps[p][:, :], ACT.Identity, bias=dims[d][3][:, ck:ck + 1],
                                   scale=dims[d][2]).then_inc(taken, 1)
                    if u % 2 == 0:
                        wait(act, taken, s + 1)
                        if not isinstance(s, int) or s >= 4:
                            act.wait_ge(stored[u % 4], has.per(0, 4) * 16)
                        act.copy(part[u % 4][:, 0, :], full[u % 4][:, :]).then_inc(hi_act, 1)
            steps(act, NI, 4, step, U)

            def vstep(s, u, has):
                if has(0):
                    wait(act, v_taken, s + 1)
                    act.copy(vs[:, bass.ds(s * 2, 2), :, 0:DH],
                             vfull[u % 2][:, :, :].rearrange("p t (h d) -> p t h d", h=H)).then_inc(v_hi, 1)
            steps(act, NT // 2, 4, vstep, 4)

        @block.vector
        def _(dve):
            def step(s, u, has):
                if has(0):
                    wait(dve, taken, s + 1)
                    if not isinstance(s, int) or s >= 4:
                        dve.wait_ge(stored[u % 4], has.per(0, 4) * 16)
                    if u % 2:
                        dve.tensor_copy(part[u % 4][:, 0, :], full[u % 4][:, :]).then_inc(hi_done, 1)
                        dve.wait_ge(hi_done, has.per(0, 2) + 1)
                    else:
                        dve.wait_ge(hi_act, has.per(0, 2) + 1)
                    dve.tensor_tensor(part[u % 4][:, 1, :], full[u % 4][:, :], part[u % 4][:, 0, :], ALU.subtract).then_inc(split, 1)
            steps(dve, NI, 4, step, U)

            def vstep(s, u, has):
                if has(0):
                    wait(dve, v_summed, s + 1)
                    wait(dve, v_split, s - 1)
                    dve.scalar_tensor_tensor(vfull[u % 2][:, :, :], pv[u][:, :, :], v_scale,
                                             v_bias[:, :].unsqueeze(1).to_broadcast([P, 2, C]), ALU.mult, ALU.add).then_inc(v_taken, 1)
                if has(1):
                    v = (u - 1) % 4
                    wait(dve, v_hi, s)
                    rows4 = vs[:, bass.ds((s - 1) * 2, 2), :, :]
                    dve.tensor_tensor(rows4[:, :, :, DH:2 * DH], vfull[v % 2][:, :, :].rearrange("p t (h d) -> p t h d", h=H),
                                      rows4[:, :, :, 0:DH], ALU.subtract).then_inc(v_split, 1)
            steps(dve, NT // 2, 4, vstep, 4)

        @block.sync
        def _(sp):
            def step(s, u, has):
                if has(0):
                    d, ck, b = place(u, has)
                    wait(sp, split, s + 1)
                    sp.dma_start(dims[d][4][:, ck * P:(ck + 1) * P, bass.ds(b * TB, TB)].rearrange("q p n -> p q n"),
                                 part[u % 4][:, :, :]).then_inc(stored[u % 4], 16)
            steps(sp, NI, 4, step, U)
            for i in range(4):
                sp.wait_ge(stored[i], NI // 4 * 16)


def attend_stage(nc, stage, qd, kd, vs, ao, causal, pd=None, qvd=None, posd=None, side=None):
    NH = B * H
    PRE = 6
    LEAD = PRE + (8 if pd is not None else 0)
    HH = H // 2
    U = 2 * H
    tiles = [(0, 0), (1, 0), (1, 1)] if causal else [(0, 0), (0, 1), (1, 0), (1, 1)]
    W = len(tiles) * P
    rows_of = [slice(0, P), slice(P, W)] if causal else [slice(0, T), slice(T, W)]
    R = 4 * DH
    with ExitStack() as ctx:
        room = Room(nc, ctx, stage)
        n_st = 3 if pd is not None else 2
        stacks = [[room.sb(f"stack{i}_{b}", [P, H // 2, T], FP16) for b in range(2)] for i in range(n_st)]
        mask = room.sb("mask", [P, W]) if causal else None
        neg = [room.sb(f"neg{i}", [P, W]) for i in range(4)]
        nmax = [room.sb(f"nmax{i}", [P, 2]) for i in range(4)]
        prob = [room.sb(f"prob{i}", [P, W]) for i in range(2)]
        pT = [room.sb(f"pT{i}", [P, 2, W], FP16) for i in range(4)]
        rsum = [room.sb(f"rsum{i}", [P, 2, H]) for i in range(2)]
        rinv = room.sb("rinv", [P, 2, HH])
        lows = room.sb("lows", [P, 2, HH, DH])
        identf = room.sb("identf", [P, P])
        sc = [room.ps(f"sc{i}", [P, 512]) for i in range(2)]
        tp = [room.ps(f"tp{i}", [P, 512]) for i in range(2)]
        VN = 2 * DH + causal
        obank = [room.ps(f"ob{i}", [P, 2, 512 if causal else HH * VN]) for i in range(2)]
        ob = [o[:, :, 0:HH * VN].rearrange("p t (h n) -> p t h n", n=VN) for o in obank]
        setup, setup2 = room.sem("setup"), room.sem("setup2")
        loaded = [room.sem(f"loaded{b}") for b in range(2)]
        if side:
            side_work = side(room)
        s_ready = room.sem("s_ready")
        masked = room.sem("masked")
        exped = room.sem("exped")
        turned = room.sem("turned")
        hi_done = room.sem("hi_done")
        lo_done = room.sem("lo_done")
        pv_done = room.sem("pv_done")
        norm_done = room.sem("norm_done")
        o_done = room.sem("o_done")
        if pd is not None:
            pos_dram = posd
            pstack = room.sb("pstack", [P, H // 2, T], FP16)
            pps = [room.ps(f"pps{i}", [P, 512]) for i in range(2)]
            raw = [room.sb(f"raw{i}", [P, 2, T + 1]) for i in range(2)]
            pos = [room.sb(f"pos{i}", [P, W]) for i in range(4)]
            p_loaded = room.sem("p_loaded")
            g_loaded = [room.dma_sem(f"g_loaded{b}") for b in range(2)]
            zeroed = room.sem("zeroed")
            p_ready = room.sem("p_ready")
            p_taken = [room.sem(f"p_taken{i}") for i in range(2)]
            p_out = [room.sem(f"p_out{i}") for i in range(2)]
            p_in = [room.sem(f"p_in{i}") for i in range(4)]
        block = ctx.enter_context(nc.Block())
        LAG = LEAD + 6

        def stack_load(engine, operand, dst, tok, k, n):
            par, slot = k // 4, k % 4
            src, q = ((qd, slot % 2), (kd, slot // 2), (qvd, slot % 2), (pd, slot // 2))[operand]
            v = src[q, :, tok].rearrange("(j two d) n -> two d j n", two=2, d=DH)[par]
            engine.dma_start(dst[par * R + slot * DH:par * R + (slot + 1) * DH, :, :], v).then_inc(n, 16)

        def batch_loads(engine, s, u, has, operands, sems, spread):
            if has(0) and u % H == 0 and (not isinstance(s, int) or s >= 2 * H):
                engine.wait_ge(s_ready, s - H)
            loads = [(o, k) for o in operands for k in range(8)]
            if spread:
                loads = loads[u % H:u % H + 1]
            elif u % H:
                loads = []
            if has(0) and loads:
                at = held(engine, has.per(0, H) * T)
                for o, k in loads:
                    stack_load(engine, o, stacks[o][u // H % 2], bass.ds(at, T), k, sems[u // H % 2])

        @block.sync
        def _(sp):
            if pd is not None:
                for k in range(8):
                    stack_load(sp, 3, pstack, slice(0, T), k, p_loaded)

            def step(s, u, has):
                batch_loads(sp, s, u, has, [1] if pd is not None else [0, 1], loaded, spread=pd is not None)
                if pd is not None:
                    if has(PRE + 1):
                        v = (u - PRE - 1) % U
                        wait(sp, p_taken[v % 2], has.per(PRE + 1, 2) + 1)
                        sp.dma_start(pos_dram[v, 0:T * (T + 1)].rearrange("(t p c) -> p t c", p=P, t=2),
                                     raw[v % 2][:, :, :]).then_inc(p_out[v % 2], 16)
                    if has(PRE + 4):
                        v = (u - PRE - 4) % U
                        n = s - PRE - 4
                        landed = held(sp, has.per(PRE + 4, 2) * 16 + 16)
                        wait(sp, masked, n - 3)
                        sp.wait_ge(p_out[v % 2], landed)
                        sp.dma_start(pos[v % 4][:, :].rearrange("p (t c) -> p t c", t=2),
                                     pos_dram[v, T:T * (T + 1)].rearrange("(t p c) -> p t c", p=P, t=2)).then_inc(p_in[v % 4], 16)
            steps(sp, NH, LAG, step, U)

        @block.gpsimd
        def _(pool):
            pool.memset(identf[:, :], 0.0).then_inc(setup, 1)
            if causal:
                pool.memset(mask[:, :], 0.0).then_inc(setup, 1)
            pool.wait_ge(setup, 1 + causal)
            pool.affine_select(out=identf[:, :], in_=identf[:, :], compare_op=ALU.not_equal, fill=1.0, base=0,
                               pattern=[[-1, P]], channel_multiplier=1).then_inc(setup2, 1)
            if causal:
                for k0 in (0, 2 * P):
                    pool.affine_select(out=mask[:, k0:k0 + P], in_=mask[:, k0:k0 + P], compare_op=ALU.is_ge,
                                       fill=-1e30, base=0, pattern=[[-1, P]], channel_multiplier=1).then_inc(setup2, 1)
            else:
                for r in raw:
                    pool.memset(r[:, :, 0:1], 0.0).then_inc(zeroed, 1)
                steps(pool, NH, LAG, lambda s, u, has: batch_loads(pool, s, u, has, [2, 0], g_loaded, spread=False), U)
            if side:
                side_work(pool)

        def item(u, k):
            v = (u - k) % U
            hd = v % H
            return v, hd // 2, slice(hd % 2 * R, hd % 2 * R + R)

        @block.tensor
        def _(pe):
            pe.wait_ge(setup2, 3 if causal else 1)
            if pd is not None:
                pe.wait_ge(p_loaded, 128)

            def step(s, u, has):
                if pd is not None and has(PRE):
                    v, j, rr = item(u, PRE)
                    if v % H == 0:
                        pe.wait_ge(g_loaded[v // H], (has.per(PRE, U) + 1) * 256)
                    wait(pe, p_taken[v % 2], has.per(PRE, 2))
                    for t in range(2):
                        last = pe.matmul(pps[v % 2][:, t * T:(t + 1) * T], stacks[2][v // H][rr, j, t * P:(t + 1) * P],
                                         pstack[rr, j, :], start=True, stop=True)
                    last.then_inc(p_ready, 1)
                if has(LEAD):
                    v, j, rr = item(u, LEAD)
                    n = s - LEAD
                    if v % H == 0:
                        pe.wait_ge(loaded[v // H], (has.per(LEAD, U) + 1) * (128 if pd is not None else 256))
                    wait(pe, masked, n - 1)
                    for t in range(2):
                        keys_ = slice(0, (t + 1) * P) if causal else slice(0, T)
                        last = pe.matmul(sc[v % 2][:, rows_of[t]], stacks[0][v // H][rr, j, t * P:(t + 1) * P],
                                         stacks[1][v // H][rr, j, keys_], start=True, stop=True)
                    last.then_inc(s_ready, 1)
                if has(LEAD + 3):
                    v, _, _ = item(u, LEAD + 3)
                    n = s - LEAD - 3
                    wait(pe, exped, n + 1)
                    wait(pe, lo_done, n - 1)
                    for k in range(len(tiles)):
                        last = pe.transpose(tp[v % 2][:, k * P:(k + 1) * P], prob[v % 2][:, k * P:(k + 1) * P], identf[:, :])
                    last.then_inc(turned, 1)
                if has(LEAD + 5):
                    v, _, _ = item(u, LEAD + 5)
                    n = s - LEAD - 5
                    if v % HH == 0:
                        wait(pe, norm_done, (has.per(LEAD + 5, HH) - 1) * 2)
                    wait(pe, lo_done, n + 1)
                    b2 = has.per(LEAD + 5, H)
                    for t in range(2):
                        mine = [(x, kt) for x, (qt, kt) in enumerate(tiles) if qt == t]
                        for x, kt in mine:
                            for part in range(2):
                                last = pe.matmul(ob[v // HH % 2][:, t, v % HH, :], pT[v % 4][:, part, x * P:(x + 1) * P],
                                                 vs[:, bass.ds(b2 * 2 + kt, 1), v % H, 0:VN].rearrange("p o n -> p (o n)"),
                                                 start=(x, kt) == mine[0] and part == 0, stop=(x, kt) == mine[-1] and part == 1)
                    last.then_inc(pv_done, 1)
            steps(pe, NH, LAG, step, U)

        def take_pos(eng, copy, s, v, has):
            n = s - PRE
            wait(eng, p_ready, n + 1)
            if not isinstance(n, int) or n >= 2:
                eng.wait_ge(p_out[v % 2], has.per(PRE, 2) * 16)
            if isinstance(n, int) and n < 2:
                eng.wait_ge(zeroed, 2)
            copy(raw[v % 2][:, :, 1:], pps[v % 2][:, :].rearrange("p (t c) -> p t c", t=2)).then_inc(p_taken[v % 2], 1)

        @block.scalar
        def _(act):
            def step(s, u, has):
                if has(LEAD + 2):
                    v, _, _ = item(u, LEAD + 2)
                    n = s - LEAD - 2
                    wait(act, masked, n + 1)
                    wait(act, turned, n - 1)
                    if v % H == 0 and not causal:
                        wait(act, o_done, (has.per(LEAD + 2, H) - 1) * 2)
                    for t in range(2):
                        last = act.activation(prob[v % 2][:, rows_of[t]], neg[v % 4][:, rows_of[t]], ACT.Exp,
                                              bias=nmax[v % 4][:, t:t + 1], scale=-1.0,
                                              accum_out=None if causal else rsum[v // H][:, t, v % H:v % H + 1])
                    last.then_inc(exped, 1)
                if has(LEAD + 3):
                    v, _, _ = item(u, LEAD + 3)
                    n = s - LEAD - 3
                    wait(act, turned, n + 1)
                    wait(act, pv_done, n - 3)
                    act.copy(pT[v % 4][:, 0, :], tp[v % 2][:, 0:W]).then_inc(hi_done, 1)
                if pd is not None and has(PRE) and u % 2 == 0:
                    v, _, _ = item(u, PRE)
                    take_pos(act, act.copy, s, v, has)
            steps(act, NH, LAG, step, U)

        @block.vector
        def _(dve):
            dve.wait_ge(setup2, 3 if causal else 1)

            def step(s, u, has):
                if has(LEAD):
                    v, n = item(u, LEAD)[0], s - LEAD
                    wait(dve, s_ready, n + 1)
                    wait(dve, exped, n - 3)
                    if pd is not None:
                        dve.wait_ge(p_in[v % 4], has.per(LEAD, 4) * 16 + 16)
                if has(LEAD + 4):
                    v, _, _ = item(u, LEAD + 4)
                    n = s - LEAD - 4
                    wait(dve, hi_done, n + 1)
                    dve.tensor_tensor(pT[v % 4][:, 1, :], tp[v % 2][:, 0:W], pT[v % 4][:, 0, :], ALU.subtract).then_inc(lo_done, 1)
                if has(LEAD):
                    v = item(u, LEAD)[0]
                    other = mask if causal else pos[v % 4]
                    for t in range(2):
                        last = dve.tensor_tensor_reduce(out=neg[v % 4][:, rows_of[t]], in0=sc[v % 2][:, rows_of[t]],
                                                        in1=other[:, rows_of[t]], scale=-DH ** -0.5, scalar=1e38,
                                                        op0=ALU.add, op1=ALU.min, accum_out=nmax[v % 4][:, t:t + 1])
                    last.then_inc(masked, 1)
                if pd is not None and has(PRE) and u % 2 == 1:
                    take_pos(dve, dve.tensor_copy, s, item(u, PRE)[0], has)
                if has(LEAD + 6) and (u - LEAD - 6) % HH == HH - 1:
                    v = (u - LEAD - 6) % U
                    n = s - LEAD - 6
                    half = v // HH % 2
                    b, hb = has.per(LEAD + 6, H), has.per(LEAD + 6, HH)
                    bank = ob[half]
                    wait(dve, pv_done, n + 1)
                    wait(dve, exped, n + 1)
                    dve.reciprocal(rinv[:, :, :], bank[:, :, :, 2 * DH] if causal else rsum[v // H][:, :, half * HH:(half + 1) * HH])
                    dve.tensor_copy(lows[:, :, :, :], bank[:, :, :, DH:2 * DH]).then_inc(norm_done, 1)
                    dve.wait_ge(norm_done, hb * 2 + 1)
                    dve.tensor_tensor(lows[:, :, :, :], lows[:, :, :, :], bank[:, :, :, 0:DH], ALU.add).then_inc(norm_done, 1)
                    dve.wait_ge(norm_done, hb * 2 + 2)
                    dve.tensor_tensor(ao[:, bass.ds(b * 2, 2), half * HH * DH:(half + 1) * HH * DH].rearrange("p t (h d) -> p t h d", h=HH),
                                      lows[:, :, :, :], rinv[:, :, :].unsqueeze(3).to_broadcast([P, 2, HH, DH]),
                                      ALU.mult).then_inc(o_done, 1)
            steps(dve, NH, LAG, step, U)


WSCALE = 64.0


def split_norm_T(nc, stage, h, ident, xhT, xlT, affine=None, gain=None, shift=None, keep=None, router=None):
    with ExitStack() as outer:
        oroom = Room(nc, outer, stage)
        if keep:
            xh, xl = keep
        else:
            xh = oroom.sb("xh", [P, NT, C], FP16)
            xl = oroom.sb("xl", [P, NT, C], FP16)
        with ExitStack() as ctx:
            room = Room(nc, ctx, stage + "n")
            xn = room.sb("xn", [P, NT, C])
            gb = room.sb("gb", [P, 2, C])
            dve_done = room.sem("dve_done")
            var_ready = room.sem("var_ready")
            root_ready = room.sem("root_ready")
            var_ready2 = room.sem("var_ready2")
            root_ready2 = room.sem("root_ready2")
            loaded = room.sem("loaded")
            x_ready = room.sem("x_ready")
            xh_ready = room.sem("xh_ready")
            xl_ready = room.sem("xl_ready")
            count = Count(dve_done)
            mean, rstd, ln_vector, ln_scalar = layernorm_stats(nc.vector, count, h, room, var_ready, root_ready)
            if affine:
                room.stage += "b"
                mean2, rstd2, ln_vector2, ln_scalar2 = layernorm_stats(nc.vector, count, xn, room, var_ready2, root_ready2)
            turn = Turn(room, [(xh, xhT, xh_ready), (xl, xlT, xl_ready)], ident, [2, 1 if router else 2])
            block = ctx.enter_context(nc.Block())

            @block.sync
            def _(sp):
                if router:
                    router.load(sp)
                if affine:
                    sp.dma_start(gb[:, 0, :], gain).then_inc(loaded, 16)
                    sp.dma_start(gb[:, 1, :], shift).then_inc(loaded, 16)

            @block.scalar
            def _(act):
                if router:
                    router.split_hi(act)
                ln_scalar(act)
                if affine:
                    ln_scalar2(act)
                for n in range(G + 2):
                    if n < G:
                        act.wait_ge(x_ready, n + 1)
                        act.copy(xh[:, group(n), :], xn[:, group(n), :]).then_inc(xh_ready, 1)
                    if 0 <= n - 1 < G:
                        turn.copy(act, act.copy, 0, n - 1)
                    if affine and n >= 2:
                        turn.copy(act, act.copy, 1, n - 2)

            @block.gpsimd
            def _(pool):
                for n in range(G):
                    pool.wait_ge(xh_ready, n + 1)
                    pool.tensor_tensor(xl[:, group(n), :], xn[:, group(n), :], xh[:, group(n), :], ALU.subtract).then_inc(xl_ready, 1)

            @block.tensor
            def _(pe):
                for n in range(G + 3):
                    if n < G:
                        turn.turn(pe, 0, n)
                    if 0 <= n - 1 < G:
                        turn.turn(pe, 1, n - 1)
                    if router and n >= 3:
                        router.logits(pe, (xhT, xlT), turn.copied, n - 3)

            @block.vector
            def _(dve):
                if router:
                    router.split_lo(dve)
                ln_vector()
                src, m, r = h, mean, rstd
                if affine:
                    with dve.Fori(0, NT // 8) as i:
                        for n in (i * 8 + k for k in range(8)):
                            dve.tensor_scalar(xn[:, n, :], h[:, n, :], mean[:, bass.ds(n, 1)], rstd[:, bass.ds(n, 1)],
                                              ALU.subtract, ALU.mult).then_inc(dve_done, 1)
                    count.n += NT
                    count.wait(dve)
                    ln_vector2()
                    dve.wait_ge(loaded, 32)
                    src, m, r = xn, mean2, rstd2
                for n in range(G + 3):
                    if n < G:
                        for t in range(n * GRP, (n + 1) * GRP):
                            last = dve.tensor_scalar(xn[:, t, :], src[:, t, :], m[:, t:t + 1], r[:, t:t + 1], ALU.subtract, ALU.mult)
                        if affine:
                            shape = [P, GRP, C]
                            link(dve, count, last)
                            link(dve, count, dve.tensor_tensor(xn[:, group(n), :], xn[:, group(n), :],
                                                               gb[:, 0, :].unsqueeze(1).to_broadcast(shape), ALU.mult))
                            last = dve.tensor_tensor(xn[:, group(n), :], xn[:, group(n), :],
                                                     gb[:, 1, :].unsqueeze(1).to_broadcast(shape), ALU.add)
                        last.then_inc(x_ready, 1)
                    if not affine and 0 <= n - 2 < G:
                        turn.copy(dve, dve.tensor_copy, 1, n - 2)


def split_weights(nc, stage, items):
    with ExitStack() as ctx:
        room = Room(nc, ctx, stage)
        raws = [room.sb(f"raw{i}", [P, hi.shape[1], hi.shape[2]]) for i, (_, hi, _) in enumerate(items)]
        loaded = [room.sem(f"loaded{i}") for i in range(len(items))]
        hi_ready = room.sem("hi_ready")
        block = ctx.enter_context(nc.Block())

        @block.sync
        def _(sp):
            for i, (src, hi, _) in enumerate(items):
                sp.dma_start(raws[i][:, :, :], src.rearrange("(k p) n -> p k n", p=P)).then_inc(loaded[i], 16)

        @block.scalar
        def _(act):
            for i, (_, hi, _) in enumerate(items):
                act.wait_ge(loaded[i], 16)
                act.activation(hi[:, :, :], raws[i][:, :, :], ACT.Copy, scale=WSCALE).then_inc(hi_ready, 1)

        @block.vector
        def _(dve):
            for i, (_, hi, lo) in enumerate(items):
                dve.wait_ge(loaded[i], 16)
                dve.wait_ge(hi_ready, i + 1)
                dve.scalar_tensor_tensor(lo[:, :, :], raws[i][:, :, :], WSCALE, hi[:, :, :], ALU.mult, ALU.subtract)


PH, PK, TOP = 8, 32, 4
PG = 4
SEG = 2 * PH
PE_TOP = 8


def experts0_stage(nc, a, h, ident, to_zero):
    with ExitStack() as outer:
        oroom = Room(nc, outer, "f0")
        NE = PE_TOP * PK
        xhT = oroom.sb("xhT", [P, CK, NT * P], FP16)
        xlT = oroom.sb("xlT", [P, CK, NT * P], FP16)
        split_norm_T(nc, "f0x", h, ident, xhT, xlT)
        xT = (xhT, xlT)
        up = [oroom.sb(f"up{i}", [P, CK, C], FP16) for i in range(2)]
        qT = oroom.sb("qT", [P, PG, NT * P])
        gel = oroom.sb("gel", [P, NT, NE])
        keys = oroom.sb("keys", [P, P])
        qa = oroom.sb("qa", [P, 2])
        blocks = oroom.sb("blocks", [P, SEG // PG])
        early = outer.enter_context(ExitStack())
        eroom = Room(nc, early, "f0e")
        wq = [eroom.sb(f"wq{i}", [P, CK, PG * P], FP16) for i in range(2)]
        down = [eroom.sb(f"down{i}", [P, CK, NE], FP16) for i in range(2)]
        split_weights(nc, "f0w", [(a["f0_wq"], *wq), (a["f0_down"], *down), (a["f0_up"], *up)])

        TB = 512
        NB = NT * P // TB
        with ExitStack() as ctx:
            room = Room(nc, ctx, "f0q")
            bq = room.sb("bq", [P, PG])
            zero = room.sb("zero", [P, 2 * C], FP16)
            zeroed, z_stored = room.sem("zeroed"), room.sem("z_stored")
            ps = [room.ps(f"q{i}", [P, TB]) for i in range(4)]
            pg = [room.ps(f"g{i}", [P, 2, NE]) for i in range(2)]
            st = room.sb("st", [P, PG * NB, 6])
            mv = room.sb("mv", [P, PG, 2])
            agg = room.sb("agg", [P, P])
            gnb = room.sb("gnb", [P, 2])
            gm = room.sb("gm", [P, 8])
            key2 = room.sb("key2", [P, P])
            ones = room.sb("ones", [P, P])
            loaded = room.sem("loaded")
            q_in_psum = room.sem("q_in_psum")
            q_done = room.sem("q_done")
            e_in_psum = room.sem("e_in_psum")
            e_done = room.sem("e_done")
            m_ready = room.sem("m_ready")
            m_summed = room.sem("m_summed")
            v_ready = room.sem("v_ready")
            roots = room.sem("roots")
            dve_done = room.sem("dve_done")
            psm = ps[0][:, 0:PG]
            psv = ps[1][:, 0:PG]
            psk = ps[2][:, 0:P]
            block = ctx.enter_context(nc.Block())

            @block.sync
            def _(sp):
                for dst, name in ((bq, "f0_bq"), (gnb, "f0_gnb"), (keys, "f0_keys"), (agg, "f0_agg"), (ones, "f0_ones"),
                                  (blocks, "f0_blocks")):
                    sp.dma_start(dst[:, :], a[name]).then_inc(loaded, 16)
                sp.wait_ge(zeroed, 1)
                rows = to_zero.rearrange("(t p) c -> p t c", p=P)
                sp.dma_start(rows, zero[:, :].unsqueeze(1).to_broadcast([P, rows.shape[1], 2 * C])).then_inc(z_stored, 16)
                sp.wait_ge(z_stored, 16)

            @block.gpsimd
            def _(pool):
                pool.memset(zero[:, :], 0.0).then_inc(zeroed, 1)

            @block.tensor
            def _(pe):
                with pe.Fori(0, NB) as b:
                    for g in range(PG):
                        pe.wait_ge(q_done, b * PG + g + 1)
                        matmul3(pe, ps[g][:, :], lambda s, k: wq[s][:, k, g * P:(g + 1) * P],
                                lambda m, k: xT[m][:, k, bass.ds(b * TB, TB)]).then_inc(q_in_psum, 1)
                with pe.Fori(0, NT // 8) as i:
                    for u in range(4):
                        pe.wait_ge(e_done, i * 4 + u + 1)
                        for t in range(2):
                            last = matmul3(pe, pg[u % 2][:, t, :], lambda s, k: xT[s][:, k, bass.ds((i * 8 + u * 2 + t) * P, P)],
                                           lambda m, k: down[m][:, k, :])
                        last.then_inc(e_in_psum, 1)
                pe.wait_ge(loaded, 96)
                pe.wait_ge(m_ready, 1)
                pe.matmul(psm, agg[:, :], mv[:, :, 0], start=True, stop=True).then_inc(m_summed, 1)
                pe.wait_ge(m_ready, 2)
                pe.matmul(psv, agg[:, :], mv[:, :, 1], start=True, stop=True).then_inc(m_summed, 1)
                pe.matmul(psk, ones[:, :], key2[:, :], start=True, stop=True).then_inc(m_summed, 1)

            @block.scalar
            def _(act):
                act.sem_inc(q_done, PG)
                act.sem_inc(e_done, 2)
                act.wait_ge(loaded, 96)
                with act.Fori(0, NB) as b:
                    for g in range(PG):
                        act.wait_ge(q_in_psum, b * PG + g + 1)
                        act.activation(qT[:, g, bass.ds(b * TB, TB)], ps[g][:, :], ACT.Identity, bias=bq[:, g:g + 1],
                                       scale=1.0 / WSCALE).then_inc(q_done, 1)
                with act.Fori(0, NT // 8) as i:
                    for u in range(4):
                        act.wait_ge(e_in_psum, i * 4 + u + 1)
                        act.activation(gel[:, bass.ds(i * 8 + u * 2, 2), :], pg[u % 2][:, :, :], ACT.Gelu,
                                       scale=1.0 / WSCALE).then_inc(e_done, 1)
                act.wait_ge(v_ready, 1)
                act.activation(gm[:, 3:4], gm[:, 2:3], ACT.Sqrt)
                act.activation(key2[:, :], psk, ACT.Sqrt).then_inc(roots, 1)

            @block.vector
            def _(dve):
                count = Count(dve_done)
                with dve.Fori(0, NB) as b:
                    for g in range(PG):
                        dve.wait_ge(q_done, b * PG + g + PG + 1)
                        dve.bn_stats(st[:, bass.ds(b + g * NB, 1), :], qT[:, g, bass.ds(b * TB, TB)]).then_inc(dve_done, 1)
                count.n += NB * PG
                count.wait(dve)
                for g in range(PG):
                    link(dve, count, dve.bn_aggr(mv[:, g, :], st[:, g * NB:(g + 1) * NB, :].rearrange("p n s -> p (n s)")))
                dve.sem_inc(m_ready, 1)
                dve.wait_ge(m_summed, 1)
                link(dve, count, dve.tensor_reduce(gm[:, 0:1], psm, AX.X, ALU.add))
                link(dve, count, dve.tensor_scalar(mv[:, :, 0], mv[:, :, 0], gm[:, 0:1], None, ALU.subtract))
                link(dve, count, dve.tensor_tensor(mv[:, :, 0], mv[:, :, 0], mv[:, :, 0], ALU.mult))
                link(dve, count, dve.tensor_tensor(mv[:, :, 1], mv[:, :, 0], mv[:, :, 1], ALU.add))
                dve.wait_ge(loaded, 96)
                link(dve, count, dve.tensor_tensor(key2[:, :], keys[:, :], keys[:, :], ALU.mult))
                dve.sem_inc(m_ready, 1)
                dve.wait_ge(m_summed, 3)
                link(dve, count, dve.tensor_reduce(gm[:, 1:2], psv, AX.X, ALU.add))
                dve.tensor_scalar(gm[:, 2:3], gm[:, 1:2], EPS, None, ALU.add).then_inc(v_ready, 1)
                dve.wait_ge(roots, 1)
                link(dve, count, dve.reciprocal(gm[:, 4:5], gm[:, 3:4]))
                link(dve, count, dve.tensor_tensor(qa[:, 0:1], gm[:, 4:5], gnb[:, 0:1], ALU.mult))
                link(dve, count, dve.tensor_tensor(gm[:, 5:6], gm[:, 0:1], qa[:, 0:1], ALU.mult))
                link(dve, count, dve.tensor_tensor(qa[:, 1:2], gnb[:, 1:2], gm[:, 5:6], ALU.subtract))
                link(dve, count, dve.tensor_scalar(key2[:, :], key2[:, :], 1e-12, None, ALU.max))
                link(dve, count, dve.reciprocal(key2[:, :], key2[:, :]))
                link(dve, count, dve.tensor_tensor(keys[:, :], keys[:, :], key2[:, :], ALU.mult))

        early.close()

        with ExitStack() as ctx:
            room = Room(nc, ctx, "f0s")
            PAD = PK + TOP
            SENT, GONE = 9.0, -9.0
            qn = [room.sb(f"qn{i}", [P, PG, P]) for i in range(2)]
            s36 = [room.sb(f"s36_{i}", [P, SEG, PAD]) for i in range(2)]
            left = [room.sb(f"left{i}", [P, SEG, PAD]) for i in range(2)]
            top8 = [room.sb(f"top8_{i}", [P, SEG, 8]) for i in range(2)]
            gap = [room.sb(f"gap{i}", [P, SEG, PK]) for i in range(2)]
            ex = gap
            wt = [room.sb(f"wt{i}", [P, SEG, PK]) for i in range(2)]
            total = [room.sb(f"total{i}", [P, SEG]) for i in range(2)]
            tail = [room.sb(f"tail{i}", [P, 1]) for i in range(2)]
            prod = room.sb("prod", [P, PH, PE_TOP, PK])
            coef = [room.sb(f"coef{i}", [P, NE]) for i in range(2)]
            ch = [room.sb(f"ch{i}", [P, NE], FP16) for i in range(2)]
            cl = [room.sb(f"cl{i}", [P, NE], FP16) for i in range(2)]
            chT = [room.sb(f"chT{i}", [P, 2, CK, P], FP16) for i in range(2)]
            sq = [room.sb(f"sq{i}", [P, PG, P]) for i in range(2)]
            norm = [room.sb(f"norm{i}", [P, SEG]) for i in range(2)]
            halves = [room.sb(f"halves{i}", [P, 2, PE_TOP, PK]) for i in range(2)]
            ps_n = [room.ps(f"n{i}", [P, SEG]) for i in range(2)]
            ps_s = [room.ps(f"s{i}", [P, PG * P]) for i in range(2)]
            ps_t = [room.ps(f"t{i}", [P, 2, CK, P]) for i in range(2)]
            ps_o = [room.ps(f"o{i}", [P, C]) for i in range(2)]
            qn_ready, s_ready, s_taken = room.sem("qn_ready"), room.sem("s_ready"), room.sem("s_taken")
            gap_ready, ex_ready, coef_ready = room.sem("gap_ready"), room.sem("ex_ready"), room.sem("coef_ready")
            t_ready, cT_ready, o_ready, o_taken = room.sem("t_ready"), room.sem("cT_ready"), room.sem("o_ready"), room.sem("o_taken")
            sq_ready, n_ready, rooted = room.sem("sq_ready"), room.sem("n_ready"), room.sem("rooted")
            wt_ready, halves_ready = room.sem("wt_ready"), room.sem("halves_ready")
            cf_ready, ch_ready, pool_done = room.sem("cf_ready"), room.sem("ch_ready"), room.sem("pool_done")
            sent_ready = room.sem("sent_ready")
            dve_done = room.sem("dve_done")
            block = ctx.enter_context(nc.Block())

            LAG = 8

            @block.scalar
            def _(act):
                def step(s, u, has):
                    if has(1):
                        wait(act, s_ready, s - 2)
                    if has(0):
                        wait(act, n_ready, s - 1)
                        act.activation(sq[u][:, :, :], qT[:, :, bass.ds(s * P, P)], ACT.Square, bias=qa[:, 1:2],
                                       scale=qa[:, 0:1]).then_inc(sq_ready, 1)
                    if has(1):
                        v = 1 - u
                        act.activation(qn[v][:, :, :], qT[:, :, bass.ds((s - 1) * P, P)], ACT.Identity, bias=qa[:, 1:2],
                                       scale=qa[:, 0:1]).then_inc(qn_ready, 1)
                    if has(3):
                        v = 1 - u
                        wait(act, gap_ready, s - 2)
                        act.activation(ex[v][:, :, :], gap[v][:, :, :], ACT.Exp).then_inc(ex_ready, 1)
                    if has(7):
                        v = 1 - u
                        wait(act, t_ready, s - 6)
                        act.copy(chT[v][:, :, :, :], ps_t[v][:, :, :, :]).then_inc(cT_ready, 1)
                    if has(5):
                        v = 1 - u
                        wait(act, cf_ready, s - 4)
                        wait(act, t_ready, s - 6)
                        act.copy(ch[v][:, :], coef[v][:, :]).then_inc(ch_ready, 1)
                    if has(1):
                        v = 1 - u
                        wait(act, n_ready, s)
                        wait(act, s_taken, s - 2)
                        act.activation(norm[v][:, :], ps_n[v][:, :], ACT.Sqrt).then_inc(rooted, 1)
                steps(act, NT, LAG, step)

            @block.tensor
            def _(pe):
                def step(s, u, has):
                    if has(0):
                        wait(pe, sq_ready, s + 1)
                        wait(pe, rooted, s - 1)
                        for g in range(PG):
                            last = pe.matmul(ps_n[u][:, g * 4:(g + 1) * 4], sq[u][:, g, :], blocks[:, :], start=True, stop=True)
                        last.then_inc(n_ready, 1)
                    if has(1):
                        v = 1 - u
                        wait(pe, qn_ready, s)
                        wait(pe, s_taken, s - 2)
                        for g in range(PG):
                            last = pe.matmul(ps_s[v][:, g * P:(g + 1) * P], qn[v][:, g, :], keys[:, :], start=True, stop=True)
                        last.then_inc(s_ready, 1)
                    if has(6):
                        wait(pe, coef_ready, s - 5)
                        wait(pe, cT_ready, s - 7)
                        for part, c in enumerate((ch[u], cl[u])):
                            for k in range(CK):
                                last = pe.matmul(ps_t[u][:, part, k, :], c[:, k * P:(k + 1) * P], ident, start=True, stop=True)
                        last.then_inc(t_ready, 1)
                    if has(7):
                        v = 1 - u
                        wait(pe, cT_ready, s - 6)
                        wait(pe, o_taken, s - 8)
                        matmul3(pe, ps_o[v][:, :], lambda p, k: chT[v][:, p, k, :], lambda m, k: up[m][:, k, :]).then_inc(o_ready, 1)
                steps(pe, NT, LAG, step)

            @block.gpsimd
            def _(pool):
                PCH = 2

                def step(s, u, has):
                    if has(0):
                        count = Count(pool_done, s * PCH)
                        w4 = wt[u][:, :, :].rearrange("p (h two) k -> p h two k", two=2)
                        w0, w1 = w4[:, :, 0, 0:PE_TOP], w4[:, :, 1, :]
                        shape = [P, PH, PE_TOP, PK]
                        wait(pool, halves_ready, s)
                        wait(pool, wt_ready, s + 1)
                        link(pool, count, pool.tensor_tensor(prod[:, :, :, :], w0.unsqueeze(3).to_broadcast(shape),
                                                             w1.unsqueeze(2).to_broadcast(shape), ALU.mult))
                    if has(2):
                        wait(pool, ch_ready, s - 1)
                        pool.tensor_tensor(cl[u][:, :], coef[u][:, :], ch[u][:, :], ALU.subtract).then_inc(coef_ready, 1)
                    if has(0):
                        link(pool, count, pool.tensor_tensor(prod[:, 0:4, :, :], prod[:, 0:4, :, :], prod[:, 4:8, :, :], ALU.add))
                        wait(pool, cf_ready, s - 1)
                        pool.tensor_tensor(halves[u][:, :, :, :], prod[:, 0:2, :, :], prod[:, 2:4, :, :], ALU.add)\
                            .then_inc(halves_ready, 1)
                steps(pool, NT, 2, lambda s, u, has: step(s, u % 2, has), 4)

            @block.vector
            def _(dve):
                KCH = 11

                def skipped(count, n):
                    dve.sem_inc(dve_done, n)
                    count.n += n

                def step(s, u, has):
                    count = Count(dve_done, s * KCH)
                    if has(5):
                        v = 1 - u
                        cf = coef[v][:, :]
                        wait(dve, coef_ready, s - 6)
                        wait(dve, halves_ready, s - 4)
                        link(dve, count, dve.tensor_tensor(cf, halves[v][:, 0, :, :].rearrange("p a b -> p (a b)"),
                                                           halves[v][:, 1, :, :].rearrange("p a b -> p (a b)"), ALU.add))
                        link(dve, count, dve.tensor_scalar(coef[v][:, NE - 1:], coef[v][:, NE - 1:], tail[v][:, 0:1], None, ALU.add))
                        dve.tensor_tensor(cf, cf, gel[:, bass.ds(s - 5, 1), :].rearrange("p o e -> p (o e)"), ALU.mult)\
                            .then_inc(cf_ready, 1)
                    else:
                        skipped(count, 2)
                    if has(2):
                        wait(dve, rooted, s - 1)
                        link(dve, count, dve.tensor_scalar(norm[u][:, :], norm[u][:, :], 1e-12, None, ALU.max))
                        link(dve, count, dve.reciprocal(norm[u][:, :], norm[u][:, :]))
                        wait(dve, s_ready, s - 1)
                        dve.tensor_tensor(s36[u][:, :, 0:PK], ps_s[u][:, :].rearrange("p (s k) -> p s k", k=PK),
                                          norm[u][:, :].unsqueeze(2).to_broadcast([P, SEG, PK]), ALU.mult).then_inc(s_taken, 1)
                        dve.wait_ge(sent_ready, 2)
                        dve.wait_ge(s_taken, s - 1)
                        for j in range(SEG):
                            last = dve.max(top8[u][:, j, :], s36[u][:, j, 0:PK])
                        link(dve, count, last)
                        link(dve, count, dve.memset(top8[u][:, :, TOP:], SENT))
                        dve.tensor_tensor(gap[u][:, :, :], s36[u][:, :, 0:PK], top8[u][:, :, 0:1].to_broadcast([P, SEG, PK]),
                                          ALU.subtract).then_inc(gap_ready, 1)
                        for j in range(SEG):
                            last = dve.match_replace(left[u][:, j, :], top8[u][:, j, :], s36[u][:, j, :], GONE)
                        link(dve, count, last)
                    else:
                        skipped(count, 5)
                    if has(3):
                        v = 1 - u
                        wait(dve, ex_ready, s - 2)
                        keep = left[v][:, :, 0:PK]
                        link(dve, count, dve.scalar_tensor_tensor(ex[v][:, :, :], keep, GONE, ex[v][:, :, :], ALU.is_equal, ALU.mult))
                        link(dve, count, dve.tensor_reduce(total[v][:, :], ex[v][:, :, :], AX.X, ALU.add))
                        link(dve, count, dve.reciprocal(total[v][:, :], total[v][:, :]))
                        wait(dve, halves_ready, s - 4)
                        link(dve, count, dve.tensor_tensor(wt[v][:, :, :], ex[v][:, :, :],
                                                           total[v][:, :].unsqueeze(2).to_broadcast([P, SEG, PK]), ALU.mult))
                        w0 = wt[v][:, :, :].rearrange("p (h two) k -> p h two k", two=2)[:, :, 0, PE_TOP:]
                        dve.tensor_reduce(tail[v][:, :], w0, AX.XY, ALU.add).then_inc(wt_ready, 1)
                    else:
                        skipped(count, 4)
                    if has(8):
                        row = h[:, bass.ds(s - 8, 1), :].rearrange("p o c -> p (o c)")
                        wait(dve, o_ready, s - 7)
                        dve.scalar_tensor_tensor(row, ps_o[u][:, :], 1.0 / WSCALE, row, ALU.mult, ALU.add).then_inc(o_taken, 1)
                    assert count.n == KCH

                for i in range(2):
                    dve.memset(s36[i][:, :, PK:], SENT).then_inc(sent_ready, 1)
                steps(dve, NT, LAG, step)


def attention1_stage(nc, a, h, ident):
    with ExitStack() as outer:
        oroom = Room(nc, outer, "a1")
        ao = oroom.sb("ao", [P, NT, C])
        wo = [oroom.sb(f"wo{i}", [P, CK, C], FP16) for i in range(2)]
        dram = {n: nc.dram_tensor(f"a1_{n}", [2, C, t], FP16, kind="Internal").ap()
                for n, t in (("q", NT * P), ("qv", NT * P), ("k", NT * P), ("p", T))}
        pos = nc.dram_tensor("a1_pos", [2 * H, T * (T + 1)], FP32, kind="Internal").ap()
        with ExitStack() as mid:
            vs = Room(nc, mid, "a1m").sb("vs", [P, NT, H, VW], FP16)
            with ExitStack() as ctx:
                room = Room(nc, ctx, "a1x")
                xT = [room.sb(f"xT{i}", [P, CK, NT * P], FP16) for i in range(2)]
                split_norm_T(nc, "a1n", h, ident, *xT, affine=True, gain=a["a1_g"], shift=a["a1_b"])
                w = {n: [room.sb(f"w{n}{i}", [P, CK, C], FP16) for i in range(2)] for n in ("q", "k", "v", "p")}
                pe_parts = [room.sb(f"pe{i}", [P, CK, T], FP16) for i in range(2)]
                split_weights(nc, "a1w", [(a[f"a1_w{n}"], *w[n]) for n in ("q", "k", "v", "p")]
                              + [(a["a1_wo"], *wo), (a["a1_pe"], *pe_parts)])
                bias = room.sb("bias", [P, 5, CK])
                v_bias = room.sb("v_bias", [P, C])
                full = room.sb("full", [P, CK, T])
                part = room.sb("part", [P, 2, CK, T], FP16)
                loaded, summed, taken, hi_done, split, stored, biased = (
                    room.sem(n) for n in ("loaded", "summed", "taken", "hi_done", "split", "stored", "biased"))
                with ExitStack() as pctx:
                    ps = Room(nc, pctx, "a1p").ps("p", [P, CK, T])
                    block = pctx.enter_context(nc.Block())

                    @block.sync
                    def _(sp):
                        sp.dma_start(bias[:, 0:4, :], a["a1_qkuv"]).then_inc(loaded, 16)
                        sp.dma_start(v_bias[:, :], a["a1_bv"]).then_inc(loaded, 16)
                        sp.wait_ge(split, 1)
                        for ck in range(CK):
                            sp.dma_start(dram["p"][:, ck * P:(ck + 1) * P, :].rearrange("q p n -> p q n"),
                                         part[:, :, ck, :]).then_inc(stored, 16)
                        sp.wait_ge(stored, 16 * CK)

                    @block.tensor
                    def _(pe):
                        for ck in range(CK):
                            last = matmul3(pe, ps[:, ck, :], lambda q, k: w["p"][q][:, k, ck * P:(ck + 1) * P],
                                           lambda m, k: pe_parts[m][:, k, :])
                        last.then_inc(summed, 1)

                    @block.scalar
                    def _(act):
                        act.wait_ge(summed, 1)
                        act.activation(full[:, :, :], ps[:, :, :], ACT.Copy, scale=WSCALE ** -2).then_inc(taken, 1)

                    @block.vector
                    def _(dve):
                        dve.wait_ge(loaded, 32)
                        dve.tensor_tensor(bias[:, 2, :], bias[:, 2, :], bias[:, 0, :], ALU.add)
                        dve.tensor_tensor(bias[:, 3, :], bias[:, 3, :], bias[:, 0, :], ALU.add)
                        dve.wait_ge(taken, 1)
                        dve.tensor_copy(part[:, 0, :, :], full[:, :, :]).then_inc(hi_done, 1)
                        dve.wait_ge(hi_done, 1)
                        dve.tensor_tensor(part[:, 1, :, :], full[:, :, :], part[:, 0, :, :], ALU.subtract).then_inc(split, 1)

                s = 1.0 / WSCALE
                project_stage(nc, "a1j", xT, [(w["q"], 0, s, bias[:, 2, :], dram["q"]),
                                              (w["q"], 0, s, bias[:, 3, :], dram["qv"]),
                                              (w["k"], 0, s, bias[:, 1, :], dram["k"])],
                              (w["v"], 0), v_bias, s, vs, matmul3)
            attend_stage(nc, "a1a", dram["q"], dram["k"], vs, ao, causal=False, pd=dram["p"], qvd=dram["qv"], posd=pos)

        with ExitStack() as ctx:
            room = Room(nc, ctx, "a1o")
            x = [room.sb(f"x{i}", [P, NT, C], FP16) for i in range(2)]
            xT = [room.sb(f"xT{i}", [P, CK, NT * P], FP16) for i in range(2)]
            o_bias = room.sb("o_bias", [P, C])
            hi_done, lo_done = room.sem("hi_done"), room.sem("lo_done")
            loaded = room.sem("loaded")
            biased = room.sem("biased")
            pr = [room.ps(f"pr{i}", [P, 2, C]) for i in range(2)]
            pr_ready, added = room.sem("pr_ready"), room.sem("added")
            turn = Turn(room, [(x[0], xT[0], hi_done), (x[1], xT[1], lo_done)], ident, [2, 1])
            block = ctx.enter_context(nc.Block())

            @block.sync
            def _(sp):
                sp.dma_start(o_bias[:, :], a["a1_bo"]).then_inc(loaded, 16)

            @block.gpsimd
            def _(pool):
                pool.wait_ge(loaded, 16)
                for n in range(G):
                    pool.tensor_tensor(h[:, group(n), :], h[:, group(n), :],
                                       o_bias[:, :].unsqueeze(1).to_broadcast([P, GRP, C]), ALU.add).then_inc(biased, 1)

            @block.scalar
            def _(act):
                for n in range(G + 1):
                    if n < G:
                        act.copy(x[0][:, group(n), :], ao[:, group(n), :]).then_inc(hi_done, 1)
                    if n >= 1:
                        turn.copy(act, act.copy, 0, n - 1)
                        turn.copy(act, act.copy, 1, n - 1)

            @block.tensor
            def _(pe):
                for n in range(G + 2):
                    if n < G:
                        turn.turn(pe, 0, n)
                        turn.turn(pe, 1, n)
                    if n >= 2:
                        project_group(pe, turn.copied, pr, pr_ready, added, n - 2,
                                      lambda out, t: matmul3(pe, out, lambda q, k: xT[q][:, k, t * P:(t + 1) * P],
                                                             lambda m, k: wo[m][:, k, :]))

            @block.vector
            def _(dve):
                for n in range(G + 3):
                    if n < G:
                        dve.wait_ge(hi_done, n + 1)
                        dve.tensor_tensor(x[1][:, group(n), :], ao[:, group(n), :], x[0][:, group(n), :],
                                          ALU.subtract).then_inc(lo_done, 1)
                    if n >= 3:
                        add_group(dve, h, pr, pr_ready, added, biased, n - 3, 1.0 / WSCALE)


ER = 7
E8 = 8
F = 1024
FC = F // P
TT = 256
TK = TT // P
PAIRS = 2 * NT * P
RT = (PAIRS + ER * (TT - 1)) // TT
GU, DN = 2 * CK * F, FC * C


def split_experts(nc, src, dst):
    CUTS = 3
    CUT = (GU + DN) // CUTS
    ITEMS = E8 * CUTS

    def side(room):
        raw = [room.sb(f"raw{i}", [P, CUT]) for i in range(2)]
        part = [room.sb(f"part{i}", [P, 2, CUT], FP16) for i in range(2)]
        w_loaded = [room.dma_sem(f"w_loaded{i}") for i in range(2)]
        w_stored = [room.dma_sem(f"w_stored{i}") for i in range(2)]
        w_scaled, w_split = room.sem("w_scaled"), room.sem("w_split")
        factor = room.sb("factor", [P, 1])

        def work(pool):
            pool.memset(factor[:, :], WSCALE).then_inc(w_scaled, 1)
            pool.wait_ge(w_scaled, 1)

            def step(s, u, has):
                if has(0):
                    wait(pool, w_split, s - 1)
                    cut = slice(u % CUTS * CUT, (u % CUTS + 1) * CUT)
                    pool.dma_start(raw[u % 2][:, :], src[bass.ds(has.per(0, CUTS), 1), :, cut]
                                   .rearrange("e p n -> p (e n)")).then_inc(w_loaded[u % 2], 16)
                if has(1):
                    v = (u - 1) % (2 * CUTS)
                    cut = slice(v % CUTS * CUT, (v % CUTS + 1) * CUT)
                    pool.wait_ge(w_loaded[v % 2], has.per(1, 2) * 16 + 16)
                    if not isinstance(s, int) or s >= 3:
                        pool.wait_ge(w_stored[v % 2], has.per(1, 2) * 16)
                    by = factor[:, 0:1].to_broadcast([P, CUT])
                    pool.tensor_tensor(part[v % 2][:, 0, :], raw[v % 2][:, :], by, ALU.mult).then_inc(w_scaled, 1)
                    pool.tensor_tensor(raw[v % 2][:, :], raw[v % 2][:, :], by, ALU.mult).then_inc(w_scaled, 1)
                    pool.wait_ge(w_scaled, s * 2 + 1)
                    pool.tensor_tensor(part[v % 2][:, 1, :], raw[v % 2][:, :], part[v % 2][:, 0, :],
                                       ALU.subtract).then_inc(w_split, 1)
                    pool.wait_ge(w_split, s)
                    pool.dma_start(dst[bass.ds(has.per(1, CUTS), 1), :, :, cut].rearrange("e p q n -> p (e q) n"),
                                   part[v % 2][:, :, :]).then_inc(w_stored[v % 2], 16)
            steps(pool, ITEMS, 1, step, 2 * CUTS)
            for i in range(2):
                pool.wait_ge(w_stored[i], ITEMS // 2 * 16)

        return work

    return side


class Router:

    def __init__(self, room, weights):
        self.weights = weights
        self.wr = [room.sb(f"wr{i}", [P, CK, E8], FP16) for i in range(2)]
        self.raw = room.sb("wr_raw", [P, CK, E8])
        self.ps = room.ps("logits", [P, NT, E8])
        self.loaded, self.hi_done, self.w_split = room.sem("r_loaded"), room.sem("r_hi_done"), room.sem("r_split")

    def load(self, sp):
        sp.dma_start(self.raw[:, :, :], self.weights.rearrange("(k p) e -> p k e", p=P)).then_inc(self.loaded, 16)

    def split_hi(self, act):
        act.wait_ge(self.loaded, 16)
        act.activation(self.wr[0][:, :, :], self.raw[:, :, :], ACT.Copy, scale=WSCALE).then_inc(self.hi_done, 1)

    def split_lo(self, dve):
        dve.wait_ge(self.hi_done, 1)
        dve.scalar_tensor_tensor(self.wr[1][:, :, :], self.raw[:, :, :], WSCALE, self.wr[0][:, :, :],
                                 ALU.mult, ALU.subtract).then_inc(self.w_split, 1)

    def logits(self, pe, xT, copied, n):
        if n == 0:
            pe.wait_ge(self.w_split, 1)
        for sem in copied:
            pe.wait_ge(sem, n + 1)
        for t in range(n * GRP, (n + 1) * GRP):
            matmul3(pe, self.ps[:, t, :], lambda q, k: xT[q][:, k, t * P:(t + 1) * P], lambda m, k: self.wr[m][:, k, :])


def route_stage(nc, a, logits, slots, coef, tile_expert, shared, wgu, wdn):
    with ExitStack() as ctx:
        room = Room(nc, ctx, "rt")
        before = room.sb("before", [P, P])
        ones = room.sb("ones", [P, P])
        lane = room.sb("lane", [P, E8])
        tile_no = room.sb("tile_no", [1, RT, E8])
        big = lambda n, dt=FP32: room.sb(n, [P, NT, E8], dt)
        logit, prob, top, hot1, hot2, hot, scan0, scan1, rank, pick = (
            big(n) for n in ("logit", "prob", "top", "hot1", "hot2", "hot", "scan0", "scan1", "rank", "pick"))
        index = big("index", mybir.dt.uint32)
        indexf = big("indexf")
        small = room.sb("small", [P, 4, NT])
        slotf = room.sb("slotf", [P, NT, 2])
        per_e = room.sb("per_e", [P, 6, E8])
        ge = room.sb("ge", [1, RT, E8])
        texp = room.sb("texp", [1, RT])
        pp = room.ps("p", [P, 2, NT, E8])
        w_loaded = room.sem("w_loaded")
        loaded, gap_ready, e_ready, hot_ready, p_ready, dve_done = (
            room.sem(n) for n in ("loaded", "gap_ready", "e_ready", "hot_ready", "p_ready", "dve_done"))
        block = ctx.enter_context(nc.Block())

        @block.sync
        def _(sp):
            for dst, name in ((before, "m_before"), (ones, "m_ones"), (lane, "m_lane")):
                sp.dma_start(dst[:, :], a[name]).then_inc(loaded, 16)
            sp.dma_start(tile_no[:, :, :], a["m_tile_no"]).then_inc(loaded, 16)
            sp.dma_start(wgu[:, :, :], shared[:, :, 0:GU]).then_inc(w_loaded, 16)
            sp.dma_start(wdn[:, :, :, :].rearrange("p q f c -> p q (f c)"), shared[:, :, GU:]).then_inc(w_loaded, 16)
            sp.wait_ge(w_loaded, 32)

        @block.tensor
        def _(pe):
            pe.wait_ge(loaded, 64)
            pe.wait_ge(hot_ready, 1)
            pe.matmul(pp[:, 0, :, :], before[:, :], hot[:, :, :], start=True, stop=True)
            pe.matmul(pp[:, 1, :, :], ones[:, :], hot[:, :, :], start=True, stop=True).then_inc(p_ready, 1)

        @block.scalar
        def _(act):
            act.wait_ge(gap_ready, 1)
            act.activation(prob[:, :, :], prob[:, :, :], ACT.Exp).then_inc(e_ready, 1)

        @block.vector
        def _(dve):
            count = Count(dve_done)
            wide = [P, NT, E8]

            def tt(out, x, y, op):
                link(dve, count, dve.tensor_tensor(out, x, y, op))

            dve.wait_ge(loaded, 64)
            link(dve, count, dve.tensor_scalar(logit[:, :, :], logits[:, :, :], 1.0 / WSCALE, None, ALU.mult))
            link(dve, count, dve.memset(logit[:, :, ER:], -1e30))
            link(dve, count, dve.tensor_reduce(small[:, 0, :], logit[:, :, :], AX.X, ALU.max))
            dve.tensor_tensor(prob[:, :, :], logit[:, :, :], small[:, 0, :].unsqueeze(2).to_broadcast(wide), ALU.subtract).then_inc(gap_ready, 1)
            dve.wait_ge(e_ready, 1)
            link(dve, count, dve.tensor_reduce(small[:, 1, :], prob[:, :, :], AX.X, ALU.add))
            link(dve, count, dve.reciprocal(small[:, 1, :], small[:, 1, :]))
            tt(prob[:, :, :], prob[:, :, :], small[:, 1, :].unsqueeze(2).to_broadcast(wide), ALU.mult)
            for n in range(NT):
                last = dve.max(top[:, n, :], prob[:, n, :])
            link(dve, count, last)
            for n in range(NT):
                last = dve.max_index(index[:, n, :], top[:, n, :], prob[:, n, :])
            link(dve, count, last)
            link(dve, count, dve.tensor_copy(indexf[:, :, :], index[:, :, :]))
            lanes = lane[:, :].unsqueeze(1).to_broadcast(wide)
            dve.tensor_tensor(hot1[:, :, :], indexf[:, :, 0:1].to_broadcast(wide), lanes, ALU.is_equal)
            tt(hot2[:, :, :], indexf[:, :, 1:2].to_broadcast(wide), lanes, ALU.is_equal)
            dve.tensor_tensor(hot[:, :, :], hot1[:, :, :], hot2[:, :, :], ALU.add).then_inc(hot_ready, 1)
            tt(small[:, 2, :], top[:, :, 0], top[:, :, 1], ALU.add)
            link(dve, count, dve.tensor_scalar(small[:, 2, :], small[:, 2, :], 1e-9, None, ALU.add))
            link(dve, count, dve.reciprocal(small[:, 2, :], small[:, 2, :]))
            tt(coef[:, :, :], top[:, :, 0:2], small[:, 2, :].unsqueeze(2).to_broadcast([P, NT, 2]), ALU.mult)
            dve.wait_ge(p_ready, 1)
            link(dve, count, dve.tensor_copy(scan0[:, :, :], pp[:, 1, :, :]))
            x, y, d = scan0, scan1, 1
            while d < NT:
                dve.tensor_copy(y[:, 0:d, :], x[:, 0:d, :])
                tt(y[:, d:, :], x[:, d:, :], x[:, 0:NT - d, :], ALU.add)
                x, y, d = y, x, 2 * d
            need, end, end2, first = (per_e[:, i, :] for i in range(4))
            link(dve, count, dve.tensor_scalar(need, x[:, NT - 1, :], TT - 1.0, 1.0 / TT, ALU.add, ALU.mult))
            link(dve, count, dve.tensor_scalar(need, need, -(0.5 - 0.5 / TT), MAGIC, ALU.add, ALU.add))
            link(dve, count, dve.tensor_scalar(need, need, MAGIC, None, ALU.subtract))
            link(dve, count, dve.tensor_copy(end, need))
            u, w, d = end, end2, 1
            while d < E8:
                dve.tensor_copy(w[:, 0:d], u[:, 0:d])
                tt(w[:, d:], u[:, d:], u[:, 0:E8 - d], ALU.add)
                u, w, d = w, u, 2 * d
            tt(first, u, need, ALU.subtract)
            link(dve, count, dve.tensor_scalar(first, first, float(TT), None, ALU.mult))
            tt(y[:, :, :], x[:, :, :], pp[:, 1, :, :], ALU.subtract)
            tt(rank[:, :, :], y[:, :, :], pp[:, 0, :, :], ALU.add)
            tt(rank[:, :, :], rank[:, :, :], first.unsqueeze(1).to_broadcast(wide), ALU.add)
            for i, hot_i in enumerate((hot1, hot2)):
                tt(pick[:, :, :], rank[:, :, :], hot_i[:, :, :], ALU.mult)
                link(dve, count, dve.tensor_reduce(slotf[:, :, i], pick[:, :, :], AX.X, ALU.add))
            link(dve, count, dve.tensor_copy(slots[:, :, :], slotf[:, :, :]))
            tt(ge[:, :, :], tile_no[:, :, :], u[0:1, :].unsqueeze(1).to_broadcast([1, RT, E8]), ALU.is_ge)
            link(dve, count, dve.tensor_reduce(texp[:, :], ge[:, :, 0:ER], AX.X, ALU.add))
            link(dve, count, dve.tensor_scalar(texp[:, :], texp[:, :], ER - 1.0, None, ALU.min))
            link(dve, count, dve.tensor_copy(tile_expert[:, :], texp[:, :]))


def expert_tiles(nc, stage, tiles, weights, ident=None, xT=None, first=0, h=None, tile_expert=None, x_sorted=None,
                 y_sorted=None, side=None):
    routed = h is None
    WS = 2 if routed else 1
    with ExitStack() as ctx:
        room = Room(nc, ctx, stage)
        if routed:
            wgu = [room.sb(f"wgu{i}", [P, 2, GU], FP16) for i in range(WS)]
            wdn = [room.sb(f"wdn{i}", [P, 2, FC, C], FP16) for i in range(WS)]
        else:
            wgu, wdn = [weights[0]], [weights[1]]
        sg = [room.sb(f"sg{i}", [P, 2, TT]) for i in range(2)]
        full = [room.sb(f"full{i}", [P, 2, TT]) for i in range(2)]
        act_p = [room.sb(f"act{i}", [P, 2, FC, TT], FP16) for i in range(2)]
        pg = [room.ps(f"g{i}", [P, 2, TT]) for i in range(2)]
        pu = [room.ps(f"u{i}", [P, 2, TT]) for i in range(2)]
        py = [room.ps(f"y{i}", [P, TK, C]) for i in range(2)]
        if routed:
            xs = [room.sb(f"xs{i}", [P, TK, 2, CK, P], FP16) for i in range(2)]
            xt = [room.sb(f"xt{i}", [P, TK, 2, CK, P], FP16) for i in range(2)]
            pt = [room.ps(f"t{i}", [P, 2, CK, P]) for i in range(2)]
            ysb = [room.sb(f"ysb{i}", [P, TK, C]) for i in range(2)]
            x_in = [room.sem(f"x_in{i}") for i in range(2)]
            turned, xt_done = room.sem("turned"), room.sem("xt_done")
            y_out = [room.sem(f"y_out{i}") for i in range(2)]
        gu_in = [room.sem(f"gu_in{i}") for i in range(WS)]
        dn_in = [room.sem(f"dn_in{i}") for i in range(WS)]
        g_ready = room.sem("g_ready")
        sg_done = room.sem("sg_done")
        a_done = room.sem("a_done")
        hi_done = room.sem("hi_done")
        lo_done = room.sem("lo_done")
        y_ready = room.sem("y_ready")
        y_taken = room.sem("y_taken")
        block = ctx.enter_context(nc.Block())
        PR = FC // 2
        if side:
            side(block)

        @block.sync
        def _(sp):
            def step(s, u, has):
                if has(0) and routed:
                    e = sp.value_load(tile_expert[0:1, bass.ds(s, 1) if not isinstance(s, int) else slice(s, s + 1)],
                                          min_val=0, max_val=ER - 1)
                    wait(sp, turned, (s - 1) * TK if isinstance(s, int) else s * TK - TK)
                    at = s * TT
                    for t in range(TK):
                        sp.dma_start(xs[u][:, t, :, :, :].rearrange("p q k c -> p (q k c)"),
                                     x_sorted[bass.ds(at + t * P, P), :]).then_inc(x_in[u], 16)
                    wait(sp, g_ready, (s - 1) * PR)
                    sp.dma_start(wgu[u % WS][:, :, :], weights[bass.ds(e, 1), :, :, 0:GU].rearrange("e p q n -> p (e q) n"))\
                        .then_inc(gu_in[u % WS], 16)
                    wait(sp, y_ready, s - 1)
                    sp.dma_start(wdn[u % WS][:, :, :, :].rearrange("p q f c -> p q (f c)"),
                                 weights[bass.ds(e, 1), :, :, GU:].rearrange("e p q n -> p (e q) n")).then_inc(dn_in[u % WS], 16)
                if routed and has(3):
                    v = 1 - u
                    wait(sp, y_taken, s - 2)
                    sp.dma_start(y_sorted[bass.ds((s - 3) * TT, TT), :].rearrange("(t p) c -> p t c", p=P),
                                 ysb[v][:, :, :]).then_inc(y_out[v], 16)
            steps(sp, tiles, 3, step)
            if routed:
                for i in range(2):
                    sp.wait_ge(y_out[i], tiles // 2 * 16)

        @block.tensor
        def _(pe):
            def turn(s, u, n_of):
                pe.wait_ge(x_in[u], n_of * 16 * TK + 16 * TK)
                for t in range(TK):
                    wait(pe, xt_done, s * TK + t - 1)
                    for q in range(2):
                        for k in range(CK):
                            last = pe.matmul(pt[t][:, q, k, :], xs[u][:, t, q, k, :], ident, start=True, stop=True)
                    last.then_inc(turned, 1)

            def step(s, u, has):
                if has(1):
                    v, n = 1 - u, s - 1
                    if routed:
                        wait(pe, xt_done, n * TK + TK)
                        pe.wait_ge(gu_in[v], has.per(1, 2) * 16 + 16)
                        moving = lambda m, k: xt[v][:, :, m, k, :]
                    else:
                        moving = lambda m, k: xT[m][:, k, bass.ds((n + first) * TT, TT)]
                    w = wgu[v % WS][:, :, :].rearrange("p q (b k f) -> p q b k f", b=2, k=CK)
                    for j in range(PR):
                        wait(pe, a_done, n * PR + j - 1)
                        for b, bank in ((0, pg[j % 2]), (1, pu[j % 2])):
                            for c in range(2):
                                f = slice((2 * j + c) * P, (2 * j + c + 1) * P)
                                last = matmul3(pe, bank[:, c, :], lambda q, k: w[:, q, b, k, f], moving)
                        last.then_inc(g_ready, 1)
                if routed and has(0):
                    turn(s, u, has.per(0, 2))
                if has(2):
                    if routed:
                        pe.wait_ge(dn_in[u], has.per(2, 2) * 16 + 16)
                    wait(pe, lo_done, (s - 1) * PR)
                    wait(pe, y_taken, s - 3)
                    for t in range(TK):
                        last = matmul3(pe, py[u][:, t, :], lambda q, f: act_p[u][:, q, f, t * P:(t + 1) * P],
                                       lambda m, f: wdn[u % WS][:, m, f, :], chunks=FC)
                    last.then_inc(y_ready, 1)
            steps(pe, tiles, 3, step)

        @block.scalar
        def _(act):
            def step(s, u, has):
                if has(1):
                    v = 1 - u
                    for j in range(PR):
                        n = (s - 1) * PR + j
                        wait(act, g_ready, n + 1)
                        wait(act, a_done, n - 1)
                        act.activation(sg[j % 2][:, :, :], pg[j % 2][:, :, :], ACT.Silu, scale=1.0 / WSCALE).then_inc(sg_done, 1)
                        wait(act, a_done, n + 1)
                        if j == 0:
                            wait(act, y_ready, s - 2)
                        act.copy(act_p[v][:, 0, 2 * j:2 * j + 2, :], full[j % 2][:, :, :]).then_inc(hi_done, 1)
                if routed and has(0):
                    for t in range(TK):
                        wait(act, turned, s * TK + t + 1)
                        if t == 0:
                            wait(act, g_ready, (s - 1) * PR)
                        act.copy(xt[u][:, t, :, :, :], pt[t][:, :, :, :]).then_inc(xt_done, 1)
                if routed and has(2):
                    wait(act, y_ready, s - 1)
                    if not isinstance(s, int) or s >= 4:
                        act.wait_ge(y_out[u], has.per(2, 2) * 16)
                    act.activation(ysb[u][:, :, :], py[u][:, :, :], ACT.Copy, scale=1.0 / WSCALE).then_inc(y_taken, 1)
            steps(act, tiles, 3, step)

        @block.vector
        def _(dve):
            def step(s, u, has):
                if has(1):
                    v = 1 - u
                    for j in range(PR):
                        n = (s - 1) * PR + j
                        wait(dve, sg_done, n + 1)
                        wait(dve, lo_done, n - 1)
                        dve.scalar_tensor_tensor(full[j % 2][:, :, :], pu[j % 2][:, :, :], 1.0 / WSCALE, sg[j % 2][:, :, :],
                                                 ALU.mult, ALU.mult).then_inc(a_done, 1)
                        wait(dve, hi_done, n + 1)
                        dve.tensor_tensor(act_p[v][:, 1, 2 * j:2 * j + 2, :], full[j % 2][:, :, :],
                                          act_p[v][:, 0, 2 * j:2 * j + 2, :], ALU.subtract).then_inc(lo_done, 1)
                if not routed and has(2):
                    rows2 = h[:, bass.ds((s - 2 + first) * TK, TK), :]
                    wait(dve, y_ready, s - 1)
                    dve.scalar_tensor_tensor(rows2, py[u][:, :, :], 1.0 / WSCALE, rows2, ALU.mult, ALU.add).then_inc(y_taken, 1)
            steps(dve, tiles, 3, step)


def moe_stage(nc, a, h, ident, w_dram, x_sorted, room):
    y_sorted = nc.dram_tensor("m_y_sorted", [RT * TT, C], FP32, kind="Internal").ap()
    slots = room.sb("slots", [P, NT, 2], I32)
    coef = room.sb("coef", [P, NT, 2])
    tile_expert = room.sb("tile_expert", [1, RT], I32)
    xT = [room.sb(f"xT{i}", [P, CK, NT * P], FP16) for i in range(2)]
    wgu = room.sb("wgu", [P, 2, GU], FP16)
    wdn = room.sb("wdn", [P, 2, FC, C], FP16)
    scattered = room.dma_sem("scattered")
    gathered = room.dma_sem("gathered")
    half = NT // TK // 2
    with ExitStack() as ctx:
        x = Room(nc, ctx, "mx").sb("x", [P, NT, 2, C], FP16)
        with ExitStack() as rctx:
            router = Router(Room(nc, rctx, "mr"), a["m_router"])
            split_norm_T(nc, "mn", h, ident, *xT, keep=(x[:, :, 0, :], x[:, :, 1, :]), router=router)
            route_stage(nc, a, router.ps, slots, coef, tile_expert, w_dram[ER], wgu, wdn)

        def scatter(block):
            @block.gpsimd
            def _(pool):
                for n in range(NT):
                    for i in range(2):
                        pool.indirect_dma_start(x_sorted[:, :], bass.IndirectOffsetOnAxis(ap=slots[:, n, i:i + 1], axis=0),
                                                x[:, n, :, :].rearrange("p q c -> p (q c)"), None).then_inc(scattered, 16)
                pool.wait_ge(scattered, NT * 2 * 16)

        expert_tiles(nc, "ma", half, (wgu, wdn), xT=xT, first=0, h=h, side=scatter)
    expert_tiles(nc, "mb", RT, w_dram, ident=ident, tile_expert=tile_expert, x_sorted=x_sorted, y_sorted=y_sorted)
    y = [room.sb(f"y{i}", [P, NT, C]) for i in range(2)]

    def gather(block):
        @block.gpsimd
        def _(pool):
            for n in range(NT):
                for i in range(2):
                    pool.indirect_dma_start(y[i][:, n, :], None, y_sorted[:, :],
                                            bass.IndirectOffsetOnAxis(ap=slots[:, n, i:i + 1], axis=0)).then_inc(gathered, 16)
            pool.wait_ge(gathered, NT * 2 * 16)
            for q in range(4):
                r = slice(q * NT // 4, (q + 1) * NT // 4)
                for i in range(2):
                    pool.tensor_tensor(y[i][:, r, :], y[i][:, r, :], coef[:, r, i:i + 1].to_broadcast([P, NT // 4, C]),
                                       ALU.mult).then_inc(weighted, 1)
                pool.wait_ge(weighted, q * 2 + 2)
                pool.tensor_tensor(y[0][:, r, :], y[0][:, r, :], y[1][:, r, :], ALU.add)

    weighted = room.sem("weighted")
    expert_tiles(nc, "mc", half, (wgu, wdn), xT=xT, first=half, h=h, side=gather)
    return y[0]


def program(nc, a, out):
    with ExitStack() as ctx:
        h = ctx.enter_context(nc.sbuf_tensor("h", [P, NT, C], FP32))
        identb = ctx.enter_context(nc.sbuf_tensor("identb", [P, P], BF16))
        identh = ctx.enter_context(nc.sbuf_tensor("identh", [P, P], FP16))
        constants_stage(nc, identb, identh)
        w_dram = nc.dram_tensor("m_w_parts", [E8, P, 2, GU + DN], FP16, kind="Internal").ap()
        x_sorted = nc.dram_tensor("m_x_sorted", [RT * TT, 2 * C], FP16, kind="Internal").ap()
        embed_stage(nc, a["ids"], a["table"], h)
        attention0_stage(nc, a, h, identb[:, :], split_experts(nc, a["m_w"], w_dram))
        experts0_stage(nc, a, h, identh[:, :], x_sorted)
        attention1_stage(nc, a, h, identh[:, :])
        y = moe_stage(nc, a, h, identh[:, :], w_dram, x_sorted, Room(nc, ctx, "m"))
        write_stage(nc, h, y, out)


def rows(v):
    return v.reshape(-1, P).T


def spread(v):
    return np.broadcast_to(v, (P, v.shape[0]))


def sinusoids(length, width):
    at = np.arange(length, dtype=np.float32)[:, None]
    rate = np.exp(np.arange(0, width, 2, dtype=np.float32) * np.float32(-np.log(10000.0) / width))
    return np.stack([np.sin(at * rate), np.cos(at * rate)], -1).reshape(length, width).astype(np.float32)


def kernel(**inputs):
    import concourse.bacc as bacc
    from concourse.bass_utils import run_bass_kernel_spmd

    f = {k: np.asarray(v) for k, v in inputs.items()}
    wqkv, bqkv = f["L0_attn_Wqkv"], f["L0_attn_bqkv"]
    laid = {
        "ids": f["x"].reshape(NT, P).T,
        "table": f["L0_tok_weight"],
        "a0_wqkv": wqkv.T,
        "a0_qkb": rows(bqkv[:2 * C]),
        "a0_vb": spread(bqkv[2 * C:]),
        "a0_wo": f["L0_attn_Wproj"].T,
        "a0_ob": spread(f["L0_attn_bproj"]),
    }
    pair = np.zeros((P, P), f["L0_ffn_sub_key0"].dtype)
    for b in range(4):
        pair[b * PK:(b + 1) * PK, b * PK:(b + 1) * PK] = f[f"L0_ffn_sub_key{b % 2}"].T
    laid.update({
        "f0_wq": f["L0_ffn_Wq"],
        "f0_down": f["L0_ffn_expert_down"].T,
        "f0_up": f["L0_ffn_expert_up"],
        "f0_bq": rows(f["L0_ffn_bq"]),
        "f0_gnb": np.stack([np.tile(f["L0_ffn_bn_gamma"], 2), np.tile(f["L0_ffn_bn_beta"], 2)], 1),
        "f0_keys": pair,
        "f0_agg": (np.tile(np.eye(P // 2), (2, 2)) / PH).astype(np.float32),
        "f0_ones": np.ones((P, P), np.float32),
        "f0_blocks": np.repeat(np.eye(4), P // 4, 0).astype(np.float32),
    })
    laid.update({f"a1_w{n}": f[f"L1_attn_W{n}"] for n in "qkvpo"})
    laid.update({
        "a1_pe": sinusoids(T, C).T,
        "a1_g": spread(f["L1_attn_ln_g"]),
        "a1_b": spread(f["L1_attn_ln_b"]),
        "a1_qkuv": np.stack([rows(f[f"L1_attn_{n}"].reshape(C)) for n in ("bq", "bk", "u_bias", "v_bias")], 1),
        "a1_bv": spread(f["L1_attn_bv"]),
        "a1_bo": spread(f["L1_attn_bo"]),
    })
    gate, up, down = (np.concatenate([f[f"L1_ffn_routed_{n}"], f[f"L1_ffn_shared_{n}"][None]]) for n in ("gate", "up", "down"))
    laid.update({
        "m_w": np.concatenate([w.transpose(0, 2, 1).reshape(E8, -1, P, w.shape[1]).transpose(0, 2, 1, 3).reshape(E8, P, -1)
                               for w in (gate, up, down)], 2),
        "m_router": np.concatenate([f["L1_ffn_router_w"], np.zeros((1, C), np.float32)]).T,
        "m_before": np.triu(np.ones((P, P), np.float32), 1),
        "m_ones": np.ones((P, P), np.float32),
        "m_lane": spread(np.arange(E8, dtype=np.float32)),
        "m_tile_no": np.repeat(np.arange(RT, dtype=np.float32)[None, :, None], E8, 2),
    })
    nc = bacc.Bacc("TRN2", target_bir_lowering=False, num_devices=1)
    arrays, args = {}, {}
    for name, a in laid.items():
        a = np.ascontiguousarray(a)
        arrays["in_" + name] = a
        args[name] = nc.dram_tensor("in_" + name, a.shape, mybir.dt.from_np(a.dtype), kind="ExternalInput").ap()
    out = nc.dram_tensor("out", (B, T, C), FP32, kind="ExternalOutput").ap()
    program(nc, args, out)
    r = run_bass_kernel_spmd(nc, [arrays], core_ids=[0])
    return r.results[0]["out"]
```
